# Optimizing a Trainium2 kernel written in Bass

```python
import numpy as np
import jax
import jax.numpy as jnp

def _softmax(x, axis=-1):
    return jax.nn.softmax(x, axis=axis)

def _gelu(x):
    return jax.nn.gelu(x, approximate=True)

def _silu(x):
    return jax.nn.silu(x)

def _sigmoid(x):
    return jax.nn.sigmoid(x)

def _layernorm(x, axis=-1, eps=1e-05):
    m = jnp.mean(x, axis=axis, keepdims=True)
    v = jnp.var(x, axis=axis, keepdims=True)
    return (x - m) / jnp.sqrt(v + eps)

def _scatter_add(tgt, idx, src, axis=0):
    return tgt.at[idx].add(src)

def _segment_sum(src, seg, n):
    return jax.ops.segment_sum(src, seg, n)
kernel_name = 'mk_decoder_postln_d1_seqx_r8_96b1c9'

def setup_inputs(seed: int=0):
    np.random.seed(seed)
    _w = jnp.asarray

    def _rec_inputs():
        import jax
        import jax.numpy as jnp
        _rk = jax.random.key(seed)
        x = -0.0003929 + 0.9999 * jax.random.normal(jax.random.fold_in(_rk, 1), (8, 128, 512), jnp.float32)
        _lenS = 128 - jax.random.randint(jax.random.fold_in(_rk, 7), (8,), 0, max(1, 128 // 4) + 1, jnp.int32)
        _lenS2 = 128 - jax.random.randint(jax.random.fold_in(_rk, 8), (8,), 0, max(1, 128 // 4) + 1, jnp.int32)
        _ctx_1024P = jax.random.normal(jax.random.fold_in(_rk, 11), (8, 16, 128), jnp.float32)
        _ctx_1024c = jax.random.dirichlet(jax.random.fold_in(_rk, 511), 0.3 * jnp.ones((16,), jnp.float32), (8, 128))
        _ctx_1024t = jnp.einsum('bsk,bkd->bsd', _ctx_1024c, _ctx_1024P)
        _ctx_1024t = _ctx_1024t * jax.lax.rsqrt(jnp.mean(jnp.square(_ctx_1024t)) + 1e-12) * 0.953939
        ctx_1024 = -1.39393e-06 + 0.999914 * (_ctx_1024t + 0.3 * jax.random.normal(jax.random.fold_in(_rk, 611), (8, 128, 128), jnp.float32))
        _validS = jnp.arange(128)[None, :] < _lenS[:, None]
        _validS2 = jnp.arange(128)[None, :] < _lenS2[:, None]
        _causal = jnp.tril(jnp.ones((128, 128), dtype=bool))
        mask_SxS2_ff0 = jnp.where(jnp.ones((128, 128), dtype=bool), 0.0, -1000000000.0).astype(jnp.float32)
        return (x, ctx_1024, mask_SxS2_ff0)
    x, ctx_1024, mask_SxS2_ff0 = _rec_inputs()

    def _L0_attn_setup():
        import jax, jax.numpy as jnp
        import numpy as np
        HEADS = 32
        key = jax.random.key(seed)
        ks = jax.random.split(key, 5)
        H = 512
        B, S = (2, 256)
        w_scale = 1.0 / np.sqrt(H)
        return {'x': jax.random.normal(ks[0], (B, S, H), dtype=jnp.float32), 'attn_qkvw': jax.random.normal(ks[1], (H, 3 * H), dtype=jnp.float32) * w_scale, 'attn_qkvb': jax.random.normal(ks[2], (3 * H,), dtype=jnp.float32) * 0.02, 'attn_ow': jax.random.normal(ks[3], (H, H), dtype=jnp.float32) * w_scale, 'attn_ob': jax.random.normal(ks[4], (H,), dtype=jnp.float32) * 0.02}
    _L0_attn_all = _L0_attn_setup()
    _L0_attn_in = {k: v for k, v in _L0_attn_all.items() if k in ('attn_qkvw', 'attn_qkvb', 'attn_ow', 'attn_ob')}
    del _L0_attn_all

    def _L0_xattn_setup():
        import math
        import jax, jax.numpy as jnp
        import numpy as np
        N_HEADS = 32
        N_KV_HEADS = 8
        N_REP = N_HEADS // N_KV_HEADS
        HEAD_DIM = 512 // N_HEADS
        key = jax.random.key(seed)
        kq, kk, kv = jax.random.split(key, 3)
        B, S, T = (2, 256, 256)
        q = jax.random.normal(kq, (B, S, N_HEADS * HEAD_DIM), dtype=jnp.float32)
        k = jax.random.normal(kk, (B, T, N_KV_HEADS * HEAD_DIM), dtype=jnp.float32)
        v = jax.random.normal(kv, (B, T, N_KV_HEADS * HEAD_DIM), dtype=jnp.float32)
        mask = jnp.zeros((S, T), dtype=jnp.float32)
        return {'q': q, 'k': k, 'v': v, 'start_pos': 0, 'mask': mask}
    _L0_xattn_all = _L0_xattn_setup()
    _L0_xattn_in = {k: v for k, v in _L0_xattn_all.items() if k in ()}
    del _L0_xattn_all

    def _L0_ffn_setup():
        import jax, jax.numpy as jnp
        import numpy as np

        @jax.custom_vjp
        def ste_sign(w):
            return jnp.sign(w)

        def _ste_fwd(w):
            return (jnp.sign(w), w)

        def _ste_bwd(w, g):
            mask = ((w > -1) & (w < 1)).astype(g.dtype)
            return (g * mask,)
        ste_sign.defvjp(_ste_fwd, _ste_bwd)
        key = jax.random.key(seed)
        k = jax.random.split(key, 6)
        B, S, H, O, E = (4, 256, 512, 512, 8)
        return {'x': jax.random.normal(k[0], (B, S, H), dtype=jnp.float32), 'weight': jax.random.normal(k[1], (O, H), dtype=jnp.float32) * 0.02, 'bias': jax.random.normal(k[2], (O,), dtype=jnp.float32) * 0.02, 'gate_w': jax.random.normal(k[3], (E, H), dtype=jnp.float32) * 0.02, 'in_channel_scale': jax.random.normal(k[4], (E, H), dtype=jnp.float32), 'out_channel_scale': jax.random.normal(k[5], (E, O), dtype=jnp.float32)}
    _L0_ffn_all = _L0_ffn_setup()
    _L0_ffn_in = {k: v for k, v in _L0_ffn_all.items() if k in ('weight', 'bias', 'gate_w', 'in_channel_scale', 'out_channel_scale')}
    del _L0_ffn_all
    return {'x': x, 'ctx_1024': ctx_1024, 'mask_SxS2_ff0': mask_SxS2_ff0, 'L0_attn_attn_qkvw': _L0_attn_in['attn_qkvw'], 'L0_attn_attn_qkvb': _L0_attn_in['attn_qkvb'], 'L0_attn_attn_ow': _L0_attn_in['attn_ow'], 'L0_attn_attn_ob': _L0_attn_in['attn_ob'], 'L0_ffn_weight': _L0_ffn_in['weight'], 'L0_ffn_bias': _L0_ffn_in['bias'], 'L0_ffn_gate_w': _L0_ffn_in['gate_w'], 'L0_ffn_in_channel_scale': _L0_ffn_in['in_channel_scale'], 'L0_ffn_out_channel_scale': _L0_ffn_in['out_channel_scale']}

def reference(x, ctx_1024, mask_SxS2_ff0, L0_attn_attn_qkvw, L0_attn_attn_qkvb, L0_attn_attn_ow, L0_attn_attn_ob, L0_ffn_weight, L0_ffn_bias, L0_ffn_gate_w, L0_ffn_in_channel_scale, L0_ffn_out_channel_scale):
    import jax
    import jax.numpy as jnp

    def _L0_attn_ref(x, attn_qkvw, attn_qkvb, attn_ow, attn_ob):
        import jax, jax.numpy as jnp
        import numpy as np
        HEADS = 32
        B, S, H = x.shape
        hd = H // HEADS
        scale = 1.0 / np.sqrt(hd)
        qkv = x @ attn_qkvw + attn_qkvb
        qkv = qkv.reshape(B, S, 3, HEADS, hd)
        q = jnp.transpose(qkv[:, :, 0], (0, 2, 1, 3))
        k = jnp.transpose(qkv[:, :, 1], (0, 2, 1, 3))
        v = jnp.transpose(qkv[:, :, 2], (0, 2, 1, 3))
        scores = jnp.einsum('bhqd,bhkd->bhqk', q, k) * scale
        probs = jax.nn.softmax(scores, axis=-1)
        ctx = jnp.einsum('bhqk,bhkd->bhqd', probs, v)
        ctx = jnp.transpose(ctx, (0, 2, 1, 3)).reshape(B, S, H)
        return ctx @ attn_ow + attn_ob

    def _L0_xattn_ref(q, k, v, start_pos, mask):
        import math
        import jax, jax.numpy as jnp
        import numpy as np
        N_HEADS = 32
        N_KV_HEADS = 8
        N_REP = N_HEADS // N_KV_HEADS
        HEAD_DIM = 512 // N_HEADS
        b, s, _ = q.shape
        t = k.shape[1]
        xq = q.reshape(b, s, N_KV_HEADS, N_REP, HEAD_DIM)
        xk = k.reshape(b, t, N_KV_HEADS, HEAD_DIM)
        xv = v.reshape(b, t, N_KV_HEADS, HEAD_DIM)
        scores = jnp.einsum('bsgrd,btgd->bgrst', xq, xk) / math.sqrt(HEAD_DIM)
        scores = scores + mask
        probs = jax.nn.softmax(scores.astype(jnp.float32), axis=-1).astype(q.dtype)
        out = jnp.einsum('bgrst,btgd->bsgrd', probs, xv)
        return out.reshape(b, s, N_HEADS * HEAD_DIM)

    def _L0_ffn_ref(x, weight, bias, gate_w, in_channel_scale, out_channel_scale):
        import jax, jax.numpy as jnp
        import numpy as np

        @jax.custom_vjp
        def ste_sign(w):
            return jnp.sign(w)

        def _ste_fwd(w):
            return (jnp.sign(w), w)

        def _ste_bwd(w, g):
            mask = ((w > -1) & (w < 1)).astype(g.dtype)
            return (g * mask,)
        ste_sign.defvjp(_ste_fwd, _ste_bwd)
        B, S, H = x.shape
        xf = x.reshape(-1, H)
        router_logits = xf @ gate_w.T
        routing = jax.nn.softmax(router_logits.astype(jnp.float32), axis=1).astype(x.dtype)
        in_scale = routing @ in_channel_scale
        out_scale = routing @ out_channel_scale
        wb = ste_sign(weight)
        out = xf * in_scale @ wb.T * out_scale + bias
        return out.reshape(B, S, -1)
    x = _layernorm(x + _L0_attn_ref(x, L0_attn_attn_qkvw, L0_attn_attn_qkvb, L0_attn_attn_ow, L0_attn_attn_ob), axis=-1)
    x = _layernorm(x + _L0_xattn_ref(x, ctx_1024, ctx_1024, 0, mask_SxS2_ff0), axis=-1)
    x = _layernorm(x + _L0_ffn_ref(x, L0_ffn_weight, L0_ffn_bias, L0_ffn_gate_w, L0_ffn_in_channel_scale, L0_ffn_out_channel_scale), axis=-1)
    return x

_drawn_inputs = setup_inputs


def setup_inputs(seed=0):
    import zlib

    import numpy as np

    out = dict(_drawn_inputs(seed))
    spreads = {'mask_SxS2_ff0': (0.0, 0.779)}
    factors = {'L0_ffn_bias': 8.0}
    for name, (base, spread) in spreads.items():
        noise = np.random.default_rng([zlib.crc32(name.encode()), seed]).standard_normal(out[name].shape)
        drawn = base * np.exp(spread * noise) if base else spread * noise
        out[name] = jnp.asarray(drawn.astype(out[name].dtype))
    for name, factor in factors.items():
        out[name] = (out[name] * factor).astype(out[name].dtype)
    return out
```

```python
from contextlib import ExitStack

import concourse.bass as bass
from concourse import mybir

F32 = mybir.dt.float32
F32R = mybir.dt.float32r
BF16 = mybir.dt.bfloat16
ALU = mybir.AluOpType
ACT = mybir.ActivationFunctionType
AX = mybir.AxisListType

P = 128
B = 8
GB = 2
NG = B // GB
TOK = GB * P
H = 512
KT = H // P
HEADS = 32
HD = H // HEADS
KVH = 8
HT = P // HD
E = 8
NPART = 3
SR = 6 * HD
SM = SR + NPART
VW = 32
NP = 4
EPS = 1e-5
LOWEST = -3.0e38
QBLK = 3 * H


class Ring:

    def __init__(self, full, empty, order, before=()):
        self.full, self.empty = full, empty
        self.unit = {}
        uses, turn = [0] * 4, 0
        placed = []
        for name in before:
            self.unit[name] = (turn % 3, uses[turn % 3], 0)
            uses[turn % 3] += 1
            turn += 1
        turn = 0
        for name in order:
            k = 3 if name[0] == "pv" else turn % 3
            turn += k < 3
            placed.append((name, k))
        per = [sum(1 for _, k in placed if k == n) for n in range(4)]
        for name, k in placed:
            self.unit[name] = (k, uses[k], per[k])
            uses[k] += 1

    def bank(self, *name):
        return self.unit[name][0]

    def wait_full(self, eng, i, *name):
        k, n, per = self.unit[name]
        eng.wait_ge(self.full[k], i * per + n + 1)

    def wait_emptied(self, eng, i, *name):
        k, n, per = self.unit[name]
        eng.wait_ge(self.empty[k], i * per + n + 1)

    def wait_free(self, eng, i, *name):
        k, n, per = self.unit[name]
        if not isinstance(i, int) or i * per + n > 0:
            eng.wait_ge(self.empty[k], i * per + n)

    def is_full(self, *name):
        return self.full[self.unit[name][0]], 1

    def is_empty(self, *name):
        return self.empty[self.unit[name][0]], 1


def schedule(a=True, b=True):
    s = [("B", "xt", 0), ("B", "xt", 1), ("B", "ctx"), ("A", "xt", 0), ("A", "xt", 1)]
    s += [("A", "q", 0), ("A", "q", 1), ("A", "q", 2)]
    s += [("B", "s", 0, g) for g in range(4)] + [("A", "q", 3)]
    s += [("B", "s", 0, g) for g in range(4, 8)] + [("A", "v", 0)]
    s += [("B", "s", 1, g) for g in range(4)] + [("A", "v", 1)]
    s += [("B", "s", 1, g) for g in range(4, 8)] + [("B", "mt", 0)]
    beside = {
        (0, 3): [("B", "mt", 1)],
        (1, 1): [("B", "ot", 0, 0)], (1, 2): [("B", "ot", 0, 1)], (1, 3): [("A", "mt", 0)],
    }
    for q in range(GB):
        for j in range(HT):
            s += [("A", "s", q, j), ("B", "st", q, j)]
            if j >= 1:
                s.append(("B", "pv", q, j - 1))
            s += beside.get((q, j), [])
        s.append(("B", "pv", q, HT - 1))
    beside = {
        (0, 0): [("B", "ot", 1, 0)], (0, 1): [("B", "ot", 1, 1)], (0, 3): [("A", "mt", 1)],
        (0, 5): [("B", "cx", 0)], (0, 6): [("B", "cx", 1)], (0, 7): [("B", "rl")],
        (1, 0): [("A", "ot", 0, 0)], (1, 1): [("A", "ot", 0, 1)], (1, 2): [("B", "rt")],
        (1, 4): [("A", "ct", 0), ("B", "rr")], (1, 5): [("B", "is", 0)], (1, 6): [("B", "is", 1)],
        (1, 7): [("A", "op", 0)],
    }
    for q in range(GB):
        for j in range(HT):
            s.append(("A", "st", q, j))
            if j >= 1:
                s.append(("A", "pv", q, j - 1))
            s += beside.get((q, j), [])
        s.append(("A", "pv", q, HT - 1))
    s += [("B", "os", 0), ("B", "ff", 0), ("A", "ot", 1, 0), ("A", "ot", 1, 1)]
    s += [("B", "os", 1), ("B", "ff", 1), ("A", "ct", 1), ("A", "op", 1)]
    return [x for x in s if (x[0] == "A" and a) or (x[0] == "B" and b)]


def first_turn():
    s = schedule(b=False)
    at = s.index(("A", "q", 2))
    s[at:at] = [("C", "mask"), ("C", "ow")]
    at = s.index(("A", "s", 0, 0))
    s[at:at] = [("C", "sign")]
    at = s.index(("A", "s", 1, 0))
    s[at:at] = [("C", "swt", 0), ("C", "swt", 1)]
    at = s.index(("A", "st", 0, 0))
    s[at:at] = [("C", "swt", 2), ("C", "swt", 3), ("C", "scales")]
    return [("C", "small")] + s


def units(steps, thread):
    out = []
    for t, *name in steps:
        if t == thread and name[0] != "pv":
            out.append(tuple(name))
        elif t == thread and name[2] % 4 == 0:
            out.append(("pv", name[1], name[2] // 4))
    return out


def decoder_layer(nc, x, ctx_1024, mask, qkvw, qkvb, ow, ob, fw, fb, gate_w, in_cs, out_cs, out, scr_q, scr_k, scr_x, scr_c):
    es = ExitStack()
    with es:
        def sb(name, shape, dt):
            return es.enter_context(nc.sbuf_tensor(name, shape, dt))

        def sem(name):
            return es.enter_context(nc.semaphore(name))

        wH = sb("wH", [P, KT, QBLK], F32R)
        wL = sb("wL", [P, KT, QBLK], F32R)
        owH = sb("owH", [P, KT, H], F32R)
        owL = sb("owL", [P, KT, H], F32R)
        swT = sb("swT", [P, KT, H], F32R)
        gT = sb("gT", [P, KT, E], F32)
        icS = sb("icS", [4 * E, H], F32R)
        ocS = sb("ocS", [4 * E, H], F32R)
        bqk = sb("bqk", [P, 2 * KT], F32)
        vbias = sb("vbias", [P, H], F32)
        obias = sb("obias", [P, H], F32)
        fbias = sb("fbias", [P, H], F32)
        mraw = sb("mraw", [P, P], F32)
        mH = sb("mH", [P, P], F32R)
        mL = sb("mL", [P, P], F32R)
        idf = sb("idf", [P, P], F32)
        idb = sb("idb", [P, P], BF16)
        idr = sb("idr", [P, 4, P], F32R)
        pick = sb("pick", [4 * E, 2], F32)
        one_row = sb("one_row", [NPART, TOK], BF16)
        half = sb("half", [P, 2], F32)
        x_in = sb("x_in", [P, GB, H], F32)
        xb = sb("xb", [P, GB, H], F32)
        xH = sb("xH", [P, KT, TOK], F32R)
        xL = sb("xL", [P, KT, TOK], F32R)
        qs = sb("qs", [P, HT, KT, TOK], BF16)
        ks = sb("ks", [P, HT, KT, TOK], BF16)
        qp = sb("qp", [P, NPART, KT, TOK], BF16)
        kp = sb("kp", [P, NPART, KT, TOK], BF16)
        wide_a = sb("wide_a", [P, 2, H], F32)
        va = sb("va", [P, GB, HEADS, VW], F32)
        pa = sb("pa", [P, NP, H], F32)
        nma = sb("nma", [P, GB, HEADS], F32)
        npa = sb("npa", [P, GB, NPART, HEADS], BF16)
        nra = sb("nra", [P, 2, HEADS], F32)
        mra = sb("mra", [NPART * HEADS, GB, P], BF16)
        rda = sb("rda", [P, HEADS], F32)
        x1 = sb("x1", [P, GB, H], F32)
        sta = sb("sta", [P, 6], F32)
        mva = sb("mva", [P, 2], F32)
        rsa = sb("rsa", [P, 2], F32)
        c_in = sb("c_in", [P, GB, P], F32)
        c_perm = sb("c_perm", [P, GB, P], F32)
        qx = sb("qx", [P, HT, KT, TOK], BF16)
        kx = sb("kx", [P, KVH, TOK], BF16)
        cp = sb("cp", [P, NPART, TOK], BF16)
        rc = sb("rc", [P, TOK], F32)
        wide_b = sb("wide_b", [P, 2, H], F32)
        vx = sb("vx", [P, GB, KVH, VW], F32)
        pb = sb("pb", [P, NP, H], F32)
        nmb = sb("nmb", [P, GB, HEADS], F32)
        npb = sb("npb", [P, GB, NPART, HEADS], BF16)
        nrb = sb("nrb", [P, 2, HEADS], F32)
        mrb = sb("mrb", [NPART * HEADS, GB, P], BF16)
        rdb = sb("rdb", [P, HEADS], F32)
        x2 = sb("x2", [P, GB, H], F32)
        stb = sb("stb", [P, 6], F32)
        mvb = sb("mvb", [P, 2], F32)
        rsb = sb("rsb", [P, 2], F32)
        lg = sb("lg", [E, TOK], F32)
        nl = sb("nl", [P, GB], F32)
        el = sb("el", [P, GB, E], F32)
        sl = sb("sl", [P, GB], F32)
        rl = sb("rl", [P, GB], F32)
        rt = sb("rt", [P, GB, E], F32)
        rtH = sb("rtH", [P, GB, E], F32R)
        rts = sb("rts", [P, GB, 4, E], F32)
        rT = sb("rT", [4 * E, TOK], F32R)
        osb = sb("osb", [P, H], F32)

        def at(name, shape, dt, host, skip=0):
            return nc.alloc_sbuf_tensor_at(name, shape, dt, offset=nc.lookup_mloc(host).addr + skip)

        KB = 1024
        wraw = at("wraw", [P, KT, QBLK], F32, qs)
        oraw = at("oraw", [P, KT, H], F32, qx)
        fraw = at("fraw", [P, KT, H], F32, qx, 8 * KB)
        sgn = at("sgn", [P, KT, H], BF16, kx)
        icr = at("icr", [4 * E, H], F32, pb)
        ocr = at("ocr", [4 * E, H], F32, pb, 2 * KB)
        cshi = at("cshi", [4 * E, H], F32R, pb, 4 * KB)
        cslo = at("cslo", [4 * E, H], F32, pb, 6 * KB)
        graw = at("graw", [E, H], F32, x2)
        braw = at("braw", [2 * KT, P], F32, x2, 2 * KB)
        bperm = at("bperm", [2 * KT, P], F32, x2, 3 * KB)
        cx = at("cx", [P, H], F32, xH)
        cH = at("cH", [P, KT, P], F32R, xH, 2 * KB)
        cL = at("cL", [P, KT, P], F32R, xL)
        x2T = at("x2T", [P, KT, TOK], F32, qx)
        zf = at("zf", [P, KT, TOK], F32, qx, 4 * KB)
        zH = at("zH", [P, KT, TOK], F32R, qx, 8 * KB)
        zL = at("zL", [P, KT, TOK], F32R, qx, 12 * KB)

        bank_a = [es.enter_context(nc.psum_tensor(f"bank_a{k}", [P, H], F32)) for k in range(4)]
        bank_b = [es.enter_context(nc.psum_tensor(f"bank_b{k}", [P, H], F32)) for k in range(4)]
        ra = Ring([sem(f"full_a{k}") for k in range(4)], [sem(f"empty_a{k}") for k in range(4)],
                  units(schedule(), "A"))
        rb = Ring([sem(f"full_b{k}") for k in range(4)], [sem(f"empty_b{k}") for k in range(4)],
                  units(schedule(), "B"), [("small",)] + [("swt", k) for k in range(4)])

        def pa_bank(*name):
            return bank_a[ra.bank(*name)]

        def pb_bank(*name):
            return bank_b[rb.bank(*name)]

        ld_small, ld_mask, ld_ow, ld_fw, ld_cs = (sem(n) for n in ("ld_small", "ld_mask", "ld_ow", "ld_fw", "ld_cs"))
        ld_w = [sem(f"ld_w{k}") for k in range(3)]
        ld_vb, ld_ob, ld_fb = sem("ld_vb"), sem("ld_ob"), sem("ld_fb")
        idents, w_high, w_low = sem("idents"), sem("w_high"), sem("w_low")
        ow_high, ow_low, signs, masks = sem("ow_high"), sem("ow_low"), sem("signs"), sem("masks")
        scale_step, scales, ones_a, ones_b, picks = sem("scale_step"), sem("scales"), sem("ones_a"), sem("ones_b"), sem("picks")
        ident_step, ones_row, rows_a, rows_b = sem("ident_step"), sem("ones_row"), sem("rows_a"), sem("rows_b")
        x_loaded, xb_made, xh_made = sem("x_loaded"), sem("xb_made"), sem("xh_made")
        a_first, a_second, a_third = sem("a_first"), sem("a_second"), sem("a_third")
        q_stored, k_stored, q_stacked, k_stacked = sem("q_stored"), sem("k_stored"), sem("q_stacked"), sem("k_stacked")
        max_split_a, max_parts_a, max_stacked_a = sem("max_split_a"), sem("max_parts_a"), sem("max_stacked_a")
        pv_a, recip_a, ch_made = sem("pv_a"), sem("recip_a"), sem("ch_made")
        ln_a, rstd_step_a, rstd_a, x1_made = sem("ln_a"), sem("rstd_step_a"), sem("rstd_a"), sem("x1_made")
        c_loaded, c_permuted, vx_made = sem("c_loaded"), sem("c_permuted"), sem("vx_made")
        bias_permuted = sem("bias_permuted")
        b_first, b_second, b_third = sem("b_first"), sem("b_second"), sem("b_third")
        c_first, c_second, c_third = sem("c_first"), sem("c_second"), sem("c_third")
        x_stored, c_stored, x_stacked, c_stacked = sem("x_stored"), sem("c_stored"), sem("x_stacked"), sem("c_stacked")
        max_split_b, max_parts_b, max_stacked_b = sem("max_split_b"), sem("max_parts_b"), sem("max_stacked_b")
        pv_b, recip_b = sem("pv_b"), sem("recip_b")
        ln_b, rstd_step_b, rstd_b, x2_made, x2_biased = sem("ln_b"), sem("rstd_step_b"), sem("rstd_b"), sem("x2_made"), sem("x2_biased")
        top_made, exp_made, route_step, route_made = sem("top_made"), sem("exp_made"), sem("route_step"), sem("route_made")
        zh_made, zl_made, y_made, out_stored = sem("zh_made"), sem("zl_made"), sem("y_made"), sem("out_stored")

        turns = [(0, first_turn())] + [(i, schedule()) for i in range(1, NG)] + [(NG, schedule(a=False))]

        def permuted(ap):
            return ap.rearrange("p (h d) -> p d h", d=HD)

        def by_head(ap):
            return ap.rearrange("p (m h d) -> p m h d", m=KT, d=HD)

        def tile_permuted(ap):
            return ap.rearrange("p (m d h) -> p m h d", m=KT, d=HD)

        def tokens(b):
            return slice(b * P, (b + 1) * P)

        def w_views(dst, src, kt, blk):
            to, of = dst[:, kt, blk * H:(blk + 1) * H], src[:, kt, blk * H:(blk + 1) * H]
            if blk == 2:
                return to, of
            return to.rearrange("p (m d h) -> p m d h", m=KT, d=HD), of.rearrange("p (m h d) -> p m d h", m=KT, d=HD)

        block = es.enter_context(nc.Block())

        @block.sync
        def _(sp):
            def load_x(i):
                sp.dma_start(x_in[:], x[GB * i:GB * (i + 1)].rearrange("b p f -> p b f")).then_inc(x_loaded, 16)

            def load_c(i):
                sp.dma_start(c_in[:], ctx_1024[GB * i:GB * (i + 1)].rearrange("b p f -> p b f")).then_inc(c_loaded, 16)

            def stack(dst, scratch, lows_first, done):
                n = 2 if lows_first else 0
                for row, first, last in ((0, 0, NPART), (3, n // 2, n // 2 + 2), (5, n, n + 1)):
                    src = scratch[first * HD:last * HD]
                    sp.dma_start(dst[row * HD:(row + last - first) * HD], src).then_inc(done, 16)

            load_x(0)
            wv = qkvw.rearrange("(kt p) n -> p kt n", p=P)
            sp.dma_start(wraw[:, :, 0:H], wv[:, :, 0:H]).then_inc(ld_w[0], 16)
            sp.dma_start(braw[:], qkvb[0:2 * H].rearrange("(t p) -> t p", p=P)).then_inc(ld_small, 16)
            sp.dma_start(graw[:], gate_w).then_inc(ld_small, 16)
            sp.dma_start(wraw[:, :, H:2 * H], wv[:, :, H:2 * H]).then_inc(ld_w[1], 16)
            sp.dma_start(wraw[:, :, 2 * H:3 * H], wv[:, :, 2 * H:3 * H]).then_inc(ld_w[2], 16)
            sp.dma_start(oraw[:], ow.rearrange("(kt p) n -> p kt n", p=P)).then_inc(ld_ow, 16)
            sp.dma_start(fraw[:], fw.rearrange("(ot p) n -> p ot n", p=P)).then_inc(ld_fw, 16)

            for t, steps in turns:
                i, ib = t, t - 1
                for thread, *step in steps:
                    name = step[0]
                    if thread == "B" and step == ["xt", 1]:
                        sp.wait_ge(b_third, 2 * (ib + 1))
                        sp.dma_start(scr_x[ib].rearrange("(c d) h f -> (d h) c f", d=HD),
                                     kp[:].rearrange("p c m t -> p c (m t)")).then_inc(x_stored, 16)
                    elif thread == "B" and name == "ctx":
                        sp.wait_ge(c_third, ib + 1)
                        sp.dma_start(scr_c[ib].rearrange("(c d) h f -> (d h) c f", d=HD), cp[:]).then_inc(c_stored, 16)
                        sp.wait_ge(x_stored, 16 * (ib + 1))
                        stack(qx[:].rearrange("r h m t -> r h (m t)"), scr_x[ib], True, x_stacked)
                        sp.wait_ge(c_stored, 16 * (ib + 1))
                        stack(kx[:], scr_c[ib], False, c_stacked)
                    elif thread == "A" and step == ["q", 1]:
                        sp.wait_ge(a_third, 4 * i + 2)
                        sp.dma_start(scr_q[i].rearrange("(c d) h f -> (d h) c f", d=HD),
                                     qp[:].rearrange("p c m t -> p c (m t)")).then_inc(q_stored, 16)
                        sp.wait_ge(q_stored, 16 * (i + 1))
                        stack(qs[:].rearrange("r h m t -> r h (m t)"), scr_q[i], True, q_stacked)
                    elif thread == "A" and step == ["q", 3]:
                        sp.wait_ge(a_third, 4 * i + 4)
                        sp.dma_start(scr_k[i].rearrange("(c d) h f -> (d h) c f", d=HD),
                                     kp[:].rearrange("p c m t -> p c (m t)")).then_inc(k_stored, 16)
                        sp.wait_ge(k_stored, 16 * (i + 1))
                        stack(ks[:].rearrange("r h m t -> r h (m t)"), scr_k[i], False, k_stacked)
                    elif thread == "A" and step == ["v", 1]:
                        if t < NG - 1:
                            ra.wait_full(sp, i, "xt", 1)
                            sp.wait_ge(xb_made, GB * (i + 1))
                            load_x(i + 1)
                        if t > 0:
                            rb.wait_full(sp, ib, "ctx")
                            sp.wait_ge(vx_made, GB * (ib + 1))
                        load_c(i)
                    elif name == "mt":
                        b = step[1]
                        k, src, dst, done, ring = (i, mra, qs, max_stacked_a, ra) if thread == "A" else (ib, mrb, qx, max_stacked_b, rb)
                        ring.wait_emptied(sp, k, "mt", b)
                        for c in range(NPART):
                            sp.dma_start(dst[SR + c:SR + c + 1, :, :, tokens(b)].rearrange("r h m t -> r (h m) t"),
                                         src[c * HEADS:(c + 1) * HEADS, b, :]).then_inc(done, 16)
                    elif thread == "C" and name == "ow":
                        sp.wait_ge(ones_row, 1)
                        sp.wait_ge(w_low, 3 * KT)
                        sp.dma_start(ks[SR:SM].rearrange("r h m t -> r (h m) t"),
                                     one_row[:].rearrange("r (o t) -> r o t", o=1).broadcast_to([NPART, HT * KT, TOK])).then_inc(rows_a, 16)
                    elif thread == "C" and step == ["swt", 3]:
                        rb.wait_full(sp, 0, "swt", 3)
                        sp.dma_start(kx[SR:SM], one_row[:].rearrange("r (o t) -> r o t", o=1).broadcast_to([NPART, KVH, TOK])).then_inc(rows_b, 16)
                    elif thread == "B" and name == "ff":
                        b = step[1]
                        sp.wait_ge(y_made, GB * ib + b + 1)
                        sp.dma_start(out[GB * ib + b], x2[:, b, :]).then_inc(out_stored, 16)
            sp.wait_ge(out_stored, 16 * B)

        @block.gpsimd
        def _(pool):
            n = 0
            pool.memset(idf[:], 0.0).then_inc(ident_step, 1)
            pool.wait_ge(ident_step, 1)
            pool.affine_select(out=idf[:], in_=idf[:], compare_op=ALU.not_equal, fill=1.0, base=0,
                               pattern=[[-1, P]], channel_multiplier=1).then_inc(idents, 1)
            pool.memset(half[:], -0.5).then_inc(picks, 1)
            pool.memset(va[:], 1.0).then_inc(ones_a, 1)
            pool.memset(pick[:, 0:1], 0.0).then_inc(picks, 1)
            pool.memset(pick[:, 1:2], 1.0).then_inc(picks, 1)
            pool.wait_ge(picks, 3)
            pool.memset(pick[0:2 * E, 0:1], 1.0).then_inc(picks, 1)
            pool.memset(pick[0:2 * E, 1:2], 0.0).then_inc(picks, 1)
            pool.memset(vx[:], 1.0).then_inc(ones_b, 1)
            pool.memset(one_row[:], 1.0).then_inc(ones_row, 1)
            pool.wait_ge(idents, 1)
            pool.tensor_copy(idb[:], idf[:]).then_inc(idents, 1)

            def split_max(i, b, ring, nm, np_, nr, steps_done, parts_done):
                base = 3 * (GB * i + b)
                ring.wait_emptied(pool, i, "s", b, HT - 1)
                pool.tensor_copy(np_[:, b, 0, :], nm[:, b, :]).then_inc(steps_done, 1)
                pool.wait_ge(steps_done, base + 1)
                pool.tensor_tensor(nr[:, 0, :], nm[:, b, :], np_[:, b, 0, :], ALU.subtract).then_inc(steps_done, 1)
                pool.wait_ge(steps_done, base + 2)
                pool.tensor_copy(np_[:, b, 1, :], nr[:, 0, :]).then_inc(steps_done, 1)
                pool.wait_ge(steps_done, base + 3)
                pool.tensor_tensor(np_[:, b, 2, :], nr[:, 0, :], np_[:, b, 1, :], ALU.subtract).then_inc(parts_done, 1)

            def rstd(n, mv, rs, stats, step_done, done):
                pool.wait_ge(stats, 3 * n + 3)
                pool.tensor_scalar(rs[:, 0:1], mv[:, 1:2], EPS, None, ALU.add).then_inc(step_done, 1)
                pool.wait_ge(step_done, n + 1)
                pool.tensor_tensor(rs[:, 1:2], rs[:, 0:1], half[:, 0:1], ALU.pow).then_inc(done, 1)

            for t, steps in turns:
                i, ib = t, t - 1
                for thread, *step in steps:
                    name = step[0]
                    if thread == "A" and step == ["xt", 0]:
                        pool.wait_ge(x_loaded, 16 * (i + 1))
                        if t == 0:
                            pool.wait_ge(ld_ob, 16)
                        else:
                            pool.wait_ge(x1_made, GB * i)
                        for b in range(GB):
                            pool.tensor_tensor(xb[:, b, :], x_in[:, b, :], obias[:], ALU.add).then_inc(xb_made, 1)
                    elif thread == "A" and name == "q":
                        j = step[1]
                        part, slot = (qp[:, 0], j) if j < 2 else (kp[:, 2], j - 2)
                        pool.wait_ge(a_second, 4 * i + j + 1)
                        mid = (qp if j < 2 else kp)[:, 1, 2 * slot:2 * slot + 2, :]
                        pool.tensor_tensor(part[:, 2 * slot:2 * slot + 2, :], wide_a[:, j % 2].rearrange("p (m t) -> p m t", m=2),
                                           mid, ALU.subtract).then_inc(a_third, 1)
                    elif thread == "A" and name == "mt":
                        split_max(i, step[1], ra, nma, npa, nra, max_split_a, max_parts_a)
                    elif thread == "A" and name == "op":
                        rstd(GB * i + step[1], mva, rsa, ln_a, rstd_step_a, rstd_a)
                    elif thread == "B" and name == "xt":
                        u = step[1]
                        if u == 0:
                            pool.wait_ge(c_loaded, 16 * (ib + 1))
                            for b in range(GB):
                                pool.tensor_copy(c_perm[:, b, :].rearrange("p (d g) -> p d g", d=HD), permuted(c_in[:, b, :])).then_inc(c_permuted, 1)
                        pool.wait_ge(b_second, 2 * ib + u + 1)
                        pool.tensor_tensor(kp[:, 0, 2 * u:2 * u + 2, :], wide_b[:, u].rearrange("p (m t) -> p m t", m=2),
                                           kp[:, 1, 2 * u:2 * u + 2, :], ALU.subtract).then_inc(b_third, 1)
                    elif thread == "B" and name == "ctx":
                        pool.wait_ge(c_second, ib + 1)
                        pool.tensor_tensor(cp[:, 2, :], rc[:], cp[:, 1, :], ALU.subtract).then_inc(c_third, 1)
                        pool.wait_ge(c_loaded, 16 * (ib + 1))
                        if ib > 0:
                            pool.wait_ge(pv_b, GB * KVH * ib)
                        for b in range(GB):
                            pool.tensor_copy(vx[:, b, :, 0:HD], c_in[:, b, :].rearrange("p (g d) -> p g d", d=HD)).then_inc(vx_made, 1)
                    elif thread == "B" and name == "mt":
                        split_max(ib, step[1], rb, nmb, npb, nrb, max_split_b, max_parts_b)
                    elif thread == "B" and name == "ot" and step[2] == 1:
                        rstd(2 * GB * ib + step[1], mvb, rsb, ln_b, rstd_step_b, rstd_b)
                    elif thread == "B" and step == ["cx", 1]:
                        rb.wait_full(pool, ib, "cx", 1)
                        if ib == 0:
                            pool.wait_ge(ld_fb, 16)
                        for b in range(GB):
                            pool.tensor_tensor(x2[:, b, :], x2[:, b, :], fbias[:], ALU.add).then_inc(x2_biased, 1)
                    elif thread == "B" and name == "is":
                        u = step[1]
                        pool.wait_ge(zh_made, 2 * ib + u + 1)
                        pool.tensor_tensor(zL[:, 2 * u:2 * u + 2, :], zf[:, 2 * u:2 * u + 2, :],
                                           zH[:, 2 * u:2 * u + 2, :].bitcast(F32), ALU.subtract).then_inc(zl_made, 1)
                    elif thread == "B" and name == "ff":
                        rstd(2 * GB * ib + GB + step[1], mvb, rsb, ln_b, rstd_step_b, rstd_b)
                    elif thread == "C" and name == "ow":
                        pool.wait_ge(ow_high, KT)
                        for kt in range(KT):
                            pool.tensor_tensor(owL[:, kt, :], oraw[:, kt, :], owH[:, kt, :].bitcast(F32), ALU.subtract).then_inc(ow_low, 1)

        @block.scalar
        def _(act):
            act.dma_start(obias[:], ob.partition_broadcast(P)).then_inc(ld_ob, 16)
            act.dma_start(vbias[:], qkvb[2 * H:3 * H].partition_broadcast(P)).then_inc(ld_vb, 16)
            act.dma_start(mraw[:], mask).then_inc(ld_mask, 16)
            act.dma_start(fbias[:], fb.partition_broadcast(P)).then_inc(ld_fb, 16)
            for k in range(4):
                act.dma_start(icr[k * E:(k + 1) * E], in_cs).then_inc(ld_cs, 16)
                act.dma_start(ocr[k * E:(k + 1) * E], out_cs).then_inc(ld_cs, 16)
            for blk in range(3):
                act.wait_ge(ld_w[blk], 16)
                for kt in range(KT):
                    act.activation(*w_views(wH, wraw, kt, blk), ACT.Copy).then_inc(w_high, 1)

            for t, steps in turns:
                i, ib = t, t - 1
                for thread, *step in steps:
                    name = step[0]
                    if thread == "A" and name == "xt":
                        u = step[1]
                        ra.wait_full(act, i, *step)
                        act.activation(xH[:, 2 * u:2 * u + 2, :], pa_bank(*step)[:].rearrange("p (m t) -> p m t", m=2), ACT.Copy).then_inc(xh_made, 1)
                    elif thread == "A" and name == "q":
                        j = step[1]
                        dst, slot, stored = (qp[:, 2], j, q_stored) if j < 2 else (kp[:, 0], j - 2, k_stored)
                        ra.wait_full(act, i, *step)
                        if t == 0 and j == 0:
                            rb.wait_emptied(act, 0, "small")
                        if t > 0:
                            act.wait_ge(stored, 16 * i)
                            if j >= 2:
                                act.wait_ge(x_stored, 16 * i)
                        for m in range(2):
                            last = act.activation(dst[:, 2 * slot + m, :], pa_bank(*step)[:, m * TOK:(m + 1) * TOK], ACT.Identity,
                                                  bias=bqk[:, 2 * j + m:2 * j + m + 1])
                        last.then_inc(a_first, 1)
                    elif name == "st":
                        b, j = step[1:]
                        k, ring, bank, pr, pv, scale = ((i, ra, pa_bank, pa, pv_a, HD ** -0.5) if thread == "A"
                                                        else (ib, rb, pb_bank, pb, pv_b, 1.0))
                        n = (GB * k + b) * HT + j
                        ring.wait_full(act, k, *step)
                        if n >= NP:
                            act.wait_ge(pv, n - NP + 1)
                        if thread == "B" and n == 0:
                            act.wait_ge(scales, 2)
                        act.activation(pr[:, n % NP, :], bank(*step)[:], ACT.Exp, scale=scale).then_inc(*ring.is_empty(*step))
                    elif name == "pv" and step[2] % 4 == 3:
                        b, u = step[1], step[2] // 4
                        k, ring, bank, wide, pv = (i, ra, pa_bank, wide_a, pv_a) if thread == "A" else (ib, rb, pb_bank, wide_b, pv_b)
                        act.wait_ge(pv, (GB * k + b) * HT + 4 * u + 4)
                        act.activation(wide[:, u, :], bank("pv", b, u)[:], ACT.Copy).then_inc(*ring.is_empty("pv", b, u))
                    elif thread == "A" and name == "ct":
                        ra.wait_full(act, i, *step)
                        act.activation(cH[:], pa_bank(*step)[:].rearrange("p (k t) -> p k t", k=KT), ACT.Copy).then_inc(ch_made, 1)
                    elif thread == "B" and name == "xt":
                        u = step[1]
                        rb.wait_full(act, ib, *step)
                        act.wait_ge(k_stored, 16 * (ib + 1))
                        act.activation(kp[:, 2, 2 * u:2 * u + 2, :], pb_bank(*step)[:].rearrange("p (m t) -> p m t", m=2), ACT.Copy,
                                       scale=HD ** -0.5).then_inc(b_first, 1)
                    elif thread == "B" and name == "ctx":
                        rb.wait_full(act, ib, *step)
                        if ib > 0:
                            act.wait_ge(c_stored, 16 * ib)
                        act.activation(cp[:, 0, :], pb_bank(*step)[:, 0:TOK], ACT.Copy).then_inc(c_first, 1)
                    elif thread == "B" and name == "cx":
                        u = step[1]
                        rb.wait_full(act, ib, *step)
                        act.activation(x2T[:, 2 * u:2 * u + 2, :], pb_bank(*step)[:].rearrange("p (m t) -> p m t", m=2), ACT.Copy).then_inc(*rb.is_empty(*step))
                    elif thread == "B" and name == "rl":
                        rb.wait_full(act, ib, *step)
                        act.activation(lg[:], pb_bank(*step)[0:E, 0:TOK], ACT.Copy).then_inc(*rb.is_empty(*step))
                    elif thread == "B" and name == "rt":
                        act.wait_ge(top_made, ib + 1)
                        for b in range(GB):
                            last = act.activation(el[:, b, :], pb_bank(*step)[:, b * E:(b + 1) * E], ACT.Exp, bias=nl[:, b:b + 1])
                        last.then_inc(*rb.is_empty(*step))
                    elif thread == "B" and name == "rr":
                        rb.wait_full(act, ib, *step)
                        act.activation(rT[:], pb_bank(*step)[0:4 * E, 0:TOK], ACT.Copy).then_inc(*rb.is_empty(*step))
                    elif thread == "B" and name == "is":
                        u = step[1]
                        rb.wait_emptied(act, ib, *step)
                        act.activation(zH[:, 2 * u:2 * u + 2, :], zf[:, 2 * u:2 * u + 2, :], ACT.Copy).then_inc(zh_made, 1)
                    elif thread == "B" and name == "os":
                        rb.wait_full(act, ib, *step)
                        if GB * ib + step[1] > 0:
                            kb, bb = (ib, 0) if step[1] else (ib - 1, 1)
                            rb.wait_emptied(act, kb, "ff", bb)
                        act.activation(osb[:], pb_bank(*step)[:], ACT.Copy).then_inc(*rb.is_empty(*step))
                    elif thread == "C" and name == "ow":
                        act.wait_ge(ld_ow, 16)
                        for kt in range(KT):
                            act.activation(owH[:, kt, :], oraw[:, kt, :], ACT.Copy).then_inc(ow_high, 1)
                    elif thread == "C" and name == "sign":
                        act.wait_ge(ld_fw, 16)
                        for k in range(KT):
                            act.activation(sgn[:, k, :], fraw[:, k, :], ACT.Sign).then_inc(signs, 1)

        @block.vector
        def _(dve):
            for blk in range(3):
                for kt in range(KT):
                    dve.wait_ge(w_high, KT * blk + kt + 1)
                    low, raw = w_views(wL, wraw, kt, blk)
                    high = wH[:, kt, blk * H:(blk + 1) * H].bitcast(F32)
                    if blk < 2:
                        high = high.rearrange("p (m d h) -> p m d h", m=KT, d=HD)
                    dve.tensor_tensor(low, raw, high, ALU.subtract).then_inc(w_low, 1)

            def normalise(n, v, st, mv, rs, stats, rstd_done, done):
                dve.wait_ge(stats, 3 * n + 1)
                dve.bn_stats(st[:], v).then_inc(stats, 1)
                dve.wait_ge(stats, 3 * n + 2)
                dve.bn_aggr(mv[:], st[:]).then_inc(stats, 1)
                dve.wait_ge(rstd_done, n + 1)
                dve.tensor_scalar(v, v, mv[:, 0:1], rs[:, 1:2], ALU.subtract, ALU.mult).then_inc(done, 1)

            for t, steps in turns:
                i, ib = t, t - 1
                for thread, *step in steps:
                    name = step[0]
                    if thread == "A" and name == "xt":
                        u = step[1]
                        dve.wait_ge(xh_made, 2 * i + u + 1)
                        dve.tensor_tensor(xL[:, 2 * u:2 * u + 2, :], pa_bank(*step)[:].rearrange("p (m t) -> p m t", m=2),
                                          xH[:, 2 * u:2 * u + 2, :].bitcast(F32), ALU.subtract).then_inc(*ra.is_empty(*step))
                    elif thread == "A" and name == "q":
                        j = step[1]
                        parts, slot, hi = (qp, j, 2) if j < 2 else (kp, j - 2, 0)
                        dve.wait_ge(a_first, 4 * i + j + 1)
                        if 4 * i + j >= 2:
                            dve.wait_ge(a_third, 4 * i + j - 1)
                        for m in range(2):
                            last = dve.scalar_tensor_tensor(wide_a[:, j % 2, m * TOK:(m + 1) * TOK], pa_bank(*step)[:, m * TOK:(m + 1) * TOK],
                                                            bqk[:, 2 * j + m:2 * j + m + 1], parts[:, hi, 2 * slot + m, :], ALU.add, ALU.subtract)
                        last.then_inc(*ra.is_empty(*step))
                        ra.wait_emptied(dve, i, *step)
                        dve.tensor_copy(parts[:, 1, 2 * slot:2 * slot + 2, :], wide_a[:, j % 2].rearrange("p (m t) -> p m t", m=2)).then_inc(a_second, 1)
                    elif thread == "A" and name == "v":
                        b = step[1]
                        ra.wait_full(dve, i, *step)
                        if t == 0 and b == 0:
                            dve.wait_ge(ld_vb, 16)
                            dve.wait_ge(ones_a, 1)
                        dve.tensor_tensor(va[:, b].rearrange("p (h m) w -> p m h w", m=KT)[:, :, :, 0:HD],
                                          pa_bank(*step)[:].rearrange("p (m h d) -> p m h d", m=KT, d=HD),
                                          vbias[:].rearrange("p (m h d) -> p m h d", m=KT, d=HD), ALU.add).then_inc(*ra.is_empty(*step))
                    elif thread == "A" and name == "s":
                        b, j = step[1:]
                        ra.wait_full(dve, i, *step)
                        dve.tensor_reduce(nma[:, b, 4 * j:4 * j + 4], pa_bank(*step)[:].rearrange("p (m t) -> p m t", m=KT), AX.X, ALU.max,
                                          negate=True).then_inc(*ra.is_empty(*step))
                    elif name == "mt":
                        b = step[1]
                        k, ring, bank, mr = (i, ra, pa_bank, mra) if thread == "A" else (ib, rb, pb_bank, mrb)
                        ring.wait_full(dve, k, *step)
                        dve.tensor_copy(mr[:, b, :], bank(*step)[0:NPART * HEADS, 0:P // 2].bitcast(BF16)).then_inc(*ring.is_empty(*step))
                    elif thread == "A" and name == "ot":
                        b, u = step[1:]
                        ra.wait_full(dve, i, *step)
                        v = pa_bank(*step)[:].rearrange("p (s c w) -> p s c w", s=4, w=VW)
                        rd = rda[:, 16 * u:16 * u + 16].rearrange("p (s c o) -> p s c o", s=4, o=1)
                        dve.reciprocal(rd, v[:, :, :, HD:HD + 1]).then_inc(recip_a, 1)
                        dve.wait_ge(recip_a, 2 * (GB * i + b) + u + 1)
                        dve.tensor_tensor(cx[:].rearrange("p (c u s d) -> p u s c d", c=KT, u=2, d=HD)[:, u], v[:, :, :, 0:HD],
                                          rd.broadcast_to([P, 4, 4, HD]), ALU.mult).then_inc(*ra.is_empty(*step))
                    elif thread == "A" and name == "ct":
                        dve.wait_ge(ch_made, GB * i + step[1] + 1)
                        dve.tensor_tensor(cL[:], pa_bank(*step)[:].rearrange("p (k t) -> p k t", k=KT), cH[:].bitcast(F32),
                                          ALU.subtract).then_inc(*ra.is_empty(*step))
                    elif thread == "A" and name == "op":
                        b = step[1]
                        n = GB * i + b
                        ra.wait_full(dve, i, *step)
                        dve.wait_ge(xb_made, n + 1)
                        dve.tensor_tensor(tile_permuted(x1[:, b, :]), by_head(pa_bank(*step)[:]), by_head(xb[:, b, :]), ALU.add).then_inc(*ra.is_empty(*step))
                        ra.wait_emptied(dve, i, *step)
                        dve.bn_stats(sta[:], x1[:, b, :]).then_inc(ln_a, 1)
                        dve.wait_ge(ln_a, 3 * n + 1)
                        dve.bn_aggr(mva[:], sta[:]).then_inc(ln_a, 2)
                        dve.wait_ge(rstd_a, n + 1)
                        dve.tensor_scalar(x1[:, b, :], x1[:, b, :], mva[:, 0:1], rsa[:, 1:2], ALU.subtract, ALU.mult).then_inc(x1_made, 1)
                    elif thread == "B" and name == "xt":
                        u = step[1]
                        dve.wait_ge(b_first, 2 * ib + u + 1)
                        v = wide_b[:, u].rearrange("p (m t) -> p m t", m=2)
                        dve.scalar_tensor_tensor(wide_b[:, u], pb_bank(*step)[:], HD ** -0.5, kp[:, 2, 2 * u:2 * u + 2, :].rearrange("p m t -> p (m t)"),
                                                 ALU.mult, ALU.subtract).then_inc(*rb.is_empty(*step))
                        rb.wait_emptied(dve, ib, *step)
                        dve.tensor_copy(kp[:, 1, 2 * u:2 * u + 2, :], v).then_inc(b_second, 1)
                    elif thread == "B" and name == "ctx":
                        dve.wait_ge(c_first, ib + 1)
                        dve.tensor_tensor(rc[:], pb_bank(*step)[:, 0:TOK], cp[:, 0, :], ALU.subtract).then_inc(*rb.is_empty(*step))
                        rb.wait_emptied(dve, ib, *step)
                        dve.tensor_copy(cp[:, 1, :], rc[:]).then_inc(c_second, 1)
                    elif thread == "B" and name == "s":
                        b, g = step[1:]
                        rb.wait_full(dve, ib, *step)
                        if g >= 2:
                            rb.wait_emptied(dve, ib, "s", b, g - 2)
                        elif b == 1:
                            rb.wait_emptied(dve, ib, "s", 0, g + 6)
                        for r in range(4):
                            col = (4 * (g % 2) + r) * KT + g // 2
                            last = dve.tensor_tensor_reduce(wide_b[:, g % 2, r * P:(r + 1) * P], pb_bank(*step)[:, r * P:(r + 1) * P], mraw[:], -1.0, -LOWEST,
                                                            ALU.add, ALU.min, nmb[:, b, col:col + 1])
                        last.then_inc(*rb.is_empty(*step))
                    elif thread == "B" and name == "ot":
                        b, u = step[1:]
                        n = 2 * GB * ib + b
                        rb.wait_full(dve, ib, *step)
                        v = pb_bank(*step)[:].rearrange("p (r c w) -> p r c w", r=4, w=VW)
                        rd = rdb[:, 16 * u:16 * u + 16].rearrange("p (r c o) -> p r c o", r=4, o=1)
                        dve.reciprocal(rd, v[:, :, :, HD:HD + 1]).then_inc(recip_b, 1)
                        dve.wait_ge(recip_b, 2 * (GB * ib + b) + u + 1)
                        if ib > 0 and u == 0:
                            dve.wait_ge(out_stored, 16 * (GB * (ib - 1) + b + 1))
                        dve.tensor_tensor(x2[:, b, :].rearrange("p (u c r d) -> p u r c d", u=2, c=4, d=HD)[:, u], v[:, :, :, 0:HD],
                                          rd.broadcast_to([P, 4, 4, HD]), ALU.mult).then_inc(*rb.is_empty(*step))
                        if u == 1:
                            rb.wait_emptied(dve, ib, "ot", b, 0)
                            rb.wait_emptied(dve, ib, "ot", b, 1)
                            dve.tensor_tensor(by_head(x2[:, b, :]), by_head(x2[:, b, :]), tile_permuted(x1[:, b, :]), ALU.add).then_inc(ln_b, 1)
                            normalise(n, x2[:, b, :], stb, mvb, rsb, ln_b, rstd_b, x2_made)
                    elif thread == "B" and name == "rt":
                        rb.wait_full(dve, ib, *step)
                        dve.tensor_reduce(nl[:], pb_bank(*step)[:, 0:GB * E].rearrange("p (b e) -> p b e", e=E), AX.X, ALU.max,
                                          negate=True).then_inc(top_made, 1)
                    elif thread == "B" and name == "rr":
                        rb.wait_emptied(dve, ib, "rt")
                        dve.tensor_reduce(sl[:], el[:], AX.X, ALU.add).then_inc(route_step, 1)
                        dve.wait_ge(route_step, 5 * ib + 1)
                        dve.reciprocal(rl[:], sl[:]).then_inc(route_step, 1)
                        dve.wait_ge(route_step, 5 * ib + 2)
                        dve.tensor_tensor(rt[:], el[:], rl[:].rearrange("p (b o) -> p b o", o=1).broadcast_to([P, GB, E]), ALU.mult).then_inc(route_step, 1)
                        dve.wait_ge(route_step, 5 * ib + 3)
                        dve.tensor_copy(rtH[:], rt[:]).then_inc(route_step, 1)
                        dve.wait_ge(route_step, 5 * ib + 4)
                        for k in (0, 2):
                            last = dve.tensor_copy(rts[:, :, k, :], rtH[:].bitcast(F32))
                            last = dve.tensor_tensor(rts[:, :, k + 1, :], rt[:], rtH[:].bitcast(F32), ALU.subtract)
                            last.then_inc(route_step if k == 0 else route_made, 1)
                    elif thread == "B" and name == "is":
                        u = step[1]
                        rb.wait_full(dve, ib, *step)
                        rb.wait_emptied(dve, ib, "cx", u)
                        dve.tensor_tensor(zf[:, 2 * u:2 * u + 2, :], pb_bank(*step)[:].rearrange("p (m t) -> p m t", m=2),
                                          x2T[:, 2 * u:2 * u + 2, :], ALU.mult).then_inc(*rb.is_empty(*step))
                    elif thread == "B" and name == "ff":
                        b = step[1]
                        n = 2 * GB * ib + GB + b
                        rb.wait_full(dve, ib, *step)
                        rb.wait_emptied(dve, ib, "os", b)
                        dve.tensor_tensor(wide_b[:, b], pb_bank(*step)[:], osb[:], ALU.mult).then_inc(*rb.is_empty(*step))
                        rb.wait_emptied(dve, ib, *step)
                        dve.wait_ge(x2_biased, GB * ib + b + 1)
                        dve.tensor_tensor(x2[:, b, :], wide_b[:, b], x2[:, b, :], ALU.add).then_inc(ln_b, 1)
                        normalise(n, x2[:, b, :], stb, mvb, rsb, ln_b, rstd_b, y_made)
                    elif thread == "C" and name == "small":
                        dve.wait_ge(ld_small, 32)
                        dve.tensor_copy(bperm[:].rearrange("p (d h) -> p d h", d=HD), permuted(braw[:])).then_inc(bias_permuted, 1)
                        rb.wait_full(dve, 0, "small")
                        dve.tensor_copy(bqk[:], pb_bank("small")[:, 0:2 * KT])
                        dve.tensor_copy(gT[:], pb_bank("small")[:, P:P + KT * E].rearrange("p (k e) -> p k e", e=E)).then_inc(*rb.is_empty("small"))
                    elif thread == "C" and name == "mask":
                        dve.wait_ge(ld_mask, 16)
                        dve.tensor_copy(mH[:], mraw[:]).then_inc(masks, 1)
                        dve.wait_ge(masks, 1)
                        dve.tensor_tensor(mL[:], mraw[:], mH[:].bitcast(F32), ALU.subtract).then_inc(masks, 1)
                        dve.wait_ge(idents, 1)
                        for r in range(4):
                            last = dve.tensor_copy(idr[:, r, :], idf[:])
                        last.then_inc(masks, 1)
                    elif thread == "C" and name == "swt":
                        rb.wait_full(dve, 0, *step)
                        dve.tensor_copy(swT[:, step[1], :], pb_bank(*step)[:, 0:H // 2].bitcast(BF16)).then_inc(*rb.is_empty(*step))
                    elif thread == "C" and name == "scales":
                        dve.wait_ge(ld_cs, 16 * 8)
                        dve.wait_ge(picks, 5)
                        for k, (raw, dst) in enumerate(((icr, icS), (ocr, ocS))):
                            dve.tensor_copy(cshi[:], raw[:]).then_inc(scale_step, 1)
                            dve.wait_ge(scale_step, 3 * k + 1)
                            dve.tensor_tensor(cslo[:], raw[:], cshi[:].bitcast(F32), ALU.subtract).then_inc(scale_step, 1)
                            dve.wait_ge(scale_step, 3 * k + 2)
                            dve.tensor_scalar(cslo[:], cslo[:], pick[:, 1:2], None, ALU.mult).then_inc(scale_step, 1)
                            dve.wait_ge(scale_step, 3 * k + 3)
                            dve.scalar_tensor_tensor(dst[:], cshi[:].bitcast(F32), pick[:, 0:1], cslo[:], ALU.mult, ALU.add).then_inc(scales, 1)
                            dve.wait_ge(scales, k + 1)

        @block.tensor
        def _(pe):
            def three(dst, left, right, start=True):
                (lh, ll), (rh, rl_) = left, right
                pe.matmul(dst, lh, rh, start=start, stop=False)
                pe.matmul(dst, lh, rl_, start=False, stop=False)
                return pe.matmul(dst, ll, rh, start=False, stop=False)

            def project(dst, lefts, rights):
                for kt in range(KT):
                    (lh, ll), (rh, rl_) = lefts(kt), rights(kt)
                    pe.matmul(dst, lh, rh, start=kt == 0, stop=False)
                    pe.matmul(dst, lh, rl_, start=False, stop=False)
                    last = pe.matmul(dst, ll, rh, start=False, stop=kt == KT - 1)
                return last

            for t, steps in turns:
                i, ib = t, t - 1
                for thread, *step in steps:
                    name = step[0]
                    if thread == "A" and name != "pv":
                        ra.wait_free(pe, i, *step)
                        dst = pa_bank(*step)
                    elif thread == "B" and name != "pv":
                        rb.wait_free(pe, ib, *step)
                        dst = pb_bank(*step)
                    if thread == "A" and name == "xt":
                        u = step[1]
                        pe.wait_ge(x_loaded, 16 * (i + 1))
                        if t == 0 and u == 0:
                            pe.wait_ge(idents, 1)
                        for m in range(2):
                            for b in range(GB):
                                kt = 2 * u + m
                                last = pe.transpose(dst[:, m * TOK + b * P:m * TOK + (b + 1) * P], x_in[:, b, kt * P:(kt + 1) * P], idf[:])
                        last.then_inc(*ra.is_full(*step))
                    elif thread == "A" and name == "q":
                        j = step[1]
                        if j == 0:
                            ra.wait_emptied(pe, i, "xt", 0)
                            ra.wait_emptied(pe, i, "xt", 1)
                        if t == 0 and j % 2 == 0:
                            pe.wait_ge(w_low, KT * (j // 2 + 1))
                        for m in range(2):
                            col = (2 * j + m) * P
                            last = project(dst[:, m * TOK:(m + 1) * TOK],
                                           lambda kt: (wH[:, kt, col:col + P], wL[:, kt, col:col + P]),
                                           lambda kt: (xH[:, kt, :], xL[:, kt, :]))
                        last.then_inc(*ra.is_full(*step))
                    elif thread == "A" and name == "v":
                        b = step[1]
                        if t == 0 and b == 0:
                            pe.wait_ge(w_low, 3 * KT)
                        project(dst[:], lambda kt: (xH[:, kt, tokens(b)], xL[:, kt, tokens(b)]),
                                lambda kt: (wH[:, kt, 2 * H:3 * H], wL[:, kt, 2 * H:3 * H])).then_inc(*ra.is_full(*step))
                    elif thread == "A" and name == "s":
                        b, j = step[1:]
                        if b == 0 and j == 0:
                            pe.wait_ge(q_stacked, 48 * (i + 1))
                            pe.wait_ge(k_stacked, 48 * (i + 1))
                        for m in range(KT):
                            last = pe.matmul(dst[:, m * P:(m + 1) * P], qs[0:SR, j, m, tokens(b)], ks[0:SR, j, m, tokens(b)], start=True, stop=True)
                        last.then_inc(*ra.is_full(*step))
                    elif name == "mt":
                        b = step[1]
                        k, ring, parts, done = (i, ra, npa, max_parts_a) if thread == "A" else (ib, rb, npb, max_parts_b)
                        if t <= 1:
                            pe.wait_ge(idents, 2)
                        pe.wait_ge(done, GB * k + b + 1)
                        pe.transpose(dst[0:NPART * HEADS, 0:P // 2].bitcast(BF16), parts[:, b].rearrange("p c h -> p (c h)"), idb[:]).then_inc(*ring.is_full(*step))
                    elif thread == "A" and name == "st":
                        b, j = step[1:]
                        if j == 0:
                            pe.wait_ge(max_stacked_a, 48 * (GB * i + b + 1))
                            if t == 0:
                                pe.wait_ge(rows_a, 16)
                        for m in range(KT):
                            last = pe.matmul(dst[:, m * P:(m + 1) * P], ks[0:SM, j, m, tokens(b)], qs[0:SM, j, m, tokens(b)], start=True, stop=True)
                        last.then_inc(*ra.is_full(*step))
                    elif thread == "A" and name == "pv":
                        b, j = step[1:]
                        n = (GB * i + b) * HT + j
                        if j % 4 == 0:
                            ra.wait_free(pe, i, "pv", b, j // 4)
                        dst = pa_bank("pv", b, j // 4)
                        ra.wait_emptied(pe, i, "st", b, j)
                        if j == 0:
                            ra.wait_emptied(pe, i, "v", b)
                        for m in range(KT):
                            last = pe.matmul(dst[m * VW:(m + 1) * VW, (j % 4) * P:(j % 4 + 1) * P], va[:, b, j * KT + m, :],
                                             pa[:, n % NP, m * P:(m + 1) * P], start=True, stop=True)
                        last.then_inc(pv_a, 1)
                    elif name == "ot":
                        b, u = step[1:]
                        k, ring, wide = (i, ra, wide_a) if thread == "A" else (ib, rb, wide_b)
                        ring.wait_emptied(pe, k, "pv", b, u)
                        for s in range(4):
                            last = pe.transpose(dst[:, s * P:(s + 1) * P], wide[:, u, s * P:(s + 1) * P], idf[:])
                        last.then_inc(*ring.is_full(*step))
                    elif thread == "A" and name == "ct":
                        b = step[1]
                        ra.wait_emptied(pe, i, "ot", b, 0)
                        ra.wait_emptied(pe, i, "ot", b, 1)
                        for kt in range(KT):
                            last = pe.transpose(dst[:, kt * P:(kt + 1) * P], cx[:, kt * P:(kt + 1) * P], idf[:])
                        last.then_inc(*ra.is_full(*step))
                    elif thread == "A" and name == "op":
                        b = step[1]
                        ra.wait_emptied(pe, i, "ct", b)
                        if t == 0 and b == 0:
                            pe.wait_ge(ow_low, KT)
                        project(dst[:], lambda kt: (cH[:, kt, :], cL[:, kt, :]),
                                lambda kt: (owH[:, kt, :], owL[:, kt, :])).then_inc(*ra.is_full(*step))
                    elif thread == "B" and name == "xt":
                        u = step[1]
                        pe.wait_ge(x1_made, GB * (ib + 1))
                        for m in range(2):
                            for b in range(GB):
                                kt = 2 * u + m
                                last = pe.transpose(dst[:, m * TOK + b * P:m * TOK + (b + 1) * P], x1[:, b, kt * P:(kt + 1) * P], idf[:])
                        last.then_inc(*rb.is_full(*step))
                    elif thread == "B" and name == "ctx":
                        pe.wait_ge(c_permuted, GB * (ib + 1))
                        for b in range(GB):
                            last = pe.transpose(dst[:, tokens(b)], c_perm[:, b, :], idf[:])
                        last.then_inc(*rb.is_full(*step))
                    elif thread == "B" and name == "s":
                        b, g = step[1:]
                        if b == 0 and g == 0:
                            pe.wait_ge(x_stacked, 48 * (ib + 1))
                            pe.wait_ge(c_stacked, 48 * (ib + 1))
                        for r in range(4):
                            last = pe.matmul(dst[:, r * P:(r + 1) * P], qx[0:SR, 4 * (g % 2) + r, g // 2, tokens(b)], kx[0:SR, g, tokens(b)],
                                             start=True, stop=True)
                        last.then_inc(*rb.is_full(*step))
                    elif thread == "B" and name == "st":
                        b, g = step[1:]
                        if g == 0:
                            pe.wait_ge(max_stacked_b, 48 * (GB * ib + b + 1))
                            if ib == 0:
                                pe.wait_ge(rows_b, 16)
                                pe.wait_ge(masks, 3)
                        d4 = dst[:].rearrange("p (r t) -> p r t", r=4)
                        pe.matmul(d4, mH[:], idr[:], start=True, stop=False)
                        pe.matmul(d4, mL[:], idr[:], start=False, stop=False)
                        a = 4 * (g % 2)
                        pe.matmul(d4, kx[0:SM, g, tokens(b)], qx[0:SM, a:a + 4, g // 2, tokens(b)], start=False, stop=True).then_inc(*rb.is_full(*step))
                    elif thread == "B" and name == "pv":
                        b, g = step[1:]
                        n = (GB * ib + b) * KVH + g
                        if g % 4 == 0:
                            rb.wait_free(pe, ib, "pv", b, g // 4)
                        dst = pb_bank("pv", b, g // 4)
                        rb.wait_emptied(pe, ib, "st", b, g)
                        if g == 0:
                            pe.wait_ge(vx_made, GB * ib + b + 1)
                        c = g % 4
                        pe.matmul(dst[c * VW:(c + 1) * VW, :], vx[:, b, g, :], pb[:, n % NP, :], start=True, stop=True).then_inc(pv_b, 1)
                    elif thread == "B" and name == "cx":
                        u = step[1]
                        pe.wait_ge(x2_made, GB * (ib + 1))
                        for m in range(2):
                            for b in range(GB):
                                kt = 2 * u + m
                                last = pe.transpose(dst[:, m * TOK + b * P:m * TOK + (b + 1) * P], x2[:, b, kt * P:(kt + 1) * P], idf[:])
                        last.then_inc(*rb.is_full(*step))
                    elif thread == "B" and name == "rl":
                        rb.wait_emptied(pe, ib, "cx", 0)
                        rb.wait_emptied(pe, ib, "cx", 1)
                        for kt in range(KT):
                            last = pe.matmul(dst[0:E, 0:TOK], gT[:, kt, :], x2T[:, kt, :], start=kt == 0, stop=kt == KT - 1)
                        last.then_inc(*rb.is_full(*step))
                    elif thread == "B" and name == "rt":
                        rb.wait_emptied(pe, ib, "rl")
                        for b in range(GB):
                            last = pe.transpose(dst[:, b * E:(b + 1) * E], lg[:, tokens(b)], idf[0:E, 0:E])
                        last.then_inc(*rb.is_full(*step))
                    elif thread == "B" and name == "rr":
                        pe.wait_ge(route_made, ib + 1)
                        for b in range(GB):
                            last = pe.transpose(dst[0:4 * E, tokens(b)], rts[:, b].rearrange("p k e -> p (k e)"), idf[:])
                        last.then_inc(*rb.is_full(*step))
                    elif thread == "B" and name == "is":
                        u = step[1]
                        rb.wait_emptied(pe, ib, "rr")
                        for m in range(2):
                            kt = 2 * u + m
                            last = pe.matmul(dst[:, m * TOK:(m + 1) * TOK], icS[:, kt * P:(kt + 1) * P], rT[:], start=True, stop=True)
                        last.then_inc(*rb.is_full(*step))
                    elif thread == "B" and name == "os":
                        pe.matmul(dst[:], rT[:, tokens(step[1])], ocS[:], start=True, stop=True).then_inc(*rb.is_full(*step))
                    elif thread == "B" and name == "ff":
                        b = step[1]
                        pe.wait_ge(zh_made, 2 * (ib + 1))
                        pe.wait_ge(zl_made, 2 * (ib + 1))
                        for kt in range(KT):
                            pe.matmul(dst[:], zH[:, kt, tokens(b)], swT[:, kt, :], start=kt == 0, stop=False)
                            last = pe.matmul(dst[:], zL[:, kt, tokens(b)], swT[:, kt, :], start=False, stop=kt == KT - 1)
                        last.then_inc(*rb.is_full(*step))
                    elif thread == "C" and name == "small":
                        pe.wait_ge(idents, 1)
                        pe.wait_ge(ld_small, 32)
                        pe.wait_ge(bias_permuted, 1)
                        dst = pb_bank("small")
                        pe.transpose(dst[:, 0:2 * KT], bperm[:], idf[0:2 * KT, 0:2 * KT])
                        for kt in range(KT):
                            last = pe.transpose(dst[:, P + kt * E:P + (kt + 1) * E], graw[:, kt * P:(kt + 1) * P], idf[0:E, 0:E])
                        last.then_inc(*rb.is_full("small"))
                    elif thread == "C" and name == "swt":
                        kt = step[1]
                        rb.wait_free(pe, 0, *step)
                        if kt == 0:
                            pe.wait_ge(signs, KT)
                            pe.wait_ge(idents, 2)
                        dst = pb_bank(*step)[:, 0:H // 2].bitcast(BF16)
                        for o in range(KT):
                            last = pe.transpose(dst[:, o * P:(o + 1) * P], sgn[:, o, kt * P:(kt + 1) * P], idb[:])
                        last.then_inc(*rb.is_full(*step))


_INS = ["x", "ctx_1024", "mask_SxS2_ff0", "L0_attn_attn_qkvw", "L0_attn_attn_qkvb", "L0_attn_attn_ow", "L0_attn_attn_ob",
        "L0_ffn_weight", "L0_ffn_bias", "L0_ffn_gate_w", "L0_ffn_in_channel_scale", "L0_ffn_out_channel_scale"]


def kernel(**inputs):
    import numpy as _np
    import concourse.bacc as _bacc
    from concourse import mybir as _mybir
    from concourse.bass_utils import run_bass_kernel_spmd as _run

    nc = _bacc.Bacc("TRN2", target_bir_lowering=False, num_devices=1, dynamic_dma_scratch_size=1024)
    arrays, args = {}, []
    for name in _INS:
        a = _np.ascontiguousarray(inputs[name])
        arrays[f"in_{name}_dram"] = a
        args.append(nc.dram_tensor(f"in_{name}_dram", a.shape, _mybir.dt.from_np(a.dtype), kind="ExternalInput").ap())
    args.append(nc.dram_tensor("out_0_dram", (B, P, H), F32, kind="ExternalOutput").ap())
    for name, heads, cols in (("scr_q", HT, KT * TOK), ("scr_k", HT, KT * TOK), ("scr_x", HT, KT * TOK), ("scr_c", KVH, TOK)):
        args.append(nc.dram_tensor(name, (NG, NPART * HD, heads, cols), BF16, kind="Internal").ap())
    decoder_layer(nc, *args)
    r = _run(nc, [arrays], core_ids=[0])
    return r.results[0]["out_0_dram"]
```

```python
from contextlib import ExitStack

import concourse.bass as bass
from concourse import mybir

F32 = mybir.dt.float32
F32R = mybir.dt.float32r
BF16 = mybir.dt.bfloat16
ALU = mybir.AluOpType
ACT = mybir.ActivationFunctionType
AX = mybir.AxisListType

P = 128
B = 8
GB = 2
NG = B // GB
TOK = GB * P
H = 512
KT = H // P
HEADS = 32
HD = H // HEADS
KVH = 8
HT = P // HD
E = 8
NPART = 3
SR = 6 * HD
SM = SR + NPART
VW = 32
NP = 2
EPS = 1e-5
LOWEST = -3.0e38
QBLK = 3 * H


class Ring:

    def __init__(self, thread, full, empty, turns):
        self.full, self.empty = full, empty
        self.slot = {}
        self.count = {}
        uses = [0] * 4
        for t, steps in turns:
            for th, lag, *name in steps:
                if th == thread and name[0] in NOT_IN_RING or th != thread and (th != "C" or thread != "B"):
                    continue
                if th == "C" and name[0] not in ("small", "swt"):
                    continue
                if name[0] == "pv":
                    if name[2] % 4:
                        continue
                    name = ["pv", name[1], name[2] // 4]
                unit = tuple(name)
                if unit not in self.slot:
                    self.slot[unit] = (3, lag)
                    if unit[0] != "pv":
                        place = full_order(thread).index(unit) if th != "C" else ORDER_C.index(unit)
                        self.slot[unit] = (place % 3, lag)
                k = self.slot[unit][0]
                self.count[unit, t] = uses[k]
                uses[k] += 1

    def before(self, i, unit):
        lag = self.slot[unit][1]
        if isinstance(i, int):
            return self.count[unit, i + lag]
        base, per = self.count[unit, 1], self.count[unit, 2] - self.count[unit, 1]
        return i * per + (base + (lag - 1) * per)

    def bank(self, *name):
        return self.slot[name][0]

    def wait_full(self, eng, i, *name):
        eng.wait_ge(self.full[self.bank(*name)], self.before(i, name) + 1)

    def wait_emptied(self, eng, i, *name):
        eng.wait_ge(self.empty[self.bank(*name)], self.before(i, name) + 1)

    def wait_free(self, eng, i, *name):
        n = self.before(i, name)
        if not isinstance(n, int) or n > 0:
            eng.wait_ge(self.empty[self.bank(*name)], n)

    def is_full(self, *name):
        return self.full[self.bank(*name)], 1

    def is_empty(self, *name):
        return self.empty[self.bank(*name)], 1


NOT_IN_RING = ("xb", "lc", "cp", "ldq", "ldk", "ldx", "ldc", "n1", "n2", "n3")
ORDER_C = [("small",)] + [("swt", k) for k in range(4)]


LAG = 2


def schedule():
    s = []

    def a(name, *idx, lag=0):
        s.append(("A", lag, name, *idx))

    def b(name, *idx):
        s.append(("B", 1, name, *idx))

    a("xt", 0); a("xt", 1)
    a("ot", 1, 0, lag=1)
    a("ot", 1, 1, lag=1)
    b("xt", 0)
    b("ctx")
    a("ct", 1, lag=1)
    b("ldx", 0)
    b("ldc")
    a("q", 0)
    a("op", 1, lag=1)
    a("q", 1)
    a("n1", 1, lag=1)
    b("xt", 1)
    a("ldq")
    a("q", 2)
    b("ldx", 1)
    fill = {2: ("q", 3), 5: ("v", 0), 8: ("v", 1)}
    for n in range(16):
        b("s", n // 8, n % 8)
        if n in fill:
            a(*fill[n])
        if n == 2:
            a("ldk")
            a("xb")
            a("lc")
        if n == 10:
            b("mt", 0)
    beside = {
        (0, 1): lambda: b("mt", 1),
        (0, 7): lambda: a("mt", 0),
        (1, 2): lambda: b("ot", 0, 0), (1, 3): lambda: b("ot", 0, 1), (1, 5): lambda: b("n2", 0), (1, 7): lambda: a("mt", 1),
    }
    for j in range(3):
        a("s", 0, j)
    for n in range(16 + LAG):
        if n + 3 < 16:
            a("s", *divmod(n + 3, HT))
        if n < 16:
            b("st", *divmod(n, HT))
        if n >= LAG:
            b("pv", *divmod(n - LAG, HT))
        if divmod(n, HT) in beside:
            beside[divmod(n, HT)]()
    beside = {
        (0, 0): [("B", "ot", 1, 0)], (0, 1): [("B", "ot", 1, 1)],
        (0, 3): [("B", "n2", 1)],
        (0, 5): [("B", "cx", 0)], (0, 6): [("B", "cx", 1)], (0, 7): [("B", "rl")],
        (1, 0): [("B", "rt")], (1, 2): [("A", "ot", 0, 0), ("A", "ot", 0, 1)],
        (1, 4): [("B", "rr"), ("A", "ct", 0)],
        (1, 5): [("A", "op", 0)], (1, 6): [("B", "is", 0)], (1, 7): [("B", "is", 1)],
    }
    for n in range(16 + LAG):
        if n < 16:
            a("st", *divmod(n, HT))
        if n >= LAG:
            a("pv", *divmod(n - LAG, HT))
        for th, *name in beside.get(divmod(n, HT), []):
            (a if th == "A" else b)(*name)
    a("n1", 0)
    a("cp")
    b("os", 0)
    b("ff", 0)
    b("os", 1)
    b("ff", 1)
    b("n3", 0)
    b("n3", 1)
    return s


def first_turn():
    s = [x for x in schedule() if x[1] == 0]
    start = [("C", "w", 0), ("A", "xt", 0), ("A", "xt", 1), ("C", "small"), ("A", "q", 0), ("C", "w", 1), ("A", "q", 1), ("C", "w", 2), ("A", "ldq"),
             ("A", "q", 2), ("A", "q", 3), ("A", "ldk"), ("A", "v", 0), ("C", "mask"), ("C", "ow"), ("A", "v", 1),
             ("A", "xb"), ("A", "lc"), ("C", "sign")]
    start = [(th, 0, *name) for th, *name in start]
    s = start + [x for x in s if x not in start]

    def insert(at, steps):
        k = s.index(at)
        s[k:k] = [("C", 0, *x) for x in steps]
    insert(("A", 0, "s", 1, 0), [("swt", 0), ("swt", 1)])
    insert(("A", 0, "st", 0, 0), [("swt", 2), ("swt", 3), ("scales",)])
    return s


def all_turns():
    return [(0, first_turn())] + [(t, schedule()) for t in range(1, NG)] + [(NG, [x for x in schedule() if x[1] == 1])]


def full_order(thread):
    return [tuple(x[2:]) for x in schedule() if x[0] == thread and x[2] not in NOT_IN_RING + ("pv",)]


def decoder_layer(nc, x, ctx_1024, mask, qkvw, qkvb, ow, ob, fw, fb, gate_w, in_cs, out_cs, out, scr_q, scr_k, scr_x, scr_c):
    es = ExitStack()
    with es:
        def sb(name, shape, dt):
            return es.enter_context(nc.sbuf_tensor(name, shape, dt))

        def sem(name):
            return es.enter_context(nc.semaphore(name))

        wH = sb("wH", [P, KT, QBLK], F32R)
        wL = sb("wL", [P, KT, QBLK], F32R)
        owH = sb("owH", [P, KT, H], F32R)
        owL = sb("owL", [P, KT, H], F32R)
        swT = sb("swT", [P, KT, H], F32R)
        gT = sb("gT", [P, KT, E], F32)
        icS = sb("icS", [4 * E, H], F32R)
        ocS = sb("ocS", [4 * E, H], F32R)
        bqk = sb("bqk", [P, 2 * KT], F32)
        vbias = sb("vbias", [P, H], F32)
        obias = sb("obias", [P, H], F32)
        fbias = sb("fbias", [P, H], F32)
        mraw = sb("mraw", [P, P], F32)
        mH = sb("mH", [P, P], F32R)
        mL = sb("mL", [P, P], F32R)
        idf = sb("idf", [P, P], F32)
        idb = sb("idb", [P, P], BF16)
        idr = sb("idr", [P, 4, P], F32R)
        pick = sb("pick", [4 * E, 2], F32)
        one_row = sb("one_row", [NPART, TOK], BF16)
        half = sb("half", [P, 2], F32)
        x_in = sb("x_in", [P, GB, H], F32)
        xb = sb("xb", [P, GB, H], F32)
        xH = sb("xH", [P, KT, TOK], F32R)
        xL = sb("xL", [P, KT, TOK], F32R)
        qs = sb("qs", [P, HT, KT, TOK], BF16)
        ks = sb("ks", [P, HT, KT, TOK], BF16)
        qp = sb("qp", [P, NPART, KT, TOK], BF16)
        kp = sb("kp", [P, NPART, KT, TOK], BF16)
        wide_a = sb("wide_a", [P, 2, H], F32)
        va = sb("va", [P, GB, HEADS, VW], F32)
        pa = sb("pa", [P, NP, H], F32)
        nma = sb("nma", [P, GB, HEADS], F32)
        npa = sb("npa", [P, GB, NPART, HEADS], BF16)
        nra = sb("nra", [P, 2, HEADS], F32)
        mra = sb("mra", [NPART * HEADS, GB, P], BF16)
        cx = sb("cx", [P, H], F32)
        cH = sb("cH", [P, KT, P], F32R)
        cL = sb("cL", [P, KT, P], F32R)
        rda = sb("rda", [P, HEADS], F32)
        x1 = sb("x1", [P, GB, H], F32)
        sta = sb("sta", [P, 6], F32)
        mva = sb("mva", [P, GB, 2], F32)
        rsa = sb("rsa", [P, GB, 2], F32)
        c_in = sb("c_in", [P, GB, P], F32)
        c_perm = sb("c_perm", [P, GB, P], F32)
        xp = sb("xp", [P, NPART, GB * KT * P], BF16)
        qx = sb("qx", [P, GB, HT, KT, P], BF16)
        kx = sb("kx", [P, KVH, TOK], BF16)
        cp = sb("cp", [P, NPART, TOK], BF16)
        wide_b = sb("wide_b", [P, 2, H], F32)
        vx = sb("vx", [P, GB, KVH, VW], F32)
        pb = sb("pb", [P, NP, H], F32)
        nmb = sb("nmb", [P, GB, HEADS], F32)
        npb = sb("npb", [P, GB, NPART, HEADS], BF16)
        nrb = sb("nrb", [P, 2, HEADS], F32)
        mrb = sb("mrb", [NPART * HEADS, GB, P], BF16)
        rdb = sb("rdb", [P, HEADS], F32)
        x2 = sb("x2", [P, GB, H], F32)
        stb = sb("stb", [P, 6], F32)
        mvb = sb("mvb", [P, GB, 2], F32)
        rsb = sb("rsb", [P, GB, 2], F32)
        lg = sb("lg", [E, TOK], F32)
        nl = sb("nl", [P, GB], F32)
        el = sb("el", [P, GB, E], F32)
        sl = sb("sl", [P, GB], F32)
        rl = sb("rl", [P, GB], F32)
        rt = sb("rt", [P, GB, E], F32)
        rtH = sb("rtH", [P, GB, E], F32R)
        rts = sb("rts", [P, GB, 4, E], F32)
        rT = sb("rT", [4 * E, TOK], F32R)

        def at(name, shape, dt, host, skip=0):
            return nc.alloc_sbuf_tensor_at(name, shape, dt, offset=nc.lookup_mloc(host).addr + skip)

        KB = 1024
        wraw = at("wraw", [P, KT, QBLK], F32, qs)
        oraw = at("oraw", [P, KT, H], F32, qx)
        fraw = at("fraw", [P, KT, H], F32, qx, 8 * KB)
        sgn = at("sgn", [P, KT, H], BF16, kx)
        rc = at("rc", [P, TOK], F32, pb, 2 * KB)
        osb = at("osb", [P, H], F32, pb)
        icr = at("icr", [4 * E, H], F32, pb)
        ocr = at("ocr", [4 * E, H], F32, pb, 2 * KB)
        cshi = at("cshi", [4 * E, H], F32R, wide_b)
        cslo = at("cslo", [4 * E, H], F32, wide_b, 2 * KB)
        graw = at("graw", [E, H], F32, x2)
        braw = at("braw", [2 * KT, P], F32, x2, 2 * KB)
        bperm = at("bperm", [2 * KT, P], F32, x2, 3 * KB)
        x2T = at("x2T", [P, KT, TOK], F32, qx)
        zf = at("zf", [P, KT, TOK], F32, qx, 4 * KB)
        zH = at("zH", [P, KT, TOK], F32R, qx, 8 * KB)
        zL = at("zL", [P, KT, TOK], F32R, qx, 12 * KB)

        bank_a = [es.enter_context(nc.psum_tensor(f"bank_a{k}", [P, H], F32)) for k in range(4)]
        bank_b = [es.enter_context(nc.psum_tensor(f"bank_b{k}", [P, H], F32)) for k in range(4)]
        turns = all_turns()
        ra = Ring("A", [sem(f"full_a{k}") for k in range(4)], [sem(f"empty_a{k}") for k in range(4)], turns)
        rb = Ring("B", [sem(f"full_b{k}") for k in range(4)], [sem(f"empty_b{k}") for k in range(4)], turns)

        def pa_bank(*name):
            return bank_a[ra.bank(*name)]

        def pb_bank(*name):
            return bank_b[rb.bank(*name)]

        ld_small, ld_mask, ld_ow, ld_fw, ld_cs = (sem(n) for n in ("ld_small", "ld_mask", "ld_ow", "ld_fw", "ld_cs"))
        ld_w = [sem(f"ld_w{k}") for k in range(3)]
        ld_vb, ld_ob, ld_fb = sem("ld_vb"), sem("ld_ob"), sem("ld_fb")
        idents, w_high, w_low = sem("idents"), sem("w_high"), sem("w_low")
        ow_high, ow_low, signs, masks = sem("ow_high"), sem("ow_low"), sem("signs"), sem("masks")
        scale_step, scales, ones_a, ones_b, picks = sem("scale_step"), sem("scales"), sem("ones_a"), sem("ones_b"), sem("picks")
        ident_step, ones_row, rows_a, rows_b = sem("ident_step"), sem("ones_row"), sem("rows_a"), sem("rows_b")
        x_loaded, xb_made, xh_made = sem("x_loaded"), sem("xb_made"), sem("xh_made")
        a_first, a_second, a_third = sem("a_first"), sem("a_second"), sem("a_third")
        q_stored, k_stored, q_stacked, k_stacked = sem("q_stored"), sem("k_stored"), sem("q_stacked"), sem("k_stacked")
        max_split_a, max_parts_a = sem("max_split_a"), sem("max_parts_a")
        max_stacked_a = [sem(f"max_stacked_a{b}") for b in range(GB)]
        pv_a, recip_a, ch_made = sem("pv_a"), sem("recip_a"), sem("ch_made")
        ln_a, rstd_step_a, rstd_a, x1_made = sem("ln_a"), sem("rstd_step_a"), sem("rstd_a"), sem("x1_made")
        c_loaded, c_permuted, vx_made = sem("c_loaded"), sem("c_permuted"), sem("vx_made")
        bias_permuted = sem("bias_permuted")
        b_first, b_second, b_third = sem("b_first"), sem("b_second"), sem("b_third")
        c_first, c_second, c_third = sem("c_first"), sem("c_second"), sem("c_third")
        x_stored, c_stored, c_stacked = sem("x_stored"), sem("c_stored"), sem("c_stacked")
        x_stacked = [sem(f"x_stacked{b}") for b in range(GB)]
        max_split_b, max_parts_b = sem("max_split_b"), sem("max_parts_b")
        max_stacked_b = [sem(f"max_stacked_b{b}") for b in range(GB)]
        pv_b, recip_b = sem("pv_b"), sem("recip_b")
        ln_b, rstd_step_b, rstd_b, x2_made, x2_biased = sem("ln_b"), sem("rstd_step_b"), sem("rstd_b"), sem("x2_made"), sem("x2_biased")
        top_made, exp_made, route_step, route_made = sem("top_made"), sem("exp_made"), sem("route_step"), sem("route_made")
        zh_made, zl_made, y_made, out_stored = sem("zh_made"), sem("zl_made"), sem("y_made"), sem("out_stored")


        def permuted(ap):
            return ap.rearrange("p (h d) -> p d h", d=HD)

        def by_head(ap):
            return ap.rearrange("p (m h d) -> p m h d", m=KT, d=HD)

        def tile_permuted(ap):
            return ap.rearrange("p (m d h) -> p m h d", m=KT, d=HD)

        def tokens(b):
            return slice(b * P, (b + 1) * P)

        def w_views(dst, src, kt, blk):
            to, of = dst[:, kt, blk * H:(blk + 1) * H], src[:, kt, blk * H:(blk + 1) * H]
            if blk == 2:
                return to, of
            return to.rearrange("p (m d h) -> p m d h", m=KT, d=HD), of.rearrange("p (m h d) -> p m d h", m=KT, d=HD)

        block = es.enter_context(nc.Block())

        @block.sync
        def _(sp):
            def load_x(i):
                sp.dma_start(x_in[:], x[GB * i:GB * (i + 1)].rearrange("b p f -> p b f")).then_inc(x_loaded, 16)

            def load_c(i):
                sp.dma_start(c_in[:], ctx_1024[GB * i:GB * (i + 1)].rearrange("b p f -> p b f")).then_inc(c_loaded, 16)

            def stack(dst, scratch, lows_first, done):
                n = 2 if lows_first else 0
                for row, first, last in ((0, 0, NPART), (3, n // 2, n // 2 + 2), (5, n, n + 1)):
                    src = scratch[first * HD:last * HD]
                    sp.dma_start(dst[row * HD:(row + last - first) * HD], src).then_inc(done, 16)

            wv = qkvw.rearrange("(kt p) n -> p kt n", p=P)
            sp.dma_start(wraw[:, :, 0:H], wv[:, :, 0:H]).then_inc(ld_w[0], 16)
            sp.dma_start(braw[:], qkvb[0:2 * H].rearrange("(t p) -> t p", p=P)).then_inc(ld_small, 16)
            sp.dma_start(graw[:], gate_w).then_inc(ld_small, 16)
            sp.dma_start(wraw[:, :, H:2 * H], wv[:, :, H:2 * H]).then_inc(ld_w[1], 16)
            sp.dma_start(wraw[:, :, 2 * H:3 * H], wv[:, :, 2 * H:3 * H]).then_inc(ld_w[2], 16)
            sp.dma_start(vbias[:], qkvb[2 * H:3 * H].partition_broadcast(P)).then_inc(ld_vb, 16)
            sp.dma_start(oraw[:], ow.rearrange("(kt p) n -> p kt n", p=P)).then_inc(ld_ow, 16)
            sp.dma_start(fraw[:], fw.rearrange("(ot p) n -> p ot n", p=P)).then_inc(ld_fw, 16)
            sp.dma_start(obias[:], ob.partition_broadcast(P)).then_inc(ld_ob, 16)
            sp.dma_start(mraw[:], mask).then_inc(ld_mask, 16)
            sp.dma_start(fbias[:], fb.partition_broadcast(P)).then_inc(ld_fb, 16)
            for k in range(4):
                sp.dma_start(icr[k * E:(k + 1) * E], in_cs).then_inc(ld_cs, 16)
                sp.dma_start(ocr[k * E:(k + 1) * E], out_cs).then_inc(ld_cs, 16)

            for t, steps in turns:
                for thread, lag, *step in steps:
                    i = ib = t - lag
                    name = step[0]
                    if thread == "B" and name == "xt":
                        b = step[1]
                        sp.wait_ge(b_third, GB * ib + b + 1)
                        part = slice(b * H, (b + 1) * H)
                        sp.dma_start(scr_x[ib].rearrange("(c d) h f -> (d h) c f", d=HD)[:, :, part],
                                     xp[:, :, part]).then_inc(x_stored, 16)
                    elif name == "ldx":
                        b = step[1]
                        part = slice(b * H, (b + 1) * H)
                        sp.wait_ge(x_stored, 16 * (GB * ib + b + 1))
                        if ib > 0:
                            rb.wait_full(sp, ib - 1, "ff", 1)
                        stack(qx[:, b].rearrange("r h m t -> r h (m t)"), scr_x[ib][:, :, part], True, x_stacked[b])
                    elif thread == "B" and name == "ctx":
                        sp.wait_ge(c_third, ib + 1)
                        sp.dma_start(scr_c[ib].rearrange("(c d) h f -> (d h) c f", d=HD), cp[:]).then_inc(c_stored, 16)
                    elif name == "ldc":
                        sp.wait_ge(c_stored, 16 * (ib + 1))
                        stack(kx[:], scr_c[ib], False, c_stacked)
                    elif thread == "A" and step == ["q", 1]:
                        sp.wait_ge(a_third, 4 * i + 2)
                        sp.dma_start(scr_q[i].rearrange("(c d) h f -> (d h) c f", d=HD),
                                     qp[:].rearrange("p c m t -> p c (m t)")).then_inc(q_stored, 16)
                    elif name == "ldq":
                        sp.wait_ge(q_stored, 16 * (i + 1))
                        if i == 0:
                            sp.wait_ge(w_low, 3 * KT)
                        stack(qs[:].rearrange("r h m t -> r h (m t)"), scr_q[i], True, q_stacked)
                    elif thread == "A" and step == ["q", 3]:
                        sp.wait_ge(a_third, 4 * i + 4)
                        sp.dma_start(scr_k[i].rearrange("(c d) h f -> (d h) c f", d=HD),
                                     kp[:].rearrange("p c m t -> p c (m t)")).then_inc(k_stored, 16)
                    elif name == "ldk":
                        sp.wait_ge(k_stored, 16 * (i + 1))
                        stack(ks[:].rearrange("r h m t -> r h (m t)"), scr_k[i], False, k_stacked)
                    elif thread == "A" and name == "xb":
                        if i < NG - 1:
                            ra.wait_full(sp, i, "xt", 1)
                            sp.wait_ge(xb_made, GB * (i + 1))
                            load_x(i + 1)
                    elif name == "mt":
                        b = step[1]
                        k, src, dst, done, ring = (i, mra, qs, max_stacked_a[b], ra) if thread == "A" else (ib, mrb, qx, max_stacked_b[b], rb)
                        ring.wait_emptied(sp, k, "mt", b)
                        for c in range(NPART):
                            row = dst[SR + c:SR + c + 1, :, :, tokens(b)] if thread == "A" else dst[SR + c:SR + c + 1, b]
                            sp.dma_start(row.rearrange("r h m t -> r (h m) t"),
                                         src[c * HEADS:(c + 1) * HEADS, b, :]).then_inc(done, 16)
                    elif thread == "A" and name == "lc":
                        if i > 0:
                            sp.wait_ge(c_permuted, GB * i)
                            sp.wait_ge(vx_made, GB * i)
                        load_c(i)
                    elif thread == "C" and name == "ow":
                        sp.wait_ge(ones_row, 1)
                        sp.wait_ge(w_low, 3 * KT)
                        sp.dma_start(ks[SR:SM].rearrange("r h m t -> r (h m) t"),
                                     one_row[:].rearrange("r (o t) -> r o t", o=1).broadcast_to([NPART, HT * KT, TOK])).then_inc(rows_a, 16)
                    elif thread == "C" and step == ["swt", 3]:
                        rb.wait_full(sp, 0, "swt", 3)
                        sp.dma_start(kx[SR:SM], one_row[:].rearrange("r (o t) -> r o t", o=1).broadcast_to([NPART, KVH, TOK])).then_inc(rows_b, 16)
                    elif thread == "B" and name == "n3":
                        b = step[1]
                        sp.wait_ge(y_made, GB * ib + b + 1)
                        sp.dma_start(out[GB * ib + b], x2[:, b, :]).then_inc(out_stored, 16)
            sp.wait_ge(out_stored, 16 * B)

        @block.gpsimd
        def _(pool):
            n = 0
            pool.memset(idf[:], 0.0).then_inc(ident_step, 1)
            pool.wait_ge(ident_step, 1)
            pool.affine_select(out=idf[:], in_=idf[:], compare_op=ALU.not_equal, fill=1.0, base=0,
                               pattern=[[-1, P]], channel_multiplier=1).then_inc(idents, 1)
            pool.memset(half[:], -0.5).then_inc(picks, 1)
            pool.memset(va[:], 1.0).then_inc(ones_a, 1)
            pool.memset(pick[:, 0:1], 0.0).then_inc(picks, 1)
            pool.memset(pick[:, 1:2], 1.0).then_inc(picks, 1)
            pool.wait_ge(picks, 3)
            pool.memset(pick[0:2 * E, 0:1], 1.0).then_inc(picks, 1)
            pool.memset(pick[0:2 * E, 1:2], 0.0).then_inc(picks, 1)
            pool.memset(vx[:], 1.0).then_inc(ones_b, 1)
            pool.memset(one_row[:], 1.0).then_inc(ones_row, 1)
            pool.wait_ge(idents, 1)
            pool.tensor_copy(idb[:], idf[:]).then_inc(idents, 1)

            def split_max(i, b, ring, nm, np_, nr, steps_done, parts_done):
                base = 3 * (GB * i + b)
                ring.wait_emptied(pool, i, "s", b, HT - 1)
                pool.tensor_copy(np_[:, b, 0, :], nm[:, b, :]).then_inc(steps_done, 1)
                pool.wait_ge(steps_done, base + 1)
                pool.tensor_tensor(nr[:, 0, :], nm[:, b, :], np_[:, b, 0, :], ALU.subtract).then_inc(steps_done, 1)
                pool.wait_ge(steps_done, base + 2)
                pool.tensor_copy(np_[:, b, 1, :], nr[:, 0, :]).then_inc(steps_done, 1)
                pool.wait_ge(steps_done, base + 3)
                pool.tensor_tensor(np_[:, b, 2, :], nr[:, 0, :], np_[:, b, 1, :], ALU.subtract).then_inc(parts_done, 1)

            def rstd(n, mv, rs, stats, step_done, done):
                pool.wait_ge(stats, 3 * n + 3)
                pool.tensor_scalar(rs[:, 0:1], mv[:, 1:2], EPS, None, ALU.add).then_inc(step_done, 1)
                pool.wait_ge(step_done, n + 1)
                pool.tensor_tensor(rs[:, 1:2], rs[:, 0:1], half[:, 0:1], ALU.pow).then_inc(done, 1)

            for t, steps in turns:
                for thread, lag, *step in steps:
                    i = ib = t - lag
                    name = step[0]
                    if thread == "A" and name == "xb":
                        pool.wait_ge(x_loaded, 16 * (i + 1))
                        if i == 0:
                            pool.wait_ge(ld_ob, 16)
                        else:
                            ra.wait_emptied(pool, i - 1, "op", 1)
                        for b in range(GB):
                            pool.tensor_tensor(xb[:, b, :], x_in[:, b, :], obias[:], ALU.add).then_inc(xb_made, 1)
                    elif thread == "A" and name == "q":
                        j = step[1]
                        part, slot = (qp[:, 0], j) if j < 2 else (kp[:, 2], j - 2)
                        pool.wait_ge(a_second, 4 * i + j + 1)
                        mid = (qp if j < 2 else kp)[:, 1, 2 * slot:2 * slot + 2, :]
                        pool.tensor_tensor(part[:, 2 * slot:2 * slot + 2, :], wide_a[:, j % 2].rearrange("p (m t) -> p m t", m=2),
                                           mid, ALU.subtract).then_inc(a_third, 1)
                    elif thread == "A" and name == "mt":
                        split_max(i, step[1], ra, nma, npa, nra, max_split_a, max_parts_a)
                    elif thread == "A" and name == "op":
                        rstd(GB * i + step[1], mva[:, step[1]], rsa[:, step[1]], ln_a, rstd_step_a, rstd_a)
                    elif thread == "B" and name == "xt":
                        u = step[1]
                        pool.wait_ge(b_second, GB * ib + u + 1)
                        own = slice(u * H, (u + 1) * H)
                        pool.tensor_tensor(xp[:, 0, own], wide_b[:, u], xp[:, 1, own], ALU.subtract).then_inc(b_third, 1)
                    elif thread == "B" and name == "ctx":
                        pool.wait_ge(c_second, ib + 1)
                        pool.tensor_tensor(cp[:, 2, :], rc[:], cp[:, 1, :], ALU.subtract).then_inc(c_third, 1)
                    elif thread == "A" and name == "cp":
                        pool.wait_ge(c_loaded, 16 * (i + 1))
                        if i == 0:
                            pool.wait_ge(ones_b, 1)
                        else:
                            rb.wait_full(pool, i - 1, "ctx")
                            pool.wait_ge(pv_b, GB * KVH * i)
                        for b in range(GB):
                            pool.tensor_copy(c_perm[:, b, :].rearrange("p (d g) -> p d g", d=HD), permuted(c_in[:, b, :])).then_inc(c_permuted, 1)
                            pool.tensor_copy(vx[:, b, :, 0:HD], c_in[:, b, :].rearrange("p (g d) -> p g d", d=HD)).then_inc(vx_made, 1)
                    elif thread == "B" and name == "mt":
                        split_max(ib, step[1], rb, nmb, npb, nrb, max_split_b, max_parts_b)
                    elif thread == "B" and name == "ot" and step[2] == 1:
                        rstd(2 * GB * ib + step[1], mvb[:, step[1]], rsb[:, step[1]], ln_b, rstd_step_b, rstd_b)
                    elif thread == "B" and step == ["cx", 1]:
                        rb.wait_full(pool, ib, "cx", 1)
                        if ib == 0:
                            pool.wait_ge(ld_fb, 16)
                        for b in range(GB):
                            pool.tensor_tensor(x2[:, b, :], x2[:, b, :], fbias[:], ALU.add).then_inc(x2_biased, 1)
                    elif thread == "B" and name == "is":
                        u = step[1]
                        pool.wait_ge(zh_made, 2 * ib + u + 1)
                        pool.tensor_tensor(zL[:, 2 * u:2 * u + 2, :], zf[:, 2 * u:2 * u + 2, :],
                                           zH[:, 2 * u:2 * u + 2, :].bitcast(F32), ALU.subtract).then_inc(zl_made, 1)
                    elif thread == "B" and name == "ff":
                        rstd(2 * GB * ib + GB + step[1], mvb[:, step[1]], rsb[:, step[1]], ln_b, rstd_step_b, rstd_b)
                    elif thread == "C" and name == "ow":
                        pool.wait_ge(ow_high, KT)
                        for kt in range(KT):
                            pool.tensor_tensor(owL[:, kt, :], oraw[:, kt, :], owH[:, kt, :].bitcast(F32), ALU.subtract).then_inc(ow_low, 1)

        @block.scalar
        def _(act):
            act.dma_start(x_in[:], x[0:GB].rearrange("b p f -> p b f")).then_inc(x_loaded, 16)

            for t, steps in turns:
                for thread, lag, *step in steps:
                    i = ib = t - lag
                    name = step[0]
                    if thread == "A" and name == "xt":
                        u = step[1]
                        ra.wait_full(act, i, *step)
                        act.activation(xH[:, 2 * u:2 * u + 2, :], pa_bank(*step)[:].rearrange("p (m t) -> p m t", m=2), ACT.Copy).then_inc(xh_made, 1)
                    elif thread == "A" and name == "q":
                        j = step[1]
                        dst, slot, stored = (qp[:, 2], j, q_stored) if j < 2 else (kp[:, 0], j - 2, k_stored)
                        ra.wait_full(act, i, *step)
                        if i == 0 and j == 0:
                            rb.wait_emptied(act, 0, "small")
                        if i > 0:
                            act.wait_ge(stored, 16 * i)
                        for m in range(2):
                            last = act.activation(dst[:, 2 * slot + m, :], pa_bank(*step)[:, m * TOK:(m + 1) * TOK], ACT.Identity,
                                                  bias=bqk[:, 2 * j + m:2 * j + m + 1])
                        last.then_inc(a_first, 1)
                    elif name == "st":
                        b, j = step[1:]
                        k, ring, bank, pr, pv, scale = ((i, ra, pa_bank, pa, pv_a, HD ** -0.5) if thread == "A"
                                                        else (ib, rb, pb_bank, pb, pv_b, 1.0))
                        n = (GB * k + b) * HT + j
                        ring.wait_full(act, k, *step)
                        if n >= NP:
                            act.wait_ge(pv, n - NP + 1)
                        if thread == "B" and n == 0:
                            act.wait_ge(scales, 2)
                        act.activation(pr[:, n % NP, :], bank(*step)[:], ACT.Exp, scale=scale).then_inc(*ring.is_empty(*step))
                    elif name == "pv" and step[2] % 4 == 3:
                        b, u = step[1], step[2] // 4
                        k, ring, bank, wide, pv = (i, ra, pa_bank, wide_a, pv_a) if thread == "A" else (ib, rb, pb_bank, wide_b, pv_b)
                        act.wait_ge(pv, (GB * k + b) * HT + 4 * u + 4)
                        act.activation(wide[:, u, :], bank("pv", b, u)[:], ACT.Copy).then_inc(*ring.is_empty("pv", b, u))
                    elif thread == "A" and name == "ct":
                        ra.wait_full(act, i, *step)
                        act.activation(cH[:], pa_bank(*step)[:].rearrange("p (k t) -> p k t", k=KT), ACT.Copy).then_inc(ch_made, 1)
                    elif thread == "B" and name == "xt":
                        u = step[1]
                        rb.wait_full(act, ib, *step)
                        if ib > 0:
                            act.wait_ge(x_stored, 16 * (GB * (ib - 1) + u + 1))
                        act.activation(xp[:, 2, u * H:(u + 1) * H], pb_bank(*step)[:], ACT.Copy,
                                       scale=HD ** -0.5).then_inc(b_first, 1)
                    elif thread == "B" and name == "ctx":
                        rb.wait_full(act, ib, *step)
                        if ib > 0:
                            act.wait_ge(c_stored, 16 * ib)
                        act.activation(cp[:, 0, :], pb_bank(*step)[:, 0:TOK], ACT.Copy).then_inc(c_first, 1)
                    elif thread == "B" and name == "cx":
                        u = step[1]
                        rb.wait_full(act, ib, *step)
                        act.activation(x2T[:, 2 * u:2 * u + 2, :], pb_bank(*step)[:].rearrange("p (m t) -> p m t", m=2), ACT.Copy).then_inc(*rb.is_empty(*step))
                    elif thread == "B" and name == "rl":
                        rb.wait_full(act, ib, *step)
                        act.activation(lg[:], pb_bank(*step)[0:E, 0:TOK], ACT.Copy).then_inc(*rb.is_empty(*step))
                    elif thread == "B" and name == "rt":
                        act.wait_ge(top_made, ib + 1)
                        for b in range(GB):
                            last = act.activation(el[:, b, :], pb_bank(*step)[:, b * E:(b + 1) * E], ACT.Exp, bias=nl[:, b:b + 1])
                        last.then_inc(*rb.is_empty(*step))
                    elif thread == "B" and name == "rr":
                        rb.wait_full(act, ib, *step)
                        act.activation(rT[:], pb_bank(*step)[0:4 * E, 0:TOK], ACT.Copy).then_inc(*rb.is_empty(*step))
                    elif thread == "B" and name == "is":
                        u = step[1]
                        rb.wait_emptied(act, ib, *step)
                        act.activation(zH[:, 2 * u:2 * u + 2, :], zf[:, 2 * u:2 * u + 2, :], ACT.Copy).then_inc(zh_made, 1)
                    elif thread == "B" and name == "os":
                        rb.wait_full(act, ib, *step)
                        if GB * ib + step[1] > 0:
                            kb, bb = (ib, 0) if step[1] else (ib - 1, 1)
                            rb.wait_emptied(act, kb, "ff", bb)
                        act.activation(osb[:], pb_bank(*step)[:], ACT.Copy).then_inc(*rb.is_empty(*step))
                    elif thread == "C" and name == "w":
                        blk = step[1]
                        act.wait_ge(ld_w[blk], 16)
                        for kt in range(KT):
                            act.activation(*w_views(wH, wraw, kt, blk), ACT.Copy).then_inc(w_high, 1)
                    elif thread == "C" and name == "ow":
                        act.wait_ge(ld_ow, 16)
                        for kt in range(KT):
                            act.activation(owH[:, kt, :], oraw[:, kt, :], ACT.Copy).then_inc(ow_high, 1)
                    elif thread == "C" and name == "sign":
                        act.wait_ge(ld_fw, 16)
                        for k in range(KT):
                            act.activation(sgn[:, k, :], fraw[:, k, :], ACT.Sign).then_inc(signs, 1)

        @block.vector
        def _(dve):
            def deviations(n, v, b):
                dve.wait_ge(ln_b, 3 * n + 1)
                dve.bn_stats(stb[:], v).then_inc(ln_b, 1)
                dve.wait_ge(ln_b, 3 * n + 2)
                dve.bn_aggr(mvb[:, b], stb[:]).then_inc(ln_b, 1)

            def normalise(n, v, b, done):
                dve.wait_ge(rstd_b, n + 1)
                dve.tensor_scalar(v, v, mvb[:, b, 0:1], rsb[:, b, 1:2], ALU.subtract, ALU.mult).then_inc(done, 1)

            for t, steps in turns:
                for thread, lag, *step in steps:
                    i = ib = t - lag
                    name = step[0]
                    if thread == "A" and name == "xt":
                        u = step[1]
                        dve.wait_ge(xh_made, 2 * i + u + 1)
                        dve.tensor_tensor(xL[:, 2 * u:2 * u + 2, :], pa_bank(*step)[:].rearrange("p (m t) -> p m t", m=2),
                                          xH[:, 2 * u:2 * u + 2, :].bitcast(F32), ALU.subtract).then_inc(*ra.is_empty(*step))
                    elif thread == "A" and name == "q":
                        j = step[1]
                        parts, slot, hi = (qp, j, 2) if j < 2 else (kp, j - 2, 0)
                        dve.wait_ge(a_first, 4 * i + j + 1)
                        if 4 * i + j >= 2:
                            dve.wait_ge(a_third, 4 * i + j - 1)
                        for m in range(2):
                            last = dve.scalar_tensor_tensor(wide_a[:, j % 2, m * TOK:(m + 1) * TOK], pa_bank(*step)[:, m * TOK:(m + 1) * TOK],
                                                            bqk[:, 2 * j + m:2 * j + m + 1], parts[:, hi, 2 * slot + m, :], ALU.add, ALU.subtract)
                        last.then_inc(*ra.is_empty(*step))
                        ra.wait_emptied(dve, i, *step)
                        dve.tensor_copy(parts[:, 1, 2 * slot:2 * slot + 2, :], wide_a[:, j % 2].rearrange("p (m t) -> p m t", m=2)).then_inc(a_second, 1)
                    elif thread == "A" and name == "v":
                        b = step[1]
                        ra.wait_full(dve, i, *step)
                        if i == 0 and b == 0:
                            dve.wait_ge(ld_vb, 16)
                            dve.wait_ge(ones_a, 1)
                        dve.tensor_tensor(va[:, b].rearrange("p (h m) w -> p m h w", m=KT)[:, :, :, 0:HD],
                                          pa_bank(*step)[:].rearrange("p (m h d) -> p m h d", m=KT, d=HD),
                                          vbias[:].rearrange("p (m h d) -> p m h d", m=KT, d=HD), ALU.add).then_inc(*ra.is_empty(*step))
                    elif thread == "A" and name == "s":
                        b, j = step[1:]
                        ra.wait_full(dve, i, *step)
                        dve.tensor_reduce(nma[:, b, 4 * j:4 * j + 4], pa_bank(*step)[:].rearrange("p (m t) -> p m t", m=KT), AX.X, ALU.max,
                                          negate=True).then_inc(*ra.is_empty(*step))
                    elif name == "mt":
                        b = step[1]
                        k, ring, bank, mr = (i, ra, pa_bank, mra) if thread == "A" else (ib, rb, pb_bank, mrb)
                        ring.wait_full(dve, k, *step)
                        dve.tensor_copy(mr[:, b, :], bank(*step)[0:NPART * HEADS, 0:P // 2].bitcast(BF16)).then_inc(*ring.is_empty(*step))
                    elif thread == "A" and name == "ot":
                        b, u = step[1:]
                        ra.wait_full(dve, i, *step)
                        v = pa_bank(*step)[:].rearrange("p (s c w) -> p s c w", s=4, w=VW)
                        rd = rda[:, 16 * u:16 * u + 16].rearrange("p (s c o) -> p s c o", s=4, o=1)
                        dve.reciprocal(rd, v[:, :, :, HD:HD + 1]).then_inc(recip_a, 1)
                        dve.wait_ge(recip_a, 2 * (GB * i + b) + u + 1)
                        dve.tensor_tensor(cx[:].rearrange("p (c u s d) -> p u s c d", c=KT, u=2, d=HD)[:, u], v[:, :, :, 0:HD],
                                          rd.broadcast_to([P, 4, 4, HD]), ALU.mult).then_inc(*ra.is_empty(*step))
                    elif thread == "A" and name == "ct":
                        dve.wait_ge(ch_made, GB * i + step[1] + 1)
                        dve.tensor_tensor(cL[:], pa_bank(*step)[:].rearrange("p (k t) -> p k t", k=KT), cH[:].bitcast(F32),
                                          ALU.subtract).then_inc(*ra.is_empty(*step))
                    elif thread == "A" and name == "op":
                        b = step[1]
                        n = GB * i + b
                        ra.wait_full(dve, i, *step)
                        dve.wait_ge(xb_made, n + 1)
                        dve.tensor_tensor(tile_permuted(x1[:, b, :]), by_head(pa_bank(*step)[:]), by_head(xb[:, b, :]), ALU.add).then_inc(*ra.is_empty(*step))
                        ra.wait_emptied(dve, i, *step)
                        dve.bn_stats(sta[:], x1[:, b, :]).then_inc(ln_a, 1)
                        dve.wait_ge(ln_a, 3 * n + 1)
                        dve.bn_aggr(mva[:, b], sta[:]).then_inc(ln_a, 2)
                    elif thread == "A" and name == "n1":
                        b = step[1]
                        dve.wait_ge(rstd_a, GB * i + b + 1)
                        dve.tensor_scalar(x1[:, b, :], x1[:, b, :], mva[:, b, 0:1], rsa[:, b, 1:2], ALU.subtract, ALU.mult).then_inc(x1_made, 1)
                    elif thread == "B" and name == "xt":
                        u = step[1]
                        dve.wait_ge(b_first, 2 * ib + u + 1)
                        dve.scalar_tensor_tensor(wide_b[:, u], pb_bank(*step)[:], HD ** -0.5, xp[:, 2, u * H:(u + 1) * H],
                                                 ALU.mult, ALU.subtract).then_inc(*rb.is_empty(*step))
                        rb.wait_emptied(dve, ib, *step)
                        dve.tensor_copy(xp[:, 1, u * H:(u + 1) * H], wide_b[:, u]).then_inc(b_second, 1)
                    elif thread == "B" and name == "ctx":
                        dve.wait_ge(c_first, ib + 1)
                        dve.tensor_tensor(rc[:], pb_bank(*step)[:, 0:TOK], cp[:, 0, :], ALU.subtract).then_inc(*rb.is_empty(*step))
                        rb.wait_emptied(dve, ib, *step)
                        dve.tensor_copy(cp[:, 1, :], rc[:]).then_inc(c_second, 1)
                    elif thread == "B" and name == "s":
                        b, g = step[1:]
                        rb.wait_full(dve, ib, *step)
                        if g >= 2:
                            rb.wait_emptied(dve, ib, "s", b, g - 2)
                        elif b == 1:
                            rb.wait_emptied(dve, ib, "s", 0, g + 6)
                        elif g == 0:
                            dve.wait_ge(b_third, GB * (ib + 1))
                        for r in range(4):
                            col = (4 * (g % 2) + r) * KT + g // 2
                            last = dve.tensor_tensor_reduce(wide_b[:, g % 2, r * P:(r + 1) * P], pb_bank(*step)[:, r * P:(r + 1) * P], mraw[:], -1.0, -LOWEST,
                                                            ALU.add, ALU.min, nmb[:, b, col:col + 1])
                        last.then_inc(*rb.is_empty(*step))
                    elif thread == "B" and name == "ot":
                        b, u = step[1:]
                        n = 2 * GB * ib + b
                        rb.wait_full(dve, ib, *step)
                        v = pb_bank(*step)[:].rearrange("p (r c w) -> p r c w", r=4, w=VW)
                        rd = rdb[:, 16 * u:16 * u + 16].rearrange("p (r c o) -> p r c o", r=4, o=1)
                        dve.reciprocal(rd, v[:, :, :, HD:HD + 1]).then_inc(recip_b, 1)
                        dve.wait_ge(recip_b, 2 * (GB * ib + b) + u + 1)
                        if ib > 0 and u == 0:
                            dve.wait_ge(out_stored, 16 * (GB * (ib - 1) + b + 1))
                        dve.tensor_tensor(x2[:, b, :].rearrange("p (u c r d) -> p u r c d", u=2, c=4, d=HD)[:, u], v[:, :, :, 0:HD],
                                          rd.broadcast_to([P, 4, 4, HD]), ALU.mult).then_inc(*rb.is_empty(*step))
                        if u == 1:
                            rb.wait_emptied(dve, ib, "ot", b, 0)
                            rb.wait_emptied(dve, ib, "ot", b, 1)
                            dve.tensor_tensor(by_head(x2[:, b, :]), by_head(x2[:, b, :]), tile_permuted(x1[:, b, :]), ALU.add).then_inc(ln_b, 1)
                            deviations(n, x2[:, b, :], b)
                    elif thread == "B" and name == "n2":
                        normalise(2 * GB * ib + step[1], x2[:, step[1], :], step[1], x2_made)
                    elif thread == "B" and name == "rt":
                        rb.wait_full(dve, ib, *step)
                        dve.tensor_reduce(nl[:], pb_bank(*step)[:, 0:GB * E].rearrange("p (b e) -> p b e", e=E), AX.X, ALU.max,
                                          negate=True).then_inc(top_made, 1)
                    elif thread == "B" and name == "rr":
                        rb.wait_emptied(dve, ib, "rt")
                        dve.tensor_reduce(sl[:], el[:], AX.X, ALU.add).then_inc(route_step, 1)
                        dve.wait_ge(route_step, 5 * ib + 1)
                        dve.reciprocal(rl[:], sl[:]).then_inc(route_step, 1)
                        dve.wait_ge(route_step, 5 * ib + 2)
                        dve.tensor_tensor(rt[:], el[:], rl[:].rearrange("p (b o) -> p b o", o=1).broadcast_to([P, GB, E]), ALU.mult).then_inc(route_step, 1)
                        dve.wait_ge(route_step, 5 * ib + 3)
                        dve.tensor_copy(rtH[:], rt[:]).then_inc(route_step, 1)
                        dve.wait_ge(route_step, 5 * ib + 4)
                        for k in (0, 2):
                            last = dve.tensor_copy(rts[:, :, k, :], rtH[:].bitcast(F32))
                            last = dve.tensor_tensor(rts[:, :, k + 1, :], rt[:], rtH[:].bitcast(F32), ALU.subtract)
                            last.then_inc(route_step if k == 0 else route_made, 1)
                    elif thread == "B" and name == "is":
                        u = step[1]
                        rb.wait_full(dve, ib, *step)
                        rb.wait_emptied(dve, ib, "cx", u)
                        dve.tensor_tensor(zf[:, 2 * u:2 * u + 2, :], pb_bank(*step)[:].rearrange("p (m t) -> p m t", m=2),
                                          x2T[:, 2 * u:2 * u + 2, :], ALU.mult).then_inc(*rb.is_empty(*step))
                    elif thread == "B" and name == "ff":
                        b = step[1]
                        n = 2 * GB * ib + GB + b
                        rb.wait_full(dve, ib, *step)
                        rb.wait_emptied(dve, ib, "os", b)
                        dve.tensor_tensor(wide_b[:, b], pb_bank(*step)[:], osb[:], ALU.mult).then_inc(*rb.is_empty(*step))
                        rb.wait_emptied(dve, ib, *step)
                        dve.wait_ge(x2_biased, GB * ib + b + 1)
                        dve.tensor_tensor(x2[:, b, :], wide_b[:, b], x2[:, b, :], ALU.add).then_inc(ln_b, 1)
                        deviations(n, x2[:, b, :], b)
                    elif thread == "B" and name == "n3":
                        normalise(2 * GB * ib + GB + step[1], x2[:, step[1], :], step[1], y_made)
                    elif thread == "C" and name == "w":
                        blk = step[1]
                        for kt in range(KT):
                            dve.wait_ge(w_high, KT * blk + kt + 1)
                            low, raw = w_views(wL, wraw, kt, blk)
                            high = wH[:, kt, blk * H:(blk + 1) * H].bitcast(F32)
                            if blk < 2:
                                high = high.rearrange("p (m d h) -> p m d h", m=KT, d=HD)
                            dve.tensor_tensor(low, raw, high, ALU.subtract).then_inc(w_low, 1)
                    elif thread == "C" and name == "small":
                        dve.wait_ge(ld_small, 32)
                        dve.tensor_copy(bperm[:].rearrange("p (d h) -> p d h", d=HD), permuted(braw[:])).then_inc(bias_permuted, 1)
                        rb.wait_full(dve, 0, "small")
                        dve.tensor_copy(bqk[:], pb_bank("small")[:, 0:2 * KT])
                        dve.tensor_copy(gT[:], pb_bank("small")[:, P:P + KT * E].rearrange("p (k e) -> p k e", e=E)).then_inc(*rb.is_empty("small"))
                    elif thread == "C" and name == "mask":
                        dve.wait_ge(ld_mask, 16)
                        dve.tensor_copy(mH[:], mraw[:]).then_inc(masks, 1)
                        dve.wait_ge(masks, 1)
                        dve.tensor_tensor(mL[:], mraw[:], mH[:].bitcast(F32), ALU.subtract).then_inc(masks, 1)
                        dve.wait_ge(idents, 1)
                        for r in range(4):
                            last = dve.tensor_copy(idr[:, r, :], idf[:])
                        last.then_inc(masks, 1)
                    elif thread == "C" and name == "swt":
                        rb.wait_full(dve, 0, *step)
                        dve.tensor_copy(swT[:, step[1], :], pb_bank(*step)[:, 0:H // 2].bitcast(BF16)).then_inc(*rb.is_empty(*step))
                    elif thread == "C" and name == "scales":
                        dve.wait_ge(ld_cs, 16 * 8)
                        dve.wait_ge(picks, 5)
                        for k, (raw, dst) in enumerate(((icr, icS), (ocr, ocS))):
                            dve.tensor_copy(cshi[:], raw[:]).then_inc(scale_step, 1)
                            dve.wait_ge(scale_step, 3 * k + 1)
                            dve.tensor_tensor(cslo[:], raw[:], cshi[:].bitcast(F32), ALU.subtract).then_inc(scale_step, 1)
                            dve.wait_ge(scale_step, 3 * k + 2)
                            dve.tensor_scalar(cslo[:], cslo[:], pick[:, 1:2], None, ALU.mult).then_inc(scale_step, 1)
                            dve.wait_ge(scale_step, 3 * k + 3)
                            dve.scalar_tensor_tensor(dst[:], cshi[:].bitcast(F32), pick[:, 0:1], cslo[:], ALU.mult, ALU.add).then_inc(scales, 1)
                            dve.wait_ge(scales, k + 1)

        @block.tensor
        def _(pe):
            def three(dst, left, right, start=True):
                (lh, ll), (rh, rl_) = left, right
                pe.matmul(dst, lh, rh, start=start, stop=False)
                pe.matmul(dst, lh, rl_, start=False, stop=False)
                return pe.matmul(dst, ll, rh, start=False, stop=False)

            def project(dst, lefts, rights):
                for kt in range(KT):
                    (lh, ll), (rh, rl_) = lefts(kt), rights(kt)
                    pe.matmul(dst, lh, rh, start=kt == 0, stop=False)
                    pe.matmul(dst, lh, rl_, start=False, stop=False)
                    last = pe.matmul(dst, ll, rh, start=False, stop=kt == KT - 1)
                return last

            for t, steps in turns:
                for thread, lag, *step in steps:
                    i = ib = t - lag
                    name = step[0]
                    if thread == "A" and name not in NOT_IN_RING + ("pv",):
                        ra.wait_free(pe, i, *step)
                        dst = pa_bank(*step)
                    elif thread == "B" and name not in NOT_IN_RING + ("pv",):
                        rb.wait_free(pe, ib, *step)
                        dst = pb_bank(*step)
                    if thread == "A" and name == "xt":
                        u = step[1]
                        pe.wait_ge(x_loaded, 16 * (i + 1))
                        if i == 0 and u == 0:
                            pe.wait_ge(idents, 1)
                        for m in range(2):
                            for b in range(GB):
                                kt = 2 * u + m
                                last = pe.transpose(dst[:, m * TOK + b * P:m * TOK + (b + 1) * P], x_in[:, b, kt * P:(kt + 1) * P], idf[:])
                        last.then_inc(*ra.is_full(*step))
                    elif thread == "A" and name == "q":
                        j = step[1]
                        if j == 0:
                            ra.wait_emptied(pe, i, "xt", 0)
                            ra.wait_emptied(pe, i, "xt", 1)
                        if i == 0 and j % 2 == 0:
                            pe.wait_ge(w_low, KT * (j // 2 + 1))
                        for m in range(2):
                            col = (2 * j + m) * P
                            last = project(dst[:, m * TOK:(m + 1) * TOK],
                                           lambda kt: (wH[:, kt, col:col + P], wL[:, kt, col:col + P]),
                                           lambda kt: (xH[:, kt, :], xL[:, kt, :]))
                        last.then_inc(*ra.is_full(*step))
                    elif thread == "A" and name == "v":
                        b = step[1]
                        if i == 0 and b == 0:
                            pe.wait_ge(w_low, 3 * KT)
                        project(dst[:], lambda kt: (xH[:, kt, tokens(b)], xL[:, kt, tokens(b)]),
                                lambda kt: (wH[:, kt, 2 * H:3 * H], wL[:, kt, 2 * H:3 * H])).then_inc(*ra.is_full(*step))
                    elif thread == "A" and name == "s":
                        b, j = step[1:]
                        if b == 0 and j == 0:
                            pe.wait_ge(q_stacked, 48 * (i + 1))
                            pe.wait_ge(k_stacked, 48 * (i + 1))
                        for m in range(KT):
                            last = pe.matmul(dst[:, m * P:(m + 1) * P], qs[0:SR, j, m, tokens(b)], ks[0:SR, j, m, tokens(b)], start=True, stop=True)
                        last.then_inc(*ra.is_full(*step))
                    elif name == "mt":
                        b = step[1]
                        k, ring, parts, done = (i, ra, npa, max_parts_a) if thread == "A" else (ib, rb, npb, max_parts_b)
                        if i == 0:
                            pe.wait_ge(idents, 2)
                        pe.wait_ge(done, GB * k + b + 1)
                        pe.transpose(dst[0:NPART * HEADS, 0:P // 2].bitcast(BF16), parts[:, b].rearrange("p c h -> p (c h)"), idb[:]).then_inc(*ring.is_full(*step))
                    elif thread == "A" and name == "st":
                        b, j = step[1:]
                        if j == 0:
                            pe.wait_ge(max_stacked_a[b], 48 * (i + 1))
                            if i == 0:
                                pe.wait_ge(rows_a, 16)
                        for m in range(KT):
                            last = pe.matmul(dst[:, m * P:(m + 1) * P], ks[0:SM, j, m, tokens(b)], qs[0:SM, j, m, tokens(b)], start=True, stop=True)
                        last.then_inc(*ra.is_full(*step))
                    elif thread == "A" and name == "pv":
                        b, j = step[1:]
                        n = (GB * i + b) * HT + j
                        if j % 4 == 0:
                            ra.wait_free(pe, i, "pv", b, j // 4)
                        dst = pa_bank("pv", b, j // 4)
                        ra.wait_emptied(pe, i, "st", b, j)
                        if j == 0:
                            ra.wait_emptied(pe, i, "v", b)
                        for m in range(KT):
                            last = pe.matmul(dst[m * VW:(m + 1) * VW, (j % 4) * P:(j % 4 + 1) * P], va[:, b, j * KT + m, :],
                                             pa[:, n % NP, m * P:(m + 1) * P], start=True, stop=True)
                        last.then_inc(pv_a, 1)
                    elif name == "ot":
                        b, u = step[1:]
                        k, ring, wide = (i, ra, wide_a) if thread == "A" else (ib, rb, wide_b)
                        ring.wait_emptied(pe, k, "pv", b, u)
                        for s in range(4):
                            last = pe.transpose(dst[:, s * P:(s + 1) * P], wide[:, u, s * P:(s + 1) * P], idf[:])
                        last.then_inc(*ring.is_full(*step))
                    elif thread == "A" and name == "ct":
                        b = step[1]
                        ra.wait_emptied(pe, i, "ot", b, 0)
                        ra.wait_emptied(pe, i, "ot", b, 1)
                        for kt in range(KT):
                            last = pe.transpose(dst[:, kt * P:(kt + 1) * P], cx[:, kt * P:(kt + 1) * P], idf[:])
                        last.then_inc(*ra.is_full(*step))
                    elif thread == "A" and name == "op":
                        b = step[1]
                        ra.wait_emptied(pe, i, "ct", b)
                        if i == 0 and b == 0:
                            pe.wait_ge(ow_low, KT)
                        project(dst[:], lambda kt: (cH[:, kt, :], cL[:, kt, :]),
                                lambda kt: (owH[:, kt, :], owL[:, kt, :])).then_inc(*ra.is_full(*step))
                    elif thread == "B" and name == "xt":
                        b = step[1]
                        pe.wait_ge(x1_made, GB * ib + b + 1)
                        for kt in range(KT):
                            last = pe.transpose(dst[:, kt * P:(kt + 1) * P], x1[:, b, kt * P:(kt + 1) * P], idf[:])
                        last.then_inc(*rb.is_full(*step))
                    elif thread == "B" and name == "ctx":
                        pe.wait_ge(c_permuted, GB * (ib + 1))
                        for b in range(GB):
                            last = pe.transpose(dst[:, tokens(b)], c_perm[:, b, :], idf[:])
                        last.then_inc(*rb.is_full(*step))
                    elif thread == "B" and name == "s":
                        b, g = step[1:]
                        if g == 0:
                            pe.wait_ge(x_stacked[b], 48 * (ib + 1))
                        if b == 0 and g == 0:
                            pe.wait_ge(c_stacked, 48 * (ib + 1))
                        for r in range(4):
                            last = pe.matmul(dst[:, r * P:(r + 1) * P], qx[0:SR, b, 4 * (g % 2) + r, g // 2, :], kx[0:SR, g, tokens(b)],
                                             start=True, stop=True)
                        last.then_inc(*rb.is_full(*step))
                    elif thread == "B" and name == "st":
                        b, g = step[1:]
                        if g == 0:
                            pe.wait_ge(max_stacked_b[b], 48 * (ib + 1))
                            if ib == 0:
                                pe.wait_ge(rows_b, 16)
                                pe.wait_ge(masks, 3)
                        d4 = dst[:].rearrange("p (r t) -> p r t", r=4)
                        pe.matmul(d4, mH[:], idr[:], start=True, stop=False)
                        pe.matmul(d4, mL[:], idr[:], start=False, stop=False)
                        a = 4 * (g % 2)
                        pe.matmul(d4, kx[0:SM, g, tokens(b)], qx[0:SM, b, a:a + 4, g // 2, :], start=False, stop=True).then_inc(*rb.is_full(*step))
                    elif thread == "B" and name == "pv":
                        b, g = step[1:]
                        n = (GB * ib + b) * KVH + g
                        if g % 4 == 0:
                            rb.wait_free(pe, ib, "pv", b, g // 4)
                        dst = pb_bank("pv", b, g // 4)
                        rb.wait_emptied(pe, ib, "st", b, g)
                        if g == 0:
                            pe.wait_ge(vx_made, GB * ib + b + 1)
                        c = g % 4
                        pe.matmul(dst[c * VW:(c + 1) * VW, :], vx[:, b, g, :], pb[:, n % NP, :], start=True, stop=True).then_inc(pv_b, 1)
                    elif thread == "B" and name == "cx":
                        u = step[1]
                        pe.wait_ge(x2_made, GB * (ib + 1))
                        for m in range(2):
                            for b in range(GB):
                                kt = 2 * u + m
                                last = pe.transpose(dst[:, m * TOK + b * P:m * TOK + (b + 1) * P], x2[:, b, kt * P:(kt + 1) * P], idf[:])
                        last.then_inc(*rb.is_full(*step))
                    elif thread == "B" and name == "rl":
                        rb.wait_emptied(pe, ib, "cx", 0)
                        rb.wait_emptied(pe, ib, "cx", 1)
                        for kt in range(KT):
                            last = pe.matmul(dst[0:E, 0:TOK], gT[:, kt, :], x2T[:, kt, :], start=kt == 0, stop=kt == KT - 1)
                        last.then_inc(*rb.is_full(*step))
                    elif thread == "B" and name == "rt":
                        rb.wait_emptied(pe, ib, "rl")
                        for b in range(GB):
                            last = pe.transpose(dst[:, b * E:(b + 1) * E], lg[:, tokens(b)], idf[0:E, 0:E])
                        last.then_inc(*rb.is_full(*step))
                    elif thread == "B" and name == "rr":
                        pe.wait_ge(route_made, ib + 1)
                        for b in range(GB):
                            last = pe.transpose(dst[0:4 * E, tokens(b)], rts[:, b].rearrange("p k e -> p (k e)"), idf[:])
                        last.then_inc(*rb.is_full(*step))
                    elif thread == "B" and name == "is":
                        u = step[1]
                        rb.wait_emptied(pe, ib, "rr")
                        for m in range(2):
                            kt = 2 * u + m
                            last = pe.matmul(dst[:, m * TOK:(m + 1) * TOK], icS[:, kt * P:(kt + 1) * P], rT[:], start=True, stop=True)
                        last.then_inc(*rb.is_full(*step))
                    elif thread == "B" and name == "os":
                        pe.matmul(dst[:], rT[:, tokens(step[1])], ocS[:], start=True, stop=True).then_inc(*rb.is_full(*step))
                    elif thread == "B" and name == "ff":
                        b = step[1]
                        pe.wait_ge(zh_made, 2 * (ib + 1))
                        pe.wait_ge(zl_made, 2 * (ib + 1))
                        for kt in range(KT):
                            pe.matmul(dst[:], zH[:, kt, tokens(b)], swT[:, kt, :], start=kt == 0, stop=False)
                            last = pe.matmul(dst[:], zL[:, kt, tokens(b)], swT[:, kt, :], start=False, stop=kt == KT - 1)
                        last.then_inc(*rb.is_full(*step))
                    elif thread == "C" and name == "small":
                        pe.wait_ge(idents, 1)
                        pe.wait_ge(ld_small, 32)
                        pe.wait_ge(bias_permuted, 1)
                        dst = pb_bank("small")
                        pe.transpose(dst[:, 0:2 * KT], bperm[:], idf[0:2 * KT, 0:2 * KT])
                        for kt in range(KT):
                            last = pe.transpose(dst[:, P + kt * E:P + (kt + 1) * E], graw[:, kt * P:(kt + 1) * P], idf[0:E, 0:E])
                        last.then_inc(*rb.is_full("small"))
                    elif thread == "C" and name == "swt":
                        kt = step[1]
                        rb.wait_free(pe, 0, *step)
                        if kt == 0:
                            pe.wait_ge(signs, KT)
                            pe.wait_ge(idents, 2)
                        dst = pb_bank(*step)[:, 0:H // 2].bitcast(BF16)
                        for o in range(KT):
                            last = pe.transpose(dst[:, o * P:(o + 1) * P], sgn[:, o, kt * P:(kt + 1) * P], idb[:])
                        last.then_inc(*rb.is_full(*step))


_INS = ["x", "ctx_1024", "mask_SxS2_ff0", "L0_attn_attn_qkvw", "L0_attn_attn_qkvb", "L0_attn_attn_ow", "L0_attn_attn_ob",
        "L0_ffn_weight", "L0_ffn_bias", "L0_ffn_gate_w", "L0_ffn_in_channel_scale", "L0_ffn_out_channel_scale"]


def kernel(**inputs):
    import numpy as _np
    import concourse.bacc as _bacc
    from concourse import mybir as _mybir
    from concourse.bass_utils import run_bass_kernel_spmd as _run

    nc = _bacc.Bacc("TRN2", target_bir_lowering=False, num_devices=1, dynamic_dma_scratch_size=1024)
    arrays, args = {}, []
    for name in _INS:
        a = _np.ascontiguousarray(inputs[name])
        arrays[f"in_{name}_dram"] = a
        args.append(nc.dram_tensor(f"in_{name}_dram", a.shape, _mybir.dt.from_np(a.dtype), kind="ExternalInput").ap())
    args.append(nc.dram_tensor("out_0_dram", (B, P, H), F32, kind="ExternalOutput").ap())
    for name, heads, cols in (("scr_q", HT, KT * TOK), ("scr_k", HT, KT * TOK), ("scr_x", HT, KT * TOK), ("scr_c", KVH, TOK)):
        args.append(nc.dram_tensor(name, (NG, NPART * HD, heads, cols), BF16, kind="Internal").ap())
    decoder_layer(nc, *args)
    r = _run(nc, [arrays], core_ids=[0])
    return r.results[0]["out_0_dram"]
```

```python
from contextlib import ExitStack

import concourse.bass as bass
from concourse import mybir

F32 = mybir.dt.float32
F32R = mybir.dt.float32r
BF16 = mybir.dt.bfloat16
ALU = mybir.AluOpType
ACT = mybir.ActivationFunctionType
AX = mybir.AxisListType

P = 128
B = 8
GB = 2
NG = B // GB
TOK = GB * P
H = 512
KT = H // P
HEADS = 32
HD = H // HEADS
KVH = 8
HT = P // HD
E = 8
NPART = 3
SR = 6 * HD
SM = SR + NPART
VW = 32
NP = 2
CONSTANTS = [("C", 0, "small")] + [("C", 0, "swt", k) for k in range(KT)]
EPS = 1e-5
LOWEST = -3.0e38
QBLK = 3 * H


def steps(table):
    out = []
    for token in table.split():
        name, _, index = token[2:].partition(":")
        out.append((token[0], int(token[1] == "'"), name, *(int(k) for k in index.split(",") if k)))
    return out


FIRST = steps("""
    C.w:0 A.xt:0 C.small A.xt:1 C.w:1 A.q:0 C.mask A.q:1 C.ow C.w:2 A.q:2 A.ldq A.q:3 A.v:1 A.lc A.v:0 C.swt:3 A.s:0,0
    A.s:0,1 C.swt:0 A.ldk A.s:0,2 A.s:0,3 A.s:0,4 A.s:0,5 A.s:0,6 A.s:0,7 A.s:1,0 A.s:1,1 A.s:1,2 A.s:1,3 A.s:1,4
    A.mt:0 A.s:1,5 A.s:1,6 A.s:1,7 C.swt:1 C.sign C.scales A.st:0,0 C.swt:2 A.st:0,1 A.st:0,2 C.rows A.pv:0,0 A.st:0,3
    A.pv:0,1 A.st:0,4 A.mt:1 A.pv:0,2 A.st:0,5 A.pv:0,3 A.st:0,6 A.pv:0,4 A.xb A.st:0,7 A.pv:0,5 A.st:1,0 A.pv:0,6
    A.st:1,1 A.pv:0,7 A.ot:0,0 A.st:1,2 A.ot:0,1 A.pv:1,0 A.st:1,3 A.pv:1,1 A.ct:0 A.st:1,4 A.pv:1,2 A.st:1,5 A.pv:1,3
    A.op:0 A.n1:0 A.st:1,6 A.pv:1,4 B.cp:0 A.st:1,7 A.pv:1,5 A.pv:1,6 A.pv:1,7 B.cp:1
""")

MIDDLE = steps("""
    A'ot:1,0 A.xt:0 A.xt:1 A'ot:1,1 B'ctx:0 B'ldc:0 B'ctx:1 B'xt:0 A'ct:1 A.q:0 A'op:1 A'n1:1 B'ldc:1 B'ldx:0 A.lc
    A.q:1 B'xt:1 A.q:2 A.ldq B'ldx:1 B's:0,0 B's:0,1 B's:0,2 A.q:3 B's:0,3 B's:0,4 B's:0,5 B's:0,6 B's:0,7 A.ldk A.v:0
    B's:1,0 B's:1,1 B's:1,2 B'mt:0 B's:1,3 B's:1,4 B's:1,5 A.v:1 B's:1,6 B'st:0,0 B's:1,7 B'st:0,1 A.s:0,0 B'st:0,2
    A.s:0,1 A.s:0,2 A.s:0,3 B'mt:1 A.s:0,4 B'pv:0,0 A.xb B'st:0,3 B'pv:0,1 A.s:0,5 B'st:0,4 B'pv:0,2 B'st:0,5 B'pv:0,3
    A.s:0,6 B'st:0,6 A.s:0,7 A.s:1,0 B'pv:0,4 A.s:1,1 B'st:0,7 A.s:1,2 B'pv:0,5 A.s:1,3 B'st:1,0 B'pv:0,6 A.s:1,4
    A.s:1,5 B'st:1,1 B'pv:0,7 A.mt:0 B'st:1,2 A.s:1,6 B'pv:1,0 B'ot:0,0 B'st:1,3 B'pv:1,1 B'ot:0,1 B'st:1,4 B'pv:1,2
    B'st:1,5 A.s:1,7 B'pv:1,3 B'st:1,6 B'n2:0 B'pv:1,4 A.st:0,0 B'st:1,7 B'pv:1,5 B'pv:1,6 B'pv:1,7 A.mt:1 B'ot:1,0
    B'ot:1,1 A.st:0,1 A.st:0,2 B'n2:1 A.pv:0,0 A.st:0,3 B'cx:0 A.pv:0,1 A.st:0,4 A.pv:0,2 A.st:0,5 A.pv:0,3 B'cx:1
    A.st:0,6 A.pv:0,4 B'rl:1 B'rl:0 A.st:0,7 A.pv:0,5 B'rt:0 A.st:1,0 B'rt:1 A.pv:0,6 A.st:1,1 A.pv:0,7 B'rr:0
    A.st:1,2 A.pv:1,0 A.ot:0,0 A.ot:0,1 A.st:1,3 A.pv:1,1 A.st:1,4 A.pv:1,2 B'rr:1 A.ct:0 B.cp:0 A.st:1,5 A.pv:1,3
    B'is:1 B'is:0 A.st:1,6 A.op:0 B'os:0 A.pv:1,4 A.n1:0 B'os:1 B'ff:0 A.st:1,7 A.pv:1,5 B'ff:1 A.pv:1,6 A.pv:1,7
    B'n3:0 B.cp:1 B'n3:1
""")

LAST = steps("""
    A'ot:1,0 A'ot:1,1 B'ctx:0 B'xt:0 A'ct:1 B'ldx:0 A'op:1 A'n1:1 B'ldc:0 B'ctx:1 B'xt:1 B's:0,0 B'ldx:1 B's:0,1
    B's:0,2 B'ldc:1 B's:0,3 B's:0,4 B's:0,5 B's:0,6 B's:0,7 B's:1,0 B'mt:0 B's:1,1 B's:1,2 B's:1,3 B's:1,4 B's:1,5
    B's:1,6 B's:1,7 B'st:0,0 B'st:0,1 B'st:0,2 B'pv:0,0 B'st:0,3 B'pv:0,1 B'st:0,4 B'mt:1 B'pv:0,2 B'st:0,5 B'pv:0,3
    B'st:0,6 B'pv:0,4 B'st:0,7 B'pv:0,5 B'st:1,0 B'pv:0,6 B'st:1,1 B'ot:0,0 B'pv:0,7 B'st:1,2 B'pv:1,0 B'st:1,3
    B'pv:1,1 B'ot:0,1 B'st:1,4 B'pv:1,2 B'n2:0 B'st:1,5 B'pv:1,3 B'st:1,6 B'pv:1,4 B'ot:1,0 B'st:1,7 B'pv:1,5 B'pv:1,6
    B'pv:1,7 B'ot:1,1 B'cx:0 B'rl:0 B'rt:0 B'cx:1 B'n2:1 B'rr:0 B'rl:1 B'rt:1 B'is:0 B'os:0 B'rr:1 B'is:1 B'ff:0
    B'os:1 B'ff:1 B'n3:0 B'n3:1
""")

TURNS = [(0, FIRST)] + [(t, MIDDLE) for t in range(1, NG)] + [(NG, LAST)]
NO_BANK = ("xb", "lc", "cp", "ldq", "ldk", "ldx", "ldc", "n1", "n2", "n3", "w", "ow", "mask", "sign", "rows", "scales")


class Ring:

    def __init__(self, threads, full, empty):
        self.full, self.empty = full, empty
        self.slot = {}
        self.count = {}
        places = {thread: [x[2:] for x in turn if x[0] == thread and x[2] not in NO_BANK + ("pv",)]
                  for thread, turn in (("A", MIDDLE), ("B", MIDDLE), ("C", CONSTANTS))}
        uses = [0] * 4
        for t, turn in TURNS:
            for thread, lag, *unit in turn:
                if thread not in threads or unit[0] in NO_BANK or unit[0] == "pv" and unit[2] % 4:
                    continue
                unit = ("pv", unit[1], unit[2] // 4) if unit[0] == "pv" else tuple(unit)
                if unit not in self.slot:
                    self.slot[unit] = (3 if unit[0] == "pv" else places[thread].index(unit) % 3, lag)
                k = self.slot[unit][0]
                self.count[unit, t] = uses[k]
                uses[k] += 1

    def before(self, i, unit):
        return self.count[unit, i + self.slot[unit][1]]

    def bank(self, *name):
        return self.slot[name][0]

    def wait_full(self, eng, i, *name):
        eng.wait_ge(self.full[self.bank(*name)], self.before(i, name) + 1)

    def wait_emptied(self, eng, i, *name):
        eng.wait_ge(self.empty[self.bank(*name)], self.before(i, name) + 1)

    def wait_free(self, eng, i, *name):
        n = self.before(i, name)
        if n > 0:
            eng.wait_ge(self.empty[self.bank(*name)], n)

    def is_full(self, *name):
        return self.full[self.bank(*name)], 1

    def is_empty(self, *name):
        return self.empty[self.bank(*name)], 1


def decoder_layer(nc, x, ctx_1024, mask, qkvw, qkvb, ow, ob, fw, fb, gate_w, in_cs, out_cs, out, scr_q, scr_k, scr_x, scr_c):
    es = ExitStack()
    with es:
        def sb(name, shape, dt):
            return es.enter_context(nc.sbuf_tensor(name, shape, dt))

        def sem(name):
            return es.enter_context(nc.semaphore(name))

        wH = sb("wH", [P, KT, QBLK], F32R)
        wL = sb("wL", [P, KT, QBLK], F32R)
        owH = sb("owH", [P, KT, H], F32R)
        owL = sb("owL", [P, KT, H], F32R)
        swT = sb("swT", [P, KT, H], F32R)
        gT = sb("gT", [P, KT, E], F32)
        icS = sb("icS", [4 * E, H], F32R)
        ocS = sb("ocS", [4 * E, H], F32R)
        bqk = sb("bqk", [P, 2 * KT], F32)
        vbias = sb("vbias", [P, H], F32)
        obias = sb("obias", [P, H], F32)
        fbias = sb("fbias", [P, H], F32)
        mraw = sb("mraw", [P, P], F32)
        mH = sb("mH", [P, P], F32R)
        mL = sb("mL", [P, P], F32R)
        idf = sb("idf", [P, P], F32)
        idb = sb("idb", [P, P], BF16)
        idr = sb("idr", [P, 4, P], F32R)
        pick = sb("pick", [4 * E, 2], F32)
        one_row = sb("one_row", [NPART, TOK], BF16)
        half = sb("half", [P, 2], F32)
        x_in = sb("x_in", [P, GB, H], F32)
        xb = sb("xb", [P, GB, H], F32)
        xH = sb("xH", [P, KT, TOK], F32R)
        xL = sb("xL", [P, KT, TOK], F32R)
        qs = sb("qs", [P, HT, KT, TOK], BF16)
        ks = sb("ks", [P, HT, KT, TOK], BF16)
        qp = sb("qp", [P, NPART, KT, TOK], BF16)
        kp = sb("kp", [P, NPART, KT, TOK], BF16)
        wide_a = sb("wide_a", [P, 2, H], F32)
        va = sb("va", [P, GB, HEADS, VW], F32)
        pa = sb("pa", [P, NP, H], F32)
        nma = sb("nma", [P, GB, HEADS], F32)
        npa = sb("npa", [P, GB, NPART, HEADS], BF16)
        nra = sb("nra", [P, 2, HEADS], F32)
        mra = sb("mra", [NPART * HEADS, GB, P], BF16)
        cx = sb("cx", [P, H], F32)
        cH = sb("cH", [P, KT, P], F32R)
        cL = sb("cL", [P, KT, P], F32R)
        rda = sb("rda", [P, HEADS], F32)
        x1 = sb("x1", [P, GB, H], F32)
        sta = sb("sta", [P, 6], F32)
        mva = sb("mva", [P, GB, 2], F32)
        rsa = sb("rsa", [P, GB, 2], F32)
        c_in = sb("c_in", [P, GB, P], F32)
        c_perm = sb("c_perm", [P, GB, P], F32)
        xp = sb("xp", [P, NPART, GB * KT * P], BF16)
        qx = sb("qx", [P, GB, HT, KT, P], BF16)
        kx = sb("kx", [P, GB, KVH, P], BF16)
        rc = sb("rc", [P, P], F32)
        cp = sb("cp", [P, GB, NPART, P], BF16)
        wide_b = sb("wide_b", [P, 2, H], F32)
        vx = sb("vx", [P, GB, KVH, VW], F32)
        pb = sb("pb", [P, NP, H], F32)
        nmb = sb("nmb", [P, GB, HEADS], F32)
        npb = sb("npb", [P, GB, NPART, HEADS], BF16)
        nrb = sb("nrb", [P, 2, HEADS], F32)
        mrb = sb("mrb", [NPART * HEADS, GB, P], BF16)
        rdb = sb("rdb", [P, HEADS], F32)
        x2 = sb("x2", [P, GB, H], F32)
        stb = sb("stb", [P, 6], F32)
        mvb = sb("mvb", [P, GB, 2], F32)
        rsb = sb("rsb", [P, GB, 2], F32)
        lg = sb("lg", [E, TOK], F32)
        nl = sb("nl", [P, GB], F32)
        el = sb("el", [P, GB, E], F32)
        sl = sb("sl", [P, GB], F32)
        rl = sb("rl", [P, GB], F32)
        rt = sb("rt", [P, GB, E], F32)
        rtH = sb("rtH", [P, GB, E], F32R)
        rts = sb("rts", [P, GB, 4, E], F32)
        rT = sb("rT", [4 * E, TOK], F32R)

        def at(name, shape, dt, host, skip=0):
            return nc.alloc_sbuf_tensor_at(name, shape, dt, offset=nc.lookup_mloc(host).addr + skip)

        KB = 1024
        wraw = at("wraw", [P, KT, QBLK], F32, qs)
        oraw = at("oraw", [P, KT, H], F32, qx)
        fraw = at("fraw", [P, KT, H], F32, qx, 8 * KB)
        sgn = at("sgn", [P, KT, H], BF16, kx)
        icr = at("icr", [4 * E, H], F32, pb)
        ocr = at("ocr", [4 * E, H], F32, pb, 2 * KB)
        cshi = at("cshi", [4 * E, H], F32R, wide_b)
        cslo = at("cslo", [4 * E, H], F32, wide_b, 2 * KB)
        graw = at("graw", [E, H], F32, x2)
        braw = at("braw", [2 * KT, P], F32, x2, 2 * KB)
        bperm = at("bperm", [2 * KT, P], F32, x2, 3 * KB)
        def per_seq(name, dt, quarter):
            return [at(f"{name}{b}", [P, KT, P], dt, qx, (8 * b + 2 * quarter) * KB) for b in range(GB)]
        x2T = per_seq("x2T", F32, 0)
        zf = per_seq("zf", F32, 1)
        zH = per_seq("zH", F32R, 2)
        zL = per_seq("zL", F32R, 3)

        bank_a = [es.enter_context(nc.psum_tensor(f"bank_a{k}", [P, H], F32)) for k in range(4)]
        bank_b = [es.enter_context(nc.psum_tensor(f"bank_b{k}", [P, H], F32)) for k in range(4)]
        ra = Ring("A", [sem(f"full_a{k}") for k in range(4)], [sem(f"empty_a{k}") for k in range(4)])
        rb = Ring("BC", [sem(f"full_b{k}") for k in range(4)], [sem(f"empty_b{k}") for k in range(4)])

        def pa_bank(*name):
            return bank_a[ra.bank(*name)]

        def pb_bank(*name):
            return bank_b[rb.bank(*name)]

        ld_small, ld_mask, ld_ow, ld_fw, ld_cs = (sem(n) for n in ("ld_small", "ld_mask", "ld_ow", "ld_fw", "ld_cs"))
        ld_w = [sem(f"ld_w{k}") for k in range(3)]
        ld_vb, ld_ob, ld_fb = sem("ld_vb"), sem("ld_ob"), sem("ld_fb")
        idents, w_high, w_low = sem("idents"), sem("w_high"), sem("w_low")
        ow_high, ow_low, signs, masks = sem("ow_high"), sem("ow_low"), sem("signs"), sem("masks")
        scale_step, scales, ones_a, ones_b, picks = sem("scale_step"), sem("scales"), sem("ones_a"), sem("ones_b"), sem("picks")
        ident_step, ones_row, rows_a, rows_b = sem("ident_step"), sem("ones_row"), sem("rows_a"), sem("rows_b")
        x_loaded, xb_made, xh_made = sem("x_loaded"), sem("xb_made"), sem("xh_made")
        a_first, a_second, a_third = sem("a_first"), sem("a_second"), sem("a_third")
        q_stored, k_stored, q_stacked, k_stacked = sem("q_stored"), sem("k_stored"), sem("q_stacked"), sem("k_stacked")
        max_split_a, max_parts_a = sem("max_split_a"), sem("max_parts_a")
        max_stacked_a = [sem(f"max_stacked_a{b}") for b in range(GB)]
        pv_a, recip_a, ch_made = sem("pv_a"), sem("recip_a"), sem("ch_made")
        ln_a, rstd_step_a, rstd_a, x1_made = sem("ln_a"), sem("rstd_step_a"), sem("rstd_a"), sem("x1_made")
        def seq_sems(*names):
            return [[sem(f"{n}{b}") for b in range(GB)] for n in names]
        c_loaded, bias_permuted, pv_b = sem("c_loaded"), sem("bias_permuted"), sem("pv_b")
        c_permuted, vx_made = seq_sems("c_permuted", "vx_made")
        b_first, b_second, b_third = seq_sems("b_first", "b_second", "b_third")
        c_first, c_second, c_third = seq_sems("c_first", "c_second", "c_third")
        x_stored, c_stored, x_stacked, c_stacked = seq_sems("x_stored", "c_stored", "x_stacked", "c_stacked")
        max_split_b, max_parts_b, max_stacked_b, recip_b = seq_sems("max_split_b", "max_parts_b", "max_stacked_b", "recip_b")
        ln_b, rstd_step_b, rstd_b, x2_made, x2_biased = seq_sems("ln_b", "rstd_step_b", "rstd_b", "x2_made", "x2_biased")
        top_made, route_step, route_made = seq_sems("top_made", "route_step", "route_made")
        zh_made, zl_made, y_made, out_stored = seq_sems("zh_made", "zl_made", "y_made", "out_stored")

        def permuted(ap):
            return ap.rearrange("p (h d) -> p d h", d=HD)

        def by_head(ap):
            return ap.rearrange("p (m h d) -> p m h d", m=KT, d=HD)

        def tile_permuted(ap):
            return ap.rearrange("p (m d h) -> p m h d", m=KT, d=HD)

        def tokens(b):
            return slice(b * P, (b + 1) * P)

        def w_views(dst, src, kt, blk):
            to, of = dst[:, kt, blk * H:(blk + 1) * H], src[:, kt, blk * H:(blk + 1) * H]
            if blk == 2:
                return to, of
            return to.rearrange("p (m d h) -> p m d h", m=KT, d=HD), of.rearrange("p (m h d) -> p m d h", m=KT, d=HD)

        block = es.enter_context(nc.Block())

        @block.sync
        def _(sp):
            def load_x(i):
                sp.dma_start(x_in[:], x[GB * i:GB * (i + 1)].rearrange("b p f -> p b f")).then_inc(x_loaded, 16)

            def load_c(i):
                sp.dma_start(c_in[:], ctx_1024[GB * i:GB * (i + 1)].rearrange("b p f -> p b f")).then_inc(c_loaded, 16)

            def stack(dst, scratch, lows_first, done):
                n = 2 if lows_first else 0
                for row, first, last in ((0, 0, NPART), (3, n // 2, n // 2 + 2), (5, n, n + 1)):
                    src = scratch[first * HD:last * HD]
                    sp.dma_start(dst[row * HD:(row + last - first) * HD], src).then_inc(done, 16)

            wv = qkvw.rearrange("(kt p) n -> p kt n", p=P)
            sp.dma_start(wraw[:, :, 0:H], wv[:, :, 0:H]).then_inc(ld_w[0], 16)
            sp.dma_start(braw[:], qkvb[0:2 * H].rearrange("(t p) -> t p", p=P)).then_inc(ld_small, 16)
            sp.dma_start(graw[:], gate_w).then_inc(ld_small, 16)
            sp.dma_start(wraw[:, :, H:2 * H], wv[:, :, H:2 * H]).then_inc(ld_w[1], 16)
            sp.dma_start(wraw[:, :, 2 * H:3 * H], wv[:, :, 2 * H:3 * H]).then_inc(ld_w[2], 16)
            sp.dma_start(vbias[:], qkvb[2 * H:3 * H].partition_broadcast(P)).then_inc(ld_vb, 16)
            sp.dma_start(oraw[:], ow.rearrange("(kt p) n -> p kt n", p=P)).then_inc(ld_ow, 16)
            sp.dma_start(fraw[:], fw.rearrange("(ot p) n -> p ot n", p=P)).then_inc(ld_fw, 16)
            sp.dma_start(obias[:], ob.partition_broadcast(P)).then_inc(ld_ob, 16)
            sp.dma_start(mraw[:], mask).then_inc(ld_mask, 16)
            sp.dma_start(fbias[:], fb.partition_broadcast(P)).then_inc(ld_fb, 16)
            for k in range(4):
                sp.dma_start(icr[k * E:(k + 1) * E], in_cs).then_inc(ld_cs, 16)
                sp.dma_start(ocr[k * E:(k + 1) * E], out_cs).then_inc(ld_cs, 16)

            for t, turn in TURNS:
                for thread, lag, *step in turn:
                    i = t - lag
                    name = step[0]
                    if thread == "B" and name == "xt":
                        b = step[1]
                        sp.wait_ge(b_third[b], i + 1)
                        sp.dma_start(scr_x[i, b].rearrange("(c d) h f -> (d h) c f", d=HD),
                                     xp[:, :, b * H:(b + 1) * H]).then_inc(x_stored[b], 16)
                    elif name == "ldx":
                        b = step[1]
                        sp.wait_ge(x_stored[b], 16 * (i + 1))
                        if i > 0:
                            sp.wait_ge(ln_b[b], 6 * i - 2)
                        stack(qx[:, b].rearrange("r h m t -> r h (m t)"), scr_x[i, b], True, x_stacked[b])
                    elif thread == "B" and name == "ctx":
                        b = step[1]
                        sp.wait_ge(c_third[b], i + 1)
                        sp.dma_start(scr_c[i, b].rearrange("(c d) h f -> (d h) c f", d=HD), cp[:, b]).then_inc(c_stored[b], 16)
                    elif name == "ldc":
                        b = step[1]
                        sp.wait_ge(c_stored[b], 16 * (i + 1))
                        if i > 0:
                            sp.wait_ge(pv_b, KVH * (GB * (i - 1) + b + 1))
                        stack(kx[:, b], scr_c[i, b], False, c_stacked[b])
                    elif thread == "A" and step == ["q", 1]:
                        sp.wait_ge(a_third, 4 * i + 2)
                        sp.dma_start(scr_q[i].rearrange("(c d) h f -> (d h) c f", d=HD),
                                     qp[:].rearrange("p c m t -> p c (m t)")).then_inc(q_stored, 16)
                    elif name == "ldq":
                        sp.wait_ge(q_stored, 16 * (i + 1))
                        if i == 0:
                            sp.wait_ge(w_low, 3 * KT)
                        stack(qs[:].rearrange("r h m t -> r h (m t)"), scr_q[i], True, q_stacked)
                    elif thread == "A" and step == ["q", 3]:
                        sp.wait_ge(a_third, 4 * i + 4)
                        sp.dma_start(scr_k[i].rearrange("(c d) h f -> (d h) c f", d=HD),
                                     kp[:].rearrange("p c m t -> p c (m t)")).then_inc(k_stored, 16)
                    elif name == "ldk":
                        sp.wait_ge(k_stored, 16 * (i + 1))
                        stack(ks[:].rearrange("r h m t -> r h (m t)"), scr_k[i], False, k_stacked)
                    elif thread == "A" and name == "xb":
                        if i < NG - 1:
                            ra.wait_full(sp, i, "xt", 1)
                            sp.wait_ge(xb_made, GB * (i + 1))
                            load_x(i + 1)
                    elif name == "mt":
                        b = step[1]
                        src, dst, done, ring = (mra, qs, max_stacked_a[b], ra) if thread == "A" else (mrb, qx, max_stacked_b[b], rb)
                        ring.wait_emptied(sp, i, "mt", b)
                        for c in range(NPART):
                            row = dst[SR + c:SR + c + 1, :, :, tokens(b)] if thread == "A" else dst[SR + c:SR + c + 1, b]
                            sp.dma_start(row.rearrange("r h m t -> r (h m) t"),
                                         src[c * HEADS:(c + 1) * HEADS, b, :]).then_inc(done, 16)
                    elif thread == "A" and name == "lc":
                        if i > 0:
                            for b in range(GB):
                                sp.wait_ge(c_permuted[b], i)
                                sp.wait_ge(vx_made[b], i)
                        load_c(i)
                    elif thread == "C" and name == "ow":
                        sp.wait_ge(ones_row, 1)
                        sp.wait_ge(w_low, 3 * KT)
                        sp.dma_start(ks[SR:SM].rearrange("r h m t -> r (h m) t"),
                                     one_row[:].rearrange("r (o t) -> r o t", o=1).broadcast_to([NPART, HT * KT, TOK])).then_inc(rows_a, 16)
                    elif thread == "C" and name == "rows":
                        for kt in range(KT):
                            rb.wait_full(sp, 0, "swt", kt)
                        for b in range(GB):
                            sp.dma_start(kx[SR:SM, b], one_row[:, 0:P].rearrange("r (o t) -> r o t", o=1).broadcast_to([NPART, KVH, P])).then_inc(rows_b, 16)
                    elif thread == "B" and name == "n3":
                        b = step[1]
                        sp.wait_ge(y_made[b], i + 1)
                        sp.dma_start(out[GB * i + b], x2[:, b, :]).then_inc(out_stored[b], 16)
            for b in range(GB):
                sp.wait_ge(out_stored[b], 16 * NG)

        @block.gpsimd
        def _(pool):
            pool.memset(idf[:], 0.0).then_inc(ident_step, 1)
            pool.wait_ge(ident_step, 1)
            pool.affine_select(out=idf[:], in_=idf[:], compare_op=ALU.not_equal, fill=1.0, base=0,
                               pattern=[[-1, P]], channel_multiplier=1).then_inc(idents, 1)
            pool.memset(half[:], -0.5).then_inc(picks, 1)
            pool.memset(va[:], 1.0).then_inc(ones_a, 1)
            pool.memset(pick[:, 0:1], 0.0).then_inc(picks, 1)
            pool.memset(pick[:, 1:2], 1.0).then_inc(picks, 1)
            pool.wait_ge(picks, 3)
            pool.memset(pick[0:2 * E, 0:1], 1.0).then_inc(picks, 1)
            pool.memset(pick[0:2 * E, 1:2], 0.0).then_inc(picks, 1)
            pool.memset(vx[:], 1.0).then_inc(ones_b, 1)
            pool.memset(one_row[:], 1.0).then_inc(ones_row, 1)
            pool.wait_ge(idents, 1)
            pool.tensor_copy(idb[:], idf[:]).then_inc(idents, 1)

            def split_max(i, b, base, ring, nm, np_, nr, steps_done, parts_done):
                ring.wait_emptied(pool, i, "s", b, HT - 1)
                pool.tensor_copy(np_[:, b, 0, :], nm[:, b, :]).then_inc(steps_done, 1)
                pool.wait_ge(steps_done, base + 1)
                pool.tensor_tensor(nr[:, 0, :], nm[:, b, :], np_[:, b, 0, :], ALU.subtract).then_inc(steps_done, 1)
                pool.wait_ge(steps_done, base + 2)
                pool.tensor_copy(np_[:, b, 1, :], nr[:, 0, :]).then_inc(steps_done, 1)
                pool.wait_ge(steps_done, base + 3)
                pool.tensor_tensor(np_[:, b, 2, :], nr[:, 0, :], np_[:, b, 1, :], ALU.subtract).then_inc(parts_done, 1)

            def rstd(n, mv, rs, stats, step_done, done):
                pool.wait_ge(stats, 3 * n + 3)
                pool.tensor_scalar(rs[:, 0:1], mv[:, 1:2], EPS, None, ALU.add).then_inc(step_done, 1)
                pool.wait_ge(step_done, n + 1)
                pool.tensor_tensor(rs[:, 1:2], rs[:, 0:1], half[:, 0:1], ALU.pow).then_inc(done, 1)

            for t, turn in TURNS:
                for thread, lag, *step in turn:
                    i = t - lag
                    name = step[0]
                    if thread == "A" and name == "xb":
                        pool.wait_ge(x_loaded, 16 * (i + 1))
                        if i == 0:
                            pool.wait_ge(ld_ob, 16)
                        else:
                            ra.wait_emptied(pool, i - 1, "op", 1)
                        for b in range(GB):
                            pool.tensor_tensor(xb[:, b, :], x_in[:, b, :], obias[:], ALU.add).then_inc(xb_made, 1)
                    elif thread == "A" and name == "q":
                        j = step[1]
                        part, slot = (qp[:, 0], j) if j < 2 else (kp[:, 2], j - 2)
                        pool.wait_ge(a_second, 4 * i + j + 1)
                        mid = (qp if j < 2 else kp)[:, 1, 2 * slot:2 * slot + 2, :]
                        pool.tensor_tensor(part[:, 2 * slot:2 * slot + 2, :], wide_a[:, j % 2].rearrange("p (m t) -> p m t", m=2),
                                           mid, ALU.subtract).then_inc(a_third, 1)
                    elif thread == "A" and name == "mt":
                        split_max(i, step[1], 3 * (GB * i + step[1]), ra, nma, npa, nra, max_split_a, max_parts_a)
                    elif thread == "A" and name == "op":
                        rstd(GB * i + step[1], mva[:, step[1]], rsa[:, step[1]], ln_a, rstd_step_a, rstd_a)
                    elif thread == "B" and name == "xt":
                        b = step[1]
                        pool.wait_ge(b_second[b], i + 1)
                        own = slice(b * H, (b + 1) * H)
                        pool.tensor_tensor(xp[:, 0, own], wide_b[:, b], xp[:, 1, own], ALU.subtract).then_inc(b_third[b], 1)
                    elif thread == "B" and name == "ctx":
                        b = step[1]
                        pool.wait_ge(c_second[b], i + 1)
                        pool.tensor_tensor(cp[:, b, 2, :], rc[:], cp[:, b, 1, :], ALU.subtract).then_inc(c_third[b], 1)
                    elif thread == "B" and name == "cp":
                        b = step[1]
                        pool.wait_ge(c_loaded, 16 * (i + 1))
                        if i == 0:
                            pool.wait_ge(ones_b, 1)
                        else:
                            rb.wait_full(pool, i - 1, "ctx", b)
                            pool.wait_ge(pv_b, KVH * (GB * (i - 1) + b + 1))
                        pool.tensor_copy(c_perm[:, b, :].rearrange("p (d g) -> p d g", d=HD), permuted(c_in[:, b, :])).then_inc(c_permuted[b], 1)
                        pool.tensor_copy(vx[:, b, :, 0:HD], c_in[:, b, :].rearrange("p (g d) -> p g d", d=HD)).then_inc(vx_made[b], 1)
                    elif thread == "B" and name == "mt":
                        b = step[1]
                        split_max(i, b, 3 * i, rb, nmb, npb, nrb, max_split_b[b], max_parts_b[b])
                    elif thread == "B" and name == "ot" and step[2] == 1:
                        b = step[1]
                        rstd(2 * i, mvb[:, b], rsb[:, b], ln_b[b], rstd_step_b[b], rstd_b[b])
                    elif thread == "B" and name == "cx":
                        b = step[1]
                        rb.wait_full(pool, i, *step)
                        if i == 0 and b == 0:
                            pool.wait_ge(ld_fb, 16)
                        pool.tensor_tensor(x2[:, b, :], x2[:, b, :], fbias[:], ALU.add).then_inc(x2_biased[b], 1)
                    elif thread == "B" and name == "is":
                        b = step[1]
                        pool.wait_ge(zh_made[b], i + 1)
                        pool.tensor_tensor(zL[b][:], zf[b][:], zH[b][:].bitcast(F32), ALU.subtract).then_inc(zl_made[b], 1)
                    elif thread == "B" and name == "ff":
                        b = step[1]
                        rstd(2 * i + 1, mvb[:, b], rsb[:, b], ln_b[b], rstd_step_b[b], rstd_b[b])
                    elif thread == "C" and name == "ow":
                        pool.wait_ge(ow_high, KT)
                        for kt in range(KT):
                            pool.tensor_tensor(owL[:, kt, :], oraw[:, kt, :], owH[:, kt, :].bitcast(F32), ALU.subtract).then_inc(ow_low, 1)

        @block.scalar
        def _(act):
            act.dma_start(x_in[:], x[0:GB].rearrange("b p f -> p b f")).then_inc(x_loaded, 16)

            for t, turn in TURNS:
                for thread, lag, *step in turn:
                    i = t - lag
                    name = step[0]
                    if thread == "A" and name == "xt":
                        u = step[1]
                        ra.wait_full(act, i, *step)
                        act.activation(xH[:, 2 * u:2 * u + 2, :], pa_bank(*step)[:].rearrange("p (m t) -> p m t", m=2), ACT.Copy).then_inc(xh_made, 1)
                    elif thread == "A" and name == "q":
                        j = step[1]
                        dst, slot, stored = (qp[:, 2], j, q_stored) if j < 2 else (kp[:, 0], j - 2, k_stored)
                        ra.wait_full(act, i, *step)
                        if i == 0 and j == 0:
                            rb.wait_emptied(act, 0, "small")
                        if i > 0:
                            act.wait_ge(stored, 16 * i)
                        for m in range(2):
                            last = act.activation(dst[:, 2 * slot + m, :], pa_bank(*step)[:, m * TOK:(m + 1) * TOK], ACT.Identity,
                                                  bias=bqk[:, 2 * j + m:2 * j + m + 1])
                        last.then_inc(a_first, 1)
                    elif name == "st":
                        b, j = step[1:]
                        ring, bank, pr, pv, scale = ((ra, pa_bank, pa, pv_a, HD ** -0.5) if thread == "A"
                                                        else (rb, pb_bank, pb, pv_b, 1.0))
                        n = (GB * i + b) * HT + j
                        ring.wait_full(act, i, *step)
                        if n >= NP:
                            act.wait_ge(pv, n - NP + 1)
                        if thread == "B" and n == 0:
                            act.wait_ge(scales, 2)
                        act.activation(pr[:, n % NP, :], bank(*step)[:], ACT.Exp, scale=scale).then_inc(*ring.is_empty(*step))
                    elif name == "pv" and step[2] % 4 == 3:
                        b, u = step[1], step[2] // 4
                        ring, bank, wide, pv = (ra, pa_bank, wide_a, pv_a) if thread == "A" else (rb, pb_bank, wide_b, pv_b)
                        act.wait_ge(pv, (GB * i + b) * HT + 4 * u + 4)
                        act.activation(wide[:, u, :], bank("pv", b, u)[:], ACT.Copy).then_inc(*ring.is_empty("pv", b, u))
                    elif thread == "A" and name == "ct":
                        ra.wait_full(act, i, *step)
                        act.activation(cH[:], pa_bank(*step)[:].rearrange("p (k t) -> p k t", k=KT), ACT.Copy).then_inc(ch_made, 1)
                    elif thread == "B" and name == "xt":
                        b = step[1]
                        rb.wait_full(act, i, *step)
                        if i > 0:
                            act.wait_ge(x_stored[b], 16 * i)
                        act.activation(xp[:, 2, b * H:(b + 1) * H], pb_bank(*step)[:], ACT.Copy, scale=HD ** -0.5).then_inc(b_first[b], 1)
                    elif thread == "B" and name == "ctx":
                        b = step[1]
                        rb.wait_full(act, i, *step)
                        if i > 0:
                            act.wait_ge(c_stored[b], 16 * i)
                        act.activation(cp[:, b, 0, :], pb_bank(*step)[:, 0:P], ACT.Copy).then_inc(c_first[b], 1)
                    elif thread == "B" and name == "cx":
                        b = step[1]
                        rb.wait_full(act, i, *step)
                        act.activation(x2T[b][:], pb_bank(*step)[:].rearrange("p (k t) -> p k t", k=KT), ACT.Copy).then_inc(*rb.is_empty(*step))
                    elif thread == "B" and name == "rl":
                        rb.wait_full(act, i, *step)
                        act.activation(lg[:, tokens(step[1])], pb_bank(*step)[0:E, 0:P], ACT.Copy).then_inc(*rb.is_empty(*step))
                    elif thread == "B" and name == "rt":
                        b = step[1]
                        act.wait_ge(top_made[b], i + 1)
                        act.activation(el[:, b, :], pb_bank(*step)[:, 0:E], ACT.Exp, bias=nl[:, b:b + 1]).then_inc(*rb.is_empty(*step))
                    elif thread == "B" and name == "rr":
                        rb.wait_full(act, i, *step)
                        act.activation(rT[:, tokens(step[1])], pb_bank(*step)[0:4 * E, 0:P], ACT.Copy).then_inc(*rb.is_empty(*step))
                    elif thread == "B" and name == "is":
                        b = step[1]
                        rb.wait_emptied(act, i, *step)
                        act.activation(zH[b][:], zf[b][:], ACT.Copy).then_inc(zh_made[b], 1)
                    elif thread == "B" and name == "os":
                        b = step[1]
                        rb.wait_full(act, i, *step)
                        rb.wait_emptied(act, i, "is", b)
                        act.activation(x2T[b][:], pb_bank(*step)[:].rearrange("p (k t) -> p k t", k=KT), ACT.Copy).then_inc(*rb.is_empty(*step))
                    elif thread == "C" and name == "w":
                        blk = step[1]
                        act.wait_ge(ld_w[blk], 16)
                        for kt in range(KT):
                            act.activation(*w_views(wH, wraw, kt, blk), ACT.Copy).then_inc(w_high, 1)
                    elif thread == "C" and name == "ow":
                        act.wait_ge(ld_ow, 16)
                        for kt in range(KT):
                            act.activation(owH[:, kt, :], oraw[:, kt, :], ACT.Copy).then_inc(ow_high, 1)
                    elif thread == "C" and name == "sign":
                        act.wait_ge(ld_fw, 16)
                        for k in range(KT):
                            act.activation(sgn[:, k, :], fraw[:, k, :], ACT.Sign).then_inc(signs, 1)

        @block.vector
        def _(dve):
            def deviations(n, v, b):
                dve.wait_ge(ln_b[b], 3 * n + 1)
                dve.bn_stats(stb[:], v).then_inc(ln_b[b], 1)
                dve.wait_ge(ln_b[b], 3 * n + 2)
                dve.bn_aggr(mvb[:, b], stb[:]).then_inc(ln_b[b], 1)

            def normalise(n, v, b, done):
                dve.wait_ge(rstd_b[b], n + 1)
                dve.tensor_scalar(v, v, mvb[:, b, 0:1], rsb[:, b, 1:2], ALU.subtract, ALU.mult).then_inc(done, 1)

            for t, turn in TURNS:
                for thread, lag, *step in turn:
                    i = t - lag
                    name = step[0]
                    if thread == "A" and name == "xt":
                        u = step[1]
                        dve.wait_ge(xh_made, 2 * i + u + 1)
                        dve.tensor_tensor(xL[:, 2 * u:2 * u + 2, :], pa_bank(*step)[:].rearrange("p (m t) -> p m t", m=2),
                                          xH[:, 2 * u:2 * u + 2, :].bitcast(F32), ALU.subtract).then_inc(*ra.is_empty(*step))
                    elif thread == "A" and name == "q":
                        j = step[1]
                        parts, slot, hi = (qp, j, 2) if j < 2 else (kp, j - 2, 0)
                        dve.wait_ge(a_first, 4 * i + j + 1)
                        if 4 * i + j >= 2:
                            dve.wait_ge(a_third, 4 * i + j - 1)
                        for m in range(2):
                            last = dve.scalar_tensor_tensor(wide_a[:, j % 2, m * TOK:(m + 1) * TOK], pa_bank(*step)[:, m * TOK:(m + 1) * TOK],
                                                            bqk[:, 2 * j + m:2 * j + m + 1], parts[:, hi, 2 * slot + m, :], ALU.add, ALU.subtract)
                        last.then_inc(*ra.is_empty(*step))
                        ra.wait_emptied(dve, i, *step)
                        dve.tensor_copy(parts[:, 1, 2 * slot:2 * slot + 2, :], wide_a[:, j % 2].rearrange("p (m t) -> p m t", m=2)).then_inc(a_second, 1)
                    elif thread == "A" and name == "v":
                        b = step[1]
                        ra.wait_full(dve, i, *step)
                        if i == 0 and b == 0:
                            dve.wait_ge(ld_vb, 16)
                            dve.wait_ge(ones_a, 1)
                        dve.tensor_tensor(va[:, b].rearrange("p (h m) w -> p m h w", m=KT)[:, :, :, 0:HD],
                                          pa_bank(*step)[:].rearrange("p (m h d) -> p m h d", m=KT, d=HD),
                                          vbias[:].rearrange("p (m h d) -> p m h d", m=KT, d=HD), ALU.add).then_inc(*ra.is_empty(*step))
                    elif thread == "A" and name == "s":
                        b, j = step[1:]
                        ra.wait_full(dve, i, *step)
                        dve.tensor_reduce(nma[:, b, 4 * j:4 * j + 4], pa_bank(*step)[:].rearrange("p (m t) -> p m t", m=KT), AX.X, ALU.max,
                                          negate=True).then_inc(*ra.is_empty(*step))
                    elif name == "mt":
                        b = step[1]
                        ring, bank, mr = (ra, pa_bank, mra) if thread == "A" else (rb, pb_bank, mrb)
                        ring.wait_full(dve, i, *step)
                        dve.tensor_copy(mr[:, b, :], bank(*step)[0:NPART * HEADS, 0:P // 2].bitcast(BF16)).then_inc(*ring.is_empty(*step))
                    elif thread == "A" and name == "ot":
                        b, u = step[1:]
                        ra.wait_full(dve, i, *step)
                        v = pa_bank(*step)[:].rearrange("p (s c w) -> p s c w", s=4, w=VW)
                        rd = rda[:, 16 * u:16 * u + 16].rearrange("p (s c o) -> p s c o", s=4, o=1)
                        dve.reciprocal(rd, v[:, :, :, HD:HD + 1]).then_inc(recip_a, 1)
                        dve.wait_ge(recip_a, 2 * (GB * i + b) + u + 1)
                        dve.tensor_tensor(cx[:].rearrange("p (c u s d) -> p u s c d", c=KT, u=2, d=HD)[:, u], v[:, :, :, 0:HD],
                                          rd.broadcast_to([P, 4, 4, HD]), ALU.mult).then_inc(*ra.is_empty(*step))
                    elif thread == "A" and name == "ct":
                        dve.wait_ge(ch_made, GB * i + step[1] + 1)
                        dve.tensor_tensor(cL[:], pa_bank(*step)[:].rearrange("p (k t) -> p k t", k=KT), cH[:].bitcast(F32),
                                          ALU.subtract).then_inc(*ra.is_empty(*step))
                    elif thread == "A" and name == "op":
                        b = step[1]
                        n = GB * i + b
                        ra.wait_full(dve, i, *step)
                        dve.wait_ge(xb_made, n + 1)
                        dve.tensor_tensor(tile_permuted(x1[:, b, :]), by_head(pa_bank(*step)[:]), by_head(xb[:, b, :]), ALU.add).then_inc(*ra.is_empty(*step))
                        ra.wait_emptied(dve, i, *step)
                        dve.bn_stats(sta[:], x1[:, b, :]).then_inc(ln_a, 1)
                        dve.wait_ge(ln_a, 3 * n + 1)
                        dve.bn_aggr(mva[:, b], sta[:]).then_inc(ln_a, 2)
                    elif thread == "A" and name == "n1":
                        b = step[1]
                        dve.wait_ge(rstd_a, GB * i + b + 1)
                        dve.tensor_scalar(x1[:, b, :], x1[:, b, :], mva[:, b, 0:1], rsa[:, b, 1:2], ALU.subtract, ALU.mult).then_inc(x1_made, 1)
                    elif thread == "B" and name == "xt":
                        b = step[1]
                        dve.wait_ge(b_first[b], i + 1)
                        own = slice(b * H, (b + 1) * H)
                        rest = wide_b[:, b]
                        dve.scalar_tensor_tensor(rest, pb_bank(*step)[:], HD ** -0.5, xp[:, 2, own], ALU.mult, ALU.subtract).then_inc(*rb.is_empty(*step))
                        rb.wait_emptied(dve, i, *step)
                        dve.tensor_copy(xp[:, 1, own], rest).then_inc(b_second[b], 1)
                    elif thread == "B" and name == "ctx":
                        b = step[1]
                        dve.wait_ge(c_first[b], i + 1)
                        if b == 1:
                            dve.wait_ge(c_third[0], i + 1)
                        elif i > 0:
                            dve.wait_ge(c_third[1], i)
                        dve.tensor_tensor(rc[:], pb_bank(*step)[:, 0:P], cp[:, b, 0, :], ALU.subtract).then_inc(*rb.is_empty(*step))
                        rb.wait_emptied(dve, i, *step)
                        dve.tensor_copy(cp[:, b, 1, :], rc[:]).then_inc(c_second[b], 1)
                    elif thread == "B" and name == "s":
                        b, g = step[1:]
                        rb.wait_full(dve, i, *step)
                        if g > 0:
                            rb.wait_emptied(dve, i, "s", b, g - 1)
                        elif i > 0:
                            dve.wait_ge(out_stored[b], 16 * i)
                        for r in range(4):
                            col = (4 * (g % 2) + r) * KT + g // 2
                            last = dve.tensor_tensor_reduce(x2[:, b, r * P:(r + 1) * P], pb_bank(*step)[:, r * P:(r + 1) * P], mraw[:], -1.0, -LOWEST,
                                                            ALU.add, ALU.min, nmb[:, b, col:col + 1])
                        last.then_inc(*rb.is_empty(*step))
                    elif thread == "B" and name == "ot":
                        b, u = step[1:]
                        rb.wait_full(dve, i, *step)
                        v = pb_bank(*step)[:].rearrange("p (r c w) -> p r c w", r=4, w=VW)
                        rd = rdb[:, 16 * u:16 * u + 16].rearrange("p (r c o) -> p r c o", r=4, o=1)
                        dve.reciprocal(rd, v[:, :, :, HD:HD + 1]).then_inc(recip_b[b], 1)
                        dve.wait_ge(recip_b[b], 2 * i + u + 1)
                        dve.tensor_tensor(x2[:, b, :].rearrange("p (u c r d) -> p u r c d", u=2, c=4, d=HD)[:, u], v[:, :, :, 0:HD],
                                          rd.broadcast_to([P, 4, 4, HD]), ALU.mult).then_inc(*rb.is_empty(*step))
                        if u == 1:
                            rb.wait_emptied(dve, i, "ot", b, 0)
                            rb.wait_emptied(dve, i, "ot", b, 1)
                            dve.tensor_tensor(by_head(x2[:, b, :]), by_head(x2[:, b, :]), tile_permuted(x1[:, b, :]), ALU.add).then_inc(ln_b[b], 1)
                            deviations(2 * i, x2[:, b, :], b)
                    elif thread == "B" and name == "n2":
                        b = step[1]
                        normalise(2 * i, x2[:, b, :], b, x2_made[b])
                    elif thread == "B" and name == "rt":
                        b = step[1]
                        rb.wait_full(dve, i, *step)
                        dve.tensor_reduce(nl[:, b:b + 1], pb_bank(*step)[:, 0:E], AX.X, ALU.max, negate=True).then_inc(top_made[b], 1)
                    elif thread == "B" and name == "rr":
                        b = step[1]
                        rb.wait_emptied(dve, i, "rt", b)
                        dve.tensor_reduce(sl[:, b:b + 1], el[:, b, :], AX.X, ALU.add).then_inc(route_step[b], 1)
                        dve.wait_ge(route_step[b], 5 * i + 1)
                        dve.reciprocal(rl[:, b:b + 1], sl[:, b:b + 1]).then_inc(route_step[b], 1)
                        dve.wait_ge(route_step[b], 5 * i + 2)
                        dve.tensor_scalar(rt[:, b, :], el[:, b, :], rl[:, b:b + 1], None, ALU.mult).then_inc(route_step[b], 1)
                        dve.wait_ge(route_step[b], 5 * i + 3)
                        dve.tensor_copy(rtH[:, b, :], rt[:, b, :]).then_inc(route_step[b], 1)
                        dve.wait_ge(route_step[b], 5 * i + 4)
                        high = rtH[:, b, :].bitcast(F32)
                        for k in (0, 2):
                            dve.tensor_copy(rts[:, b, k, :], high)
                            last = dve.tensor_tensor(rts[:, b, k + 1, :], rt[:, b, :], high, ALU.subtract)
                            last.then_inc((route_step if k == 0 else route_made)[b], 1)
                    elif thread == "B" and name == "is":
                        b = step[1]
                        rb.wait_full(dve, i, *step)
                        rb.wait_emptied(dve, i, "cx", b)
                        dve.tensor_tensor(zf[b][:], pb_bank(*step)[:].rearrange("p (k t) -> p k t", k=KT), x2T[b][:], ALU.mult).then_inc(*rb.is_empty(*step))
                    elif thread == "B" and name == "ff":
                        b = step[1]
                        rb.wait_full(dve, i, *step)
                        rb.wait_emptied(dve, i, "os", b)
                        scaled = x2T[b][:].rearrange("p k t -> p (k t)")
                        dve.tensor_tensor(scaled, pb_bank(*step)[:], scaled, ALU.mult).then_inc(*rb.is_empty(*step))
                        rb.wait_emptied(dve, i, *step)
                        dve.wait_ge(x2_biased[b], i + 1)
                        dve.tensor_tensor(x2[:, b, :], scaled, x2[:, b, :], ALU.add).then_inc(ln_b[b], 1)
                        deviations(2 * i + 1, x2[:, b, :], b)
                    elif thread == "B" and name == "n3":
                        b = step[1]
                        normalise(2 * i + 1, x2[:, b, :], b, y_made[b])
                    elif thread == "C" and name == "w":
                        blk = step[1]
                        for kt in range(KT):
                            dve.wait_ge(w_high, KT * blk + kt + 1)
                            low, raw = w_views(wL, wraw, kt, blk)
                            high = wH[:, kt, blk * H:(blk + 1) * H].bitcast(F32)
                            if blk < 2:
                                high = high.rearrange("p (m d h) -> p m d h", m=KT, d=HD)
                            dve.tensor_tensor(low, raw, high, ALU.subtract).then_inc(w_low, 1)
                    elif thread == "C" and name == "small":
                        dve.wait_ge(ld_small, 32)
                        dve.tensor_copy(bperm[:].rearrange("p (d h) -> p d h", d=HD), permuted(braw[:])).then_inc(bias_permuted, 1)
                        rb.wait_full(dve, 0, "small")
                        dve.tensor_copy(bqk[:], pb_bank("small")[:, 0:2 * KT])
                        dve.tensor_copy(gT[:], pb_bank("small")[:, P:P + KT * E].rearrange("p (k e) -> p k e", e=E)).then_inc(*rb.is_empty("small"))
                    elif thread == "C" and name == "mask":
                        dve.wait_ge(ld_mask, 16)
                        dve.tensor_copy(mH[:], mraw[:]).then_inc(masks, 1)
                        dve.wait_ge(masks, 1)
                        dve.tensor_tensor(mL[:], mraw[:], mH[:].bitcast(F32), ALU.subtract).then_inc(masks, 1)
                        dve.wait_ge(idents, 1)
                        for r in range(4):
                            last = dve.tensor_copy(idr[:, r, :], idf[:])
                        last.then_inc(masks, 1)
                    elif thread == "C" and name == "swt":
                        rb.wait_full(dve, 0, *step)
                        dve.tensor_copy(swT[:, step[1], :], pb_bank(*step)[:, 0:H // 2].bitcast(BF16)).then_inc(*rb.is_empty(*step))
                    elif thread == "C" and name == "scales":
                        dve.wait_ge(ld_cs, 16 * 8)
                        dve.wait_ge(picks, 5)
                        for k, (raw, dst) in enumerate(((icr, icS), (ocr, ocS))):
                            dve.tensor_copy(cshi[:], raw[:]).then_inc(scale_step, 1)
                            dve.wait_ge(scale_step, 3 * k + 1)
                            dve.tensor_tensor(cslo[:], raw[:], cshi[:].bitcast(F32), ALU.subtract).then_inc(scale_step, 1)
                            dve.wait_ge(scale_step, 3 * k + 2)
                            dve.tensor_scalar(cslo[:], cslo[:], pick[:, 1:2], None, ALU.mult).then_inc(scale_step, 1)
                            dve.wait_ge(scale_step, 3 * k + 3)
                            dve.scalar_tensor_tensor(dst[:], cshi[:].bitcast(F32), pick[:, 0:1], cslo[:], ALU.mult, ALU.add).then_inc(scales, 1)
                            dve.wait_ge(scales, k + 1)

        @block.tensor
        def _(pe):
            def project(dst, lefts, rights):
                for kt in range(KT):
                    (lh, ll), (rh, rl_) = lefts(kt), rights(kt)
                    pe.matmul(dst, lh, rh, start=kt == 0, stop=False)
                    pe.matmul(dst, lh, rl_, start=False, stop=False)
                    last = pe.matmul(dst, ll, rh, start=False, stop=kt == KT - 1)
                return last

            for t, turn in TURNS:
                for thread, lag, *step in turn:
                    i = t - lag
                    name = step[0]
                    if thread == "A" and name not in NO_BANK + ("pv",):
                        ra.wait_free(pe, i, *step)
                        dst = pa_bank(*step)
                    elif thread == "B" and name not in NO_BANK + ("pv",):
                        rb.wait_free(pe, i, *step)
                        dst = pb_bank(*step)
                    if thread == "A" and name == "xt":
                        u = step[1]
                        pe.wait_ge(x_loaded, 16 * (i + 1))
                        if i == 0 and u == 0:
                            pe.wait_ge(idents, 1)
                        for m in range(2):
                            for b in range(GB):
                                kt = 2 * u + m
                                last = pe.transpose(dst[:, m * TOK + b * P:m * TOK + (b + 1) * P], x_in[:, b, kt * P:(kt + 1) * P], idf[:])
                        last.then_inc(*ra.is_full(*step))
                    elif thread == "A" and name == "q":
                        j = step[1]
                        if j == 0:
                            ra.wait_emptied(pe, i, "xt", 0)
                            ra.wait_emptied(pe, i, "xt", 1)
                        if i == 0 and j % 2 == 0:
                            pe.wait_ge(w_low, KT * (j // 2 + 1))
                        for m in range(2):
                            col = (2 * j + m) * P
                            last = project(dst[:, m * TOK:(m + 1) * TOK],
                                           lambda kt: (wH[:, kt, col:col + P], wL[:, kt, col:col + P]),
                                           lambda kt: (xH[:, kt, :], xL[:, kt, :]))
                        last.then_inc(*ra.is_full(*step))
                    elif thread == "A" and name == "v":
                        b = step[1]
                        if i == 0 and b == 0:
                            pe.wait_ge(w_low, 3 * KT)
                        project(dst[:], lambda kt: (xH[:, kt, tokens(b)], xL[:, kt, tokens(b)]),
                                lambda kt: (wH[:, kt, 2 * H:3 * H], wL[:, kt, 2 * H:3 * H])).then_inc(*ra.is_full(*step))
                    elif thread == "A" and name == "s":
                        b, j = step[1:]
                        if b == 0 and j == 0:
                            pe.wait_ge(q_stacked, 48 * (i + 1))
                            pe.wait_ge(k_stacked, 48 * (i + 1))
                        for m in range(KT):
                            last = pe.matmul(dst[:, m * P:(m + 1) * P], qs[0:SR, j, m, tokens(b)], ks[0:SR, j, m, tokens(b)], start=True, stop=True)
                        last.then_inc(*ra.is_full(*step))
                    elif name == "mt":
                        b = step[1]
                        ring, parts, done = (ra, npa, max_parts_a) if thread == "A" else (rb, npb, max_parts_b[b])
                        if i == 0:
                            pe.wait_ge(idents, 2)
                        pe.wait_ge(done, GB * i + b + 1 if thread == "A" else i + 1)
                        pe.transpose(dst[0:NPART * HEADS, 0:P // 2].bitcast(BF16), parts[:, b].rearrange("p c h -> p (c h)"), idb[:]).then_inc(*ring.is_full(*step))
                    elif thread == "A" and name == "st":
                        b, j = step[1:]
                        if j == 0:
                            pe.wait_ge(max_stacked_a[b], 48 * (i + 1))
                            if i == 0:
                                pe.wait_ge(rows_a, 16)
                        for m in range(KT):
                            last = pe.matmul(dst[:, m * P:(m + 1) * P], ks[0:SM, j, m, tokens(b)], qs[0:SM, j, m, tokens(b)], start=True, stop=True)
                        last.then_inc(*ra.is_full(*step))
                    elif thread == "A" and name == "pv":
                        b, j = step[1:]
                        n = (GB * i + b) * HT + j
                        if j % 4 == 0:
                            ra.wait_free(pe, i, "pv", b, j // 4)
                        dst = pa_bank("pv", b, j // 4)
                        ra.wait_emptied(pe, i, "st", b, j)
                        if j == 0:
                            ra.wait_emptied(pe, i, "v", b)
                        for m in range(KT):
                            last = pe.matmul(dst[m * VW:(m + 1) * VW, (j % 4) * P:(j % 4 + 1) * P], va[:, b, j * KT + m, :],
                                             pa[:, n % NP, m * P:(m + 1) * P], start=True, stop=True)
                        last.then_inc(pv_a, 1)
                    elif name == "ot":
                        b, u = step[1:]
                        ring, wide = (ra, wide_a) if thread == "A" else (rb, wide_b)
                        ring.wait_emptied(pe, i, "pv", b, u)
                        for s in range(4):
                            last = pe.transpose(dst[:, s * P:(s + 1) * P], wide[:, u, s * P:(s + 1) * P], idf[:])
                        last.then_inc(*ring.is_full(*step))
                    elif thread == "A" and name == "ct":
                        b = step[1]
                        ra.wait_emptied(pe, i, "ot", b, 0)
                        ra.wait_emptied(pe, i, "ot", b, 1)
                        for kt in range(KT):
                            last = pe.transpose(dst[:, kt * P:(kt + 1) * P], cx[:, kt * P:(kt + 1) * P], idf[:])
                        last.then_inc(*ra.is_full(*step))
                    elif thread == "A" and name == "op":
                        b = step[1]
                        ra.wait_emptied(pe, i, "ct", b)
                        if i == 0 and b == 0:
                            pe.wait_ge(ow_low, KT)
                        project(dst[:], lambda kt: (cH[:, kt, :], cL[:, kt, :]),
                                lambda kt: (owH[:, kt, :], owL[:, kt, :])).then_inc(*ra.is_full(*step))
                    elif thread == "B" and name == "xt":
                        b = step[1]
                        pe.wait_ge(x1_made, GB * i + b + 1)
                        for kt in range(KT):
                            last = pe.transpose(dst[:, kt * P:(kt + 1) * P], x1[:, b, kt * P:(kt + 1) * P], idf[:])
                        last.then_inc(*rb.is_full(*step))
                    elif thread == "B" and name == "ctx":
                        b = step[1]
                        pe.wait_ge(c_permuted[b], i + 1)
                        pe.transpose(dst[:, 0:P], c_perm[:, b, :], idf[:]).then_inc(*rb.is_full(*step))
                    elif thread == "B" and name == "s":
                        b, g = step[1:]
                        if g == 0:
                            pe.wait_ge(x_stacked[b], 48 * (i + 1))
                            pe.wait_ge(c_stacked[b], 48 * (i + 1))
                        for r in range(4):
                            last = pe.matmul(dst[:, r * P:(r + 1) * P], qx[0:SR, b, 4 * (g % 2) + r, g // 2, :], kx[0:SR, b, g, :],
                                             start=True, stop=True)
                        last.then_inc(*rb.is_full(*step))
                    elif thread == "B" and name == "st":
                        b, g = step[1:]
                        if g == 0:
                            pe.wait_ge(max_stacked_b[b], 48 * (i + 1))
                            if i == 0:
                                pe.wait_ge(rows_b, 16 * GB)
                                pe.wait_ge(masks, 3)
                        d4 = dst[:].rearrange("p (r t) -> p r t", r=4)
                        pe.matmul(d4, mH[:], idr[:], start=True, stop=False)
                        pe.matmul(d4, mL[:], idr[:], start=False, stop=False)
                        a = 4 * (g % 2)
                        pe.matmul(d4, kx[0:SM, b, g, :], qx[0:SM, b, a:a + 4, g // 2, :], start=False, stop=True).then_inc(*rb.is_full(*step))
                    elif thread == "B" and name == "pv":
                        b, g = step[1:]
                        n = (GB * i + b) * KVH + g
                        if g % 4 == 0:
                            rb.wait_free(pe, i, "pv", b, g // 4)
                        dst = pb_bank("pv", b, g // 4)
                        rb.wait_emptied(pe, i, "st", b, g)
                        if g == 0:
                            pe.wait_ge(vx_made[b], i + 1)
                        c = g % 4
                        pe.matmul(dst[c * VW:(c + 1) * VW, :], vx[:, b, g, :], pb[:, n % NP, :], start=True, stop=True).then_inc(pv_b, 1)
                    elif thread == "B" and name == "cx":
                        b = step[1]
                        pe.wait_ge(x2_made[b], i + 1)
                        for kt in range(KT):
                            last = pe.transpose(dst[:, kt * P:(kt + 1) * P], x2[:, b, kt * P:(kt + 1) * P], idf[:])
                        last.then_inc(*rb.is_full(*step))
                    elif thread == "B" and name == "rl":
                        b = step[1]
                        rb.wait_emptied(pe, i, "cx", b)
                        for kt in range(KT):
                            last = pe.matmul(dst[0:E, 0:P], gT[:, kt, :], x2T[b][:, kt, :], start=kt == 0, stop=kt == KT - 1)
                        last.then_inc(*rb.is_full(*step))
                    elif thread == "B" and name == "rt":
                        b = step[1]
                        rb.wait_emptied(pe, i, "rl", b)
                        pe.transpose(dst[:, 0:E], lg[:, tokens(b)], idf[0:E, 0:E]).then_inc(*rb.is_full(*step))
                    elif thread == "B" and name == "rr":
                        b = step[1]
                        pe.wait_ge(route_made[b], i + 1)
                        pe.transpose(dst[0:4 * E, 0:P], rts[:, b].rearrange("p k e -> p (k e)"), idf[:]).then_inc(*rb.is_full(*step))
                    elif thread == "B" and name == "is":
                        b = step[1]
                        rb.wait_emptied(pe, i, "rr", b)
                        for kt in range(KT):
                            last = pe.matmul(dst[:, kt * P:(kt + 1) * P], icS[:, kt * P:(kt + 1) * P], rT[:, tokens(b)], start=True, stop=True)
                        last.then_inc(*rb.is_full(*step))
                    elif thread == "B" and name == "os":
                        pe.matmul(dst[:], rT[:, tokens(step[1])], ocS[:], start=True, stop=True).then_inc(*rb.is_full(*step))
                    elif thread == "B" and name == "ff":
                        b = step[1]
                        pe.wait_ge(zh_made[b], i + 1)
                        pe.wait_ge(zl_made[b], i + 1)
                        for kt in range(KT):
                            pe.matmul(dst[:], zH[b][:, kt, :], swT[:, kt, :], start=kt == 0, stop=False)
                            last = pe.matmul(dst[:], zL[b][:, kt, :], swT[:, kt, :], start=False, stop=kt == KT - 1)
                        last.then_inc(*rb.is_full(*step))
                    elif thread == "C" and name == "small":
                        pe.wait_ge(idents, 1)
                        pe.wait_ge(ld_small, 32)
                        pe.wait_ge(bias_permuted, 1)
                        dst = pb_bank("small")
                        pe.transpose(dst[:, 0:2 * KT], bperm[:], idf[0:2 * KT, 0:2 * KT])
                        for kt in range(KT):
                            last = pe.transpose(dst[:, P + kt * E:P + (kt + 1) * E], graw[:, kt * P:(kt + 1) * P], idf[0:E, 0:E])
                        last.then_inc(*rb.is_full("small"))
                    elif thread == "C" and name == "swt":
                        kt = step[1]
                        rb.wait_free(pe, 0, *step)
                        pe.wait_ge(signs, KT)
                        pe.wait_ge(idents, 2)
                        dst = pb_bank(*step)[:, 0:H // 2].bitcast(BF16)
                        for o in range(KT):
                            last = pe.transpose(dst[:, o * P:(o + 1) * P], sgn[:, o, kt * P:(kt + 1) * P], idb[:])
                        last.then_inc(*rb.is_full(*step))


_INS = ["x", "ctx_1024", "mask_SxS2_ff0", "L0_attn_attn_qkvw", "L0_attn_attn_qkvb", "L0_attn_attn_ow", "L0_attn_attn_ob",
        "L0_ffn_weight", "L0_ffn_bias", "L0_ffn_gate_w", "L0_ffn_in_channel_scale", "L0_ffn_out_channel_scale"]


def kernel(**inputs):
    import numpy as _np
    import concourse.bacc as _bacc
    from concourse import mybir as _mybir
    from concourse.bass_utils import run_bass_kernel_spmd as _run

    nc = _bacc.Bacc("TRN2", target_bir_lowering=False, num_devices=1, dynamic_dma_scratch_size=1024)
    arrays, args = {}, []
    for name in _INS:
        a = _np.ascontiguousarray(inputs[name])
        arrays[f"in_{name}_dram"] = a
        args.append(nc.dram_tensor(f"in_{name}_dram", a.shape, _mybir.dt.from_np(a.dtype), kind="ExternalInput").ap())
    args.append(nc.dram_tensor("out_0_dram", (B, P, H), F32, kind="ExternalOutput").ap())
    for name, shape in (("scr_q", (NG, NPART * HD, HT, KT * TOK)), ("scr_k", (NG, NPART * HD, HT, KT * TOK)),
                        ("scr_x", (NG, GB, NPART * HD, HT, KT * P)), ("scr_c", (NG, GB, NPART * HD, KVH, P))):
        args.append(nc.dram_tensor(name, shape, BF16, kind="Internal").ap())
    decoder_layer(nc, *args)
    r = _run(nc, [arrays], core_ids=[0])
    return r.results[0]["out_0_dram"]
```
